# Optimizing a Trainium2 kernel written in Bass

```python
import numpy as np
import jax
import jax.numpy as jnp

def _softmax(x, axis=-1):
    return jax.nn.softmax(x, axis=axis)

def _gelu(x):
    return jax.nn.gelu(x, approximate=True)

def _silu(x):
    return jax.nn.silu(x)

def _sigmoid(x):
    return jax.nn.sigmoid(x)

def _layernorm(x, axis=-1, eps=1e-05):
    m = jnp.mean(x, axis=axis, keepdims=True)
    v = jnp.var(x, axis=axis, keepdims=True)
    return (x - m) / jnp.sqrt(v + eps)

def _scatter_add(tgt, idx, src, axis=0):
    return tgt.at[idx].add(src)

def _segment_sum(src, seg, n):
    return jax.ops.segment_sum(src, seg, n)
kernel_name = 'mk_decoder_preln_d2_seqx_r8_51af06'

def setup_inputs(seed: int=0):
    np.random.seed(seed)
    _w = jnp.asarray

    def _rec_inputs():
        import jax
        import jax.numpy as jnp
        _rk = jax.random.key(seed)
        x = -0.0002928 + 1 * jax.random.normal(jax.random.fold_in(_rk, 1), (32, 128, 128), jnp.float32)
        _lenS = 128 - jax.random.randint(jax.random.fold_in(_rk, 7), (32,), 0, max(1, 128 // 4) + 1, jnp.int32)
        _lenS2 = 128 - jax.random.randint(jax.random.fold_in(_rk, 8), (32,), 0, max(1, 128 // 4) + 1, jnp.int32)
        _ctx_1024P = jax.random.normal(jax.random.fold_in(_rk, 11), (32, 16, 128), jnp.float32)
        _ctx_1024c = jax.random.dirichlet(jax.random.fold_in(_rk, 511), 0.3 * jnp.ones((16,), jnp.float32), (32, 128))
        _ctx_1024t = jnp.einsum('bsk,bkd->bsd', _ctx_1024c, _ctx_1024P)
        _ctx_1024t = _ctx_1024t * jax.lax.rsqrt(jnp.mean(jnp.square(_ctx_1024t)) + 1e-12) * 0.953939
        ctx_1024 = -1.39393e-06 + 0.999914 * (_ctx_1024t + 0.3 * jax.random.normal(jax.random.fold_in(_rk, 611), (32, 128, 128), jnp.float32))
        itok_S_0_31 = jax.random.randint(jax.random.fold_in(_rk, 12), (128,), 0, 32, jnp.int32)
        return (x, ctx_1024, itok_S_0_31)
    x, ctx_1024, itok_S_0_31 = _rec_inputs()

    def _L0_attn_setup():
        import jax, jax.numpy as jnp
        import numpy as np
        B, T, D = (2, 256, 128)
        H = 16
        HD = D // H
        DL = 64
        NR = 64
        EPS = 1.1920929e-07

        def _rms_norm(x, w):
            ms = jnp.mean(jnp.square(x), axis=-1, keepdims=True)
            return x * jax.lax.rsqrt(ms + EPS) * w
        key = jax.random.key(seed)
        ks = jax.random.split(key, 10)
        s = 0.02
        return {'x': jax.random.normal(ks[0], (B, T, D), dtype=jnp.float32), 'W_DQ': jax.random.normal(ks[1], (DL, HD), dtype=jnp.float32) * s, 'W_UQ': jax.random.normal(ks[2], (HD, DL), dtype=jnp.float32) * s, 'W_DKV': jax.random.normal(ks[3], (2 * DL, HD), dtype=jnp.float32) * s, 'W_UKV': jax.random.normal(ks[4], (2 * HD, 2 * DL), dtype=jnp.float32) * s, 'W_QR': jax.random.normal(ks[5], (NR, HD), dtype=jnp.float32) * s, 'W_KR': jax.random.normal(ks[6], (NR, HD), dtype=jnp.float32) * s, 'W_O': jax.random.normal(ks[7], (HD, HD), dtype=jnp.float32) * s, 'q_norm_w': jnp.ones((HD,), dtype=jnp.float32), 'k_norm_w': jnp.ones((HD,), dtype=jnp.float32)}
    _L0_attn_all = _L0_attn_setup()
    _L0_attn_in = {k: v for k, v in _L0_attn_all.items() if k in ('W_DQ', 'W_UQ', 'W_DKV', 'W_UKV', 'W_QR', 'W_KR', 'W_O', 'q_norm_w', 'k_norm_w')}
    del _L0_attn_all

    def _L0_xattn_setup():
        import jax, jax.numpy as jnp
        import numpy as np
        import math

        def _extend(chunk):
            prev = jnp.pad(chunk[:, :-1], ((0, 0), (1, 0), (0, 0), (0, 0), (0, 0)))
            nxt = jnp.pad(chunk[:, 1:], ((0, 0), (0, 1), (0, 0), (0, 0), (0, 0)))
            return jnp.stack((prev, chunk, nxt), axis=-1)

        def local_xl_attention(q, kv, Wq, Wkv, Wc, w):
            b, L, dm = q.shape
            dh = Wkv.shape[1] // 2
            nh = dm // dh
            C = L // w
            qp = (q @ Wq).reshape(b, L, nh, dh) / math.sqrt(dh)
            kvp = kv @ Wkv
            k = kvp[..., :dh][:, :, None, :]
            v = kvp[..., dh:][:, :, None, :]
            cq = qp.reshape(b, C, w, nh, dh)
            ck_e = _extend(k.reshape(b, C, w, 1, dh))
            attn = jnp.einsum('bcxhd,bzyode->bcxhey', cq, ck_e)
            attn = attn.reshape(b, L, nh, 3 * w)
            probs = jax.nn.softmax(attn, axis=-1)
            cp = probs.reshape(b, C, w, nh, 3, w)
            cv_e = _extend(v.reshape(b, C, w, 1, dh))
            ctx = jnp.einsum('bcwhpd,bzdoep->bcwhe', cp, cv_e)
            out = ctx.reshape(b, L, dm) @ Wc
            return out
        key = jax.random.key(seed)
        ks = jax.random.split(key, 5)
        B, L, DM, NH = (1, 512, 128, 16)
        DH = DM // NH
        scale = 0.02
        return {'q': jax.random.normal(ks[0], (B, L, DM), dtype=jnp.float32), 'kv': jax.random.normal(ks[1], (B, L, DM), dtype=jnp.float32), 'Wq': jax.random.normal(ks[2], (DM, DM), dtype=jnp.float32) * scale, 'Wkv': jax.random.normal(ks[3], (DM, 2 * DH), dtype=jnp.float32) * scale, 'Wc': jax.random.normal(ks[4], (DM, DM), dtype=jnp.float32) * scale, 'w': 64}
    _L0_xattn_all = _L0_xattn_setup()
    _L0_xattn_in = {k: v for k, v in _L0_xattn_all.items() if k in ('Wq', 'Wkv', 'Wc')}
    del _L0_xattn_all

    def _L0_ffn_setup():
        import jax, jax.numpy as jnp
        import numpy as np
        from jax import lax
        T, B, I, M, O = (32, 64, 128, 128, 128)

        def _xavier(key, shape):
            fan_out, fan_in = shape
            limit = float(np.sqrt(6.0 / (fan_in + fan_out)))
            return jax.random.uniform(key, shape, jnp.float32, -limit, limit)
        key = jax.random.key(seed)
        ks = jax.random.split(key, 9)
        x = jax.random.normal(ks[0], (T, B, I), jnp.float32)
        return {'x': x, 'wf': _xavier(ks[1], (M, I)), 'uf': _xavier(ks[2], (M, M)), 'bf': jnp.zeros((M,), jnp.float32), 'wi': _xavier(ks[3], (M, I)), 'ui': _xavier(ks[4], (M, M)), 'bi': jnp.zeros((M,), jnp.float32), 'wc': _xavier(ks[5], (M, I)), 'uc': _xavier(ks[6], (M, M)), 'bc': jnp.zeros((M,), jnp.float32), 'wo': _xavier(ks[7], (O, I)), 'uo': _xavier(ks[8], (O, M)), 'bo': jnp.zeros((O,), jnp.float32), 'in_c': jnp.zeros((M,), jnp.float32)}
    _L0_ffn_all = _L0_ffn_setup()
    _L0_ffn_in = {k: v for k, v in _L0_ffn_all.items() if k in ('wf', 'uf', 'bf', 'wi', 'ui', 'bi', 'wc', 'uc', 'bc', 'wo', 'uo', 'bo', 'in_c')}
    del _L0_ffn_all

    def _L1_attn_setup():
        import jax, jax.numpy as jnp
        import numpy as np
        EMBED_DIM = 128
        NUM_HEADS = 16
        HEAD_DIM = EMBED_DIM // NUM_HEADS

        def _sinusoid_pos_emb(seq_len, dim):
            pos = jnp.arange(seq_len, dtype=jnp.float32)
            idx = jnp.arange(dim // 2, dtype=jnp.float32)
            inv_freq = 1.0 / 10000.0 ** (2.0 * idx / dim)
            ang = pos[:, None] * inv_freq[None, :]
            return jnp.concatenate([jnp.sin(ang), jnp.cos(ang)], axis=-1)

        def _relative_shift(x):
            b, h, s, _ = x.shape
            x = jnp.pad(x, ((0, 0), (0, 0), (0, 0), (1, 0)))
            x = x.reshape(b, h, s + 1, s)
            return x[:, :, 1:, :].reshape(b, h, s, s)
        key = jax.random.key(seed)
        ks = jax.random.split(key, 12)
        D = EMBED_DIM
        sc = 1.0 / np.sqrt(D)
        inp = {'x': jax.random.normal(ks[0], (2, 256, D), dtype=jnp.float32)}
        for i, name in enumerate(['Wq', 'Wk', 'Wv', 'Wp', 'Wo']):
            inp[name] = jax.random.normal(ks[1 + i], (D, D), dtype=jnp.float32) * sc
            inp['b' + name[1].lower()] = jnp.zeros((D,), dtype=jnp.float32)
        inp['u'] = jax.random.normal(ks[6], (1, NUM_HEADS, 1, HEAD_DIM), dtype=jnp.float32) * 0.05
        inp['v'] = jax.random.normal(ks[7], (1, NUM_HEADS, 1, HEAD_DIM), dtype=jnp.float32) * 0.05
        return inp
    _L1_attn_all = _L1_attn_setup()
    _L1_attn_in = {k: v for k, v in _L1_attn_all.items() if k in ('Wq', 'bq', 'Wk', 'bk', 'Wv', 'bv', 'Wp', 'bp', 'Wo', 'bo', 'u', 'v')}
    del _L1_attn_all

    def _L1_xattn_setup():
        import jax, jax.numpy as jnp
        import numpy as np
        NUM_LAYERS = 32
        IN_SIZE = 128
        OUT_SIZE = 128
        B, S = (32, 32)
        key = jax.random.key(seed)
        k1, k2, k3 = jax.random.split(key, 3)
        x = jax.random.normal(k1, (B, S, IN_SIZE), dtype=jnp.float32)
        layer_idx = jax.random.randint(k2, (S,), 0, NUM_LAYERS, dtype=jnp.int32)
        weight = jax.random.normal(k3, (NUM_LAYERS, OUT_SIZE, IN_SIZE), dtype=jnp.float32)
        return {'x': x, 'layer_idx': layer_idx, 'weight': weight}
    _L1_xattn_all = _L1_xattn_setup()
    _L1_xattn_in = {k: v for k, v in _L1_xattn_all.items() if k in ()}
    del _L1_xattn_all

    def _L1_ffn_setup():
        import jax, jax.numpy as jnp
        import numpy as np
        B, S, H = (2, 128, 128)
        E, F = (16, 64)
        G, TOPK_G, TOPK = (4, 2, 4)
        N_SHARED = 2
        ROUTE_SCALE = 1.0
        FS = N_SHARED * F

        def _gate(x, w_gate):
            T = x.shape[0]
            scores = jax.nn.sigmoid(x @ w_gate.T)
            sv = scores.reshape(T, G, E // G)
            group_scores = jax.lax.top_k(sv, 2)[0].sum(-1)
            top_groups = jax.lax.top_k(group_scores, TOPK_G)[1]
            allowed = jnp.zeros((T, G), dtype=bool).at[jnp.arange(T)[:, None], top_groups].set(True)
            masked = jnp.where(allowed[:, :, None], sv, -jnp.inf).reshape(T, E)
            _, idx = jax.lax.top_k(masked, TOPK)
            w = jnp.take_along_axis(scores, idx, axis=1)
            w = w / (w.sum(-1, keepdims=True) + 1e-06) * ROUTE_SCALE
            return (w, idx)

        def _swiglu(x, w1, w3, w2):
            return jax.nn.silu(x @ w1.T) * (x @ w3.T) @ w2.T
        key = jax.random.key(seed)
        ks = jax.random.split(key, 8)
        scale = 0.02
        return {'hidden_states': jax.random.normal(ks[0], (B, S, H), dtype=jnp.float32), 'w_gate': jax.random.normal(ks[1], (E, H), dtype=jnp.float32) * scale, 'w1_e': jax.random.normal(ks[2], (E, F, H), dtype=jnp.float32) * scale, 'w3_e': jax.random.normal(ks[3], (E, F, H), dtype=jnp.float32) * scale, 'w2_e': jax.random.normal(ks[4], (E, H, F), dtype=jnp.float32) * scale, 'w1_s': jax.random.normal(ks[5], (FS, H), dtype=jnp.float32) * scale, 'w3_s': jax.random.normal(ks[6], (FS, H), dtype=jnp.float32) * scale, 'w2_s': jax.random.normal(ks[7], (H, FS), dtype=jnp.float32) * scale}
    _L1_ffn_all = _L1_ffn_setup()
    _L1_ffn_in = {k: v for k, v in _L1_ffn_all.items() if k in ('w_gate', 'w1_e', 'w3_e', 'w2_e', 'w1_s', 'w3_s', 'w2_s')}
    del _L1_ffn_all
    return {'x': x, 'ctx_1024': ctx_1024, 'itok_S_0_31': itok_S_0_31, 'L0_attn_W_DQ': _L0_attn_in['W_DQ'], 'L0_attn_W_UQ': _L0_attn_in['W_UQ'], 'L0_attn_W_DKV': _L0_attn_in['W_DKV'], 'L0_attn_W_UKV': _L0_attn_in['W_UKV'], 'L0_attn_W_QR': _L0_attn_in['W_QR'], 'L0_attn_W_KR': _L0_attn_in['W_KR'], 'L0_attn_W_O': _L0_attn_in['W_O'], 'L0_attn_q_norm_w': _L0_attn_in['q_norm_w'], 'L0_attn_k_norm_w': _L0_attn_in['k_norm_w'], 'L0_xattn_Wq': _L0_xattn_in['Wq'], 'L0_xattn_Wkv': _L0_xattn_in['Wkv'], 'L0_xattn_Wc': _L0_xattn_in['Wc'], 'L0_ffn_wf': _L0_ffn_in['wf'], 'L0_ffn_uf': _L0_ffn_in['uf'], 'L0_ffn_bf': _L0_ffn_in['bf'], 'L0_ffn_wi': _L0_ffn_in['wi'], 'L0_ffn_ui': _L0_ffn_in['ui'], 'L0_ffn_bi': _L0_ffn_in['bi'], 'L0_ffn_wc': _L0_ffn_in['wc'], 'L0_ffn_uc': _L0_ffn_in['uc'], 'L0_ffn_bc': _L0_ffn_in['bc'], 'L0_ffn_wo': _L0_ffn_in['wo'], 'L0_ffn_uo': _L0_ffn_in['uo'], 'L0_ffn_bo': _L0_ffn_in['bo'], 'L0_ffn_in_c': _L0_ffn_in['in_c'], 'L1_attn_Wq': _L1_attn_in['Wq'], 'L1_attn_bq': _L1_attn_in['bq'], 'L1_attn_Wk': _L1_attn_in['Wk'], 'L1_attn_bk': _L1_attn_in['bk'], 'L1_attn_Wv': _L1_attn_in['Wv'], 'L1_attn_bv': _L1_attn_in['bv'], 'L1_attn_Wp': _L1_attn_in['Wp'], 'L1_attn_bp': _L1_attn_in['bp'], 'L1_attn_Wo': _L1_attn_in['Wo'], 'L1_attn_bo': _L1_attn_in['bo'], 'L1_attn_u': _L1_attn_in['u'], 'L1_attn_v': _L1_attn_in['v'], 'L1_ffn_w_gate': _L1_ffn_in['w_gate'], 'L1_ffn_w1_e': _L1_ffn_in['w1_e'], 'L1_ffn_w3_e': _L1_ffn_in['w3_e'], 'L1_ffn_w2_e': _L1_ffn_in['w2_e'], 'L1_ffn_w1_s': _L1_ffn_in['w1_s'], 'L1_ffn_w3_s': _L1_ffn_in['w3_s'], 'L1_ffn_w2_s': _L1_ffn_in['w2_s']}

def reference(x, ctx_1024, itok_S_0_31, L0_attn_W_DQ, L0_attn_W_UQ, L0_attn_W_DKV, L0_attn_W_UKV, L0_attn_W_QR, L0_attn_W_KR, L0_attn_W_O, L0_attn_q_norm_w, L0_attn_k_norm_w, L0_xattn_Wq, L0_xattn_Wkv, L0_xattn_Wc, L0_ffn_wf, L0_ffn_uf, L0_ffn_bf, L0_ffn_wi, L0_ffn_ui, L0_ffn_bi, L0_ffn_wc, L0_ffn_uc, L0_ffn_bc, L0_ffn_wo, L0_ffn_uo, L0_ffn_bo, L0_ffn_in_c, L1_attn_Wq, L1_attn_bq, L1_attn_Wk, L1_attn_bk, L1_attn_Wv, L1_attn_bv, L1_attn_Wp, L1_attn_bp, L1_attn_Wo, L1_attn_bo, L1_attn_u, L1_attn_v, L1_ffn_w_gate, L1_ffn_w1_e, L1_ffn_w3_e, L1_ffn_w2_e, L1_ffn_w1_s, L1_ffn_w3_s, L1_ffn_w2_s):
    import jax
    import jax.numpy as jnp

    def _L0_attn_ref(x, W_DQ, W_UQ, W_DKV, W_UKV, W_QR, W_KR, W_O, q_norm_w, k_norm_w):
        import jax, jax.numpy as jnp
        import numpy as np
        B, T, D = (2, 256, 128)
        H = 16
        HD = D // H
        DL = 64
        NR = 64
        EPS = 1.1920929e-07

        def _rms_norm(x, w):
            ms = jnp.mean(jnp.square(x), axis=-1, keepdims=True)
            return x * jax.lax.rsqrt(ms + EPS) * w
        b, t, d = x.shape
        scale = HD ** (-0.5)
        xh = x.reshape(b, t, H, HD).transpose(0, 2, 1, 3)
        c_q = jnp.einsum('bhtd,ld->bhtl', xh, W_DQ)
        q_c = jnp.einsum('bhtl,dl->bhtd', c_q, W_UQ)
        q_c_norm = _rms_norm(q_c, q_norm_w)
        q_r = jnp.einsum('bhtd,rd->bhtr', q_c_norm, W_QR)
        q = jnp.concatenate([q_c_norm, q_r], axis=-1)
        c_kv = jnp.einsum('bhtd,ld->bhtl', xh, W_DKV)
        kv = jnp.einsum('bhtl,dl->bhtd', c_kv, W_UKV)
        k_c, v_c = (kv[..., :HD], kv[..., HD:])
        k_c_norm = _rms_norm(k_c, k_norm_w)
        k_r = jnp.einsum('bhtd,rd->bhtr', xh, W_KR)
        k = jnp.concatenate([k_c_norm, k_r], axis=-1)
        scores = jnp.einsum('bhqd,bhkd->bhqk', q, k) * scale
        causal = jnp.triu(jnp.full((t, t), -jnp.inf, dtype=scores.dtype), k=1)
        attn = jax.nn.softmax(scores + causal, axis=-1)
        ctx = jnp.einsum('bhqk,bhkd->bhqd', attn, v_c)
        out = jnp.einsum('bhtd,od->bhto', ctx, W_O)
        return out.transpose(0, 2, 1, 3).reshape(b, t, d)

    def _L0_xattn_ref(q, kv, Wq, Wkv, Wc, w):
        import jax, jax.numpy as jnp
        import numpy as np
        import math

        def _extend(chunk):
            prev = jnp.pad(chunk[:, :-1], ((0, 0), (1, 0), (0, 0), (0, 0), (0, 0)))
            nxt = jnp.pad(chunk[:, 1:], ((0, 0), (0, 1), (0, 0), (0, 0), (0, 0)))
            return jnp.stack((prev, chunk, nxt), axis=-1)

        def local_xl_attention(q, kv, Wq, Wkv, Wc, w):
            b, L, dm = q.shape
            dh = Wkv.shape[1] // 2
            nh = dm // dh
            C = L // w
            qp = (q @ Wq).reshape(b, L, nh, dh) / math.sqrt(dh)
            kvp = kv @ Wkv
            k = kvp[..., :dh][:, :, None, :]
            v = kvp[..., dh:][:, :, None, :]
            cq = qp.reshape(b, C, w, nh, dh)
            ck_e = _extend(k.reshape(b, C, w, 1, dh))
            attn = jnp.einsum('bcxhd,bzyode->bcxhey', cq, ck_e)
            attn = attn.reshape(b, L, nh, 3 * w)
            probs = jax.nn.softmax(attn, axis=-1)
            cp = probs.reshape(b, C, w, nh, 3, w)
            cv_e = _extend(v.reshape(b, C, w, 1, dh))
            ctx = jnp.einsum('bcwhpd,bzdoep->bcwhe', cp, cv_e)
            out = ctx.reshape(b, L, dm) @ Wc
            return out
        return local_xl_attention(q, kv, Wq, Wkv, Wc, w)

    def _L0_ffn_ref(x, wf, uf, bf, wi, ui, bi, wc, uc, bc, wo, uo, bo, in_c):
        import jax, jax.numpy as jnp
        import numpy as np
        from jax import lax
        T, B, I, M, O = (32, 64, 128, 128, 128)

        def _xavier(key, shape):
            fan_out, fan_in = shape
            limit = float(np.sqrt(6.0 / (fan_in + fan_out)))
            return jax.random.uniform(key, shape, jnp.float32, -limit, limit)
        batch = x.shape[1]
        c0 = jnp.broadcast_to(in_c, (batch, in_c.shape[0]))

        def step(c, xt):
            ft = jax.nn.sigmoid(xt @ wf.T + c @ uf.T + bf)
            it = jax.nn.sigmoid(xt @ wi.T + c @ ui.T + bi)
            gt = jnp.tanh(xt @ wc.T + c @ uc.T + bc)
            c = ft * c + it * gt
            return (c, None)
        c_final, _ = lax.scan(step, c0, x)
        h = jnp.tanh(jnp.einsum('tbi,oi->tbo', x, wo) + c_final @ uo.T + bo)
        return h

    def _L1_attn_ref(x, Wq, bq, Wk, bk, Wv, bv, Wp, bp, Wo, bo, u, v):
        import jax, jax.numpy as jnp
        import numpy as np
        EMBED_DIM = 128
        NUM_HEADS = 16
        HEAD_DIM = EMBED_DIM // NUM_HEADS

        def _sinusoid_pos_emb(seq_len, dim):
            pos = jnp.arange(seq_len, dtype=jnp.float32)
            idx = jnp.arange(dim // 2, dtype=jnp.float32)
            inv_freq = 1.0 / 10000.0 ** (2.0 * idx / dim)
            ang = pos[:, None] * inv_freq[None, :]
            return jnp.concatenate([jnp.sin(ang), jnp.cos(ang)], axis=-1)

        def _relative_shift(x):
            b, h, s, _ = x.shape
            x = jnp.pad(x, ((0, 0), (0, 0), (0, 0), (1, 0)))
            x = x.reshape(b, h, s + 1, s)
            return x[:, :, 1:, :].reshape(b, h, s, s)
        B, S, D = x.shape
        H, P = (NUM_HEADS, HEAD_DIM)

        def heads(t):
            return t.reshape(B, S, H, P).transpose(0, 2, 1, 3)
        q = heads(x @ Wq + bq)
        k = heads(x @ Wk + bk)
        val = heads(x @ Wv + bv)
        pos = _sinusoid_pos_emb(S, D) @ Wp + bp
        pos = pos.reshape(S, H, P).transpose(1, 0, 2)
        content_score = jnp.einsum('bhsp,bhtp->bhst', q + u, k)
        pos_score = jnp.einsum('bhsp,htp->bhst', q + v, pos)
        pos_score = _relative_shift(pos_score)
        score = (content_score + pos_score) / jnp.sqrt(jnp.float32(P))
        weights = jax.nn.softmax(score, axis=-1)
        out = jnp.einsum('bhst,bhtp->bhsp', weights, val)
        out = out.transpose(0, 2, 1, 3).reshape(B, S, D)
        return out @ Wo + bo

    def _L1_xattn_ref(x, layer_idx, weight):
        import jax, jax.numpy as jnp
        import numpy as np
        NUM_LAYERS = 32
        IN_SIZE = 128
        OUT_SIZE = 128
        B, S = (32, 32)
        w = weight[layer_idx]
        return jnp.einsum('bsd,sod->bso', x, w)

    def _L1_ffn_ref(hidden_states, w_gate, w1_e, w3_e, w2_e, w1_s, w3_s, w2_s):
        import jax, jax.numpy as jnp
        import numpy as np
        B, S, H = (2, 128, 128)
        E, F = (16, 64)
        G, TOPK_G, TOPK = (4, 2, 4)
        N_SHARED = 2
        ROUTE_SCALE = 1.0
        FS = N_SHARED * F

        def _gate(x, w_gate):
            T = x.shape[0]
            scores = jax.nn.sigmoid(x @ w_gate.T)
            sv = scores.reshape(T, G, E // G)
            group_scores = jax.lax.top_k(sv, 2)[0].sum(-1)
            top_groups = jax.lax.top_k(group_scores, TOPK_G)[1]
            allowed = jnp.zeros((T, G), dtype=bool).at[jnp.arange(T)[:, None], top_groups].set(True)
            masked = jnp.where(allowed[:, :, None], sv, -jnp.inf).reshape(T, E)
            _, idx = jax.lax.top_k(masked, TOPK)
            w = jnp.take_along_axis(scores, idx, axis=1)
            w = w / (w.sum(-1, keepdims=True) + 1e-06) * ROUTE_SCALE
            return (w, idx)

        def _swiglu(x, w1, w3, w2):
            return jax.nn.silu(x @ w1.T) * (x @ w3.T) @ w2.T
        shape = hidden_states.shape
        x = hidden_states.reshape(-1, H)
        weights, idx = _gate(x, w_gate)
        combine = (jax.nn.one_hot(idx, E, dtype=x.dtype) * weights[..., None]).sum(1)
        g = jax.nn.silu(jnp.einsum('th,efh->tef', x, w1_e))
        u = jnp.einsum('th,efh->tef', x, w3_e)
        routed = jnp.einsum('tef,ehf,te->th', g * u, w2_e, combine)
        shared = _swiglu(x, w1_s, w3_s, w2_s)
        return (routed + shared).reshape(shape)
    x = x + _L0_attn_ref(_layernorm(x, axis=-1), L0_attn_W_DQ, L0_attn_W_UQ, L0_attn_W_DKV, L0_attn_W_UKV, L0_attn_W_QR, L0_attn_W_KR, L0_attn_W_O, L0_attn_q_norm_w, L0_attn_k_norm_w)
    x = x + _L0_xattn_ref(_layernorm(x, axis=-1), ctx_1024, L0_xattn_Wq, L0_xattn_Wkv, L0_xattn_Wc, 64)
    x = x + _L0_ffn_ref(_layernorm(x, axis=-1), L0_ffn_wf, L0_ffn_uf, L0_ffn_bf, L0_ffn_wi, L0_ffn_ui, L0_ffn_bi, L0_ffn_wc, L0_ffn_uc, L0_ffn_bc, L0_ffn_wo, L0_ffn_uo, L0_ffn_bo, L0_ffn_in_c)
    x = x + _L1_attn_ref(_layernorm(x, axis=-1), L1_attn_Wq, L1_attn_bq, L1_attn_Wk, L1_attn_bk, L1_attn_Wv, L1_attn_bv, L1_attn_Wp, L1_attn_bp, L1_attn_Wo, L1_attn_bo, L1_attn_u, L1_attn_v)
    x = x + _L1_xattn_ref(_layernorm(x, axis=-1), itok_S_0_31, ctx_1024)
    x = x + _L1_ffn_ref(_layernorm(x, axis=-1), L1_ffn_w_gate, L1_ffn_w1_e, L1_ffn_w3_e, L1_ffn_w2_e, L1_ffn_w1_s, L1_ffn_w3_s, L1_ffn_w2_s)
    return x

_drawn_inputs = setup_inputs


def setup_inputs(seed=0):
    import zlib

    import numpy as np

    out = dict(_drawn_inputs(seed))
    spreads = {'L0_attn_q_norm_w': (1.0, 0.6),
     'L0_attn_k_norm_w': (1.0, 0.6),
     'L0_ffn_bf': (0.0, 0.641),
     'L0_ffn_bi': (0.0, 0.684),
     'L0_ffn_bc': (0.0, 0.1),
     'L0_ffn_bo': (0.0, 0.1),
     'L0_ffn_in_c': (0.0, 2.0),
     'L1_attn_bq': (0.0, 0.529),
     'L1_attn_bk': (0.0, 2.0),
     'L1_attn_bv': (0.0, 0.1),
     'L1_attn_bp': (0.0, 0.8),
     'L1_attn_bo': (0.0, 0.1)}
    factors = {'L0_attn_W_DQ': 8.0,
     'L0_attn_W_UQ': 8.0,
     'L0_attn_W_DKV': 8.0,
     'L0_attn_W_UKV': 8.0,
     'L0_attn_W_QR': 8.0,
     'L0_attn_W_KR': 8.0,
     'L0_attn_W_O': 8.0,
     'L0_xattn_Wq': 45.338,
     'L1_attn_u': 6.829,
     'L1_attn_v': 8.0,
     'L1_ffn_w_gate': 8.0,
     'L1_ffn_w1_e': 8.0,
     'L1_ffn_w3_e': 8.0,
     'L1_ffn_w2_e': 8.0,
     'L1_ffn_w1_s': 8.0,
     'L1_ffn_w3_s': 8.0,
     'L1_ffn_w2_s': 8.0}
    for name, (base, spread) in spreads.items():
        noise = np.random.default_rng([zlib.crc32(name.encode()), seed]).standard_normal(out[name].shape)
        drawn = base * np.exp(spread * noise) if base else spread * noise
        out[name] = jnp.asarray(drawn.astype(out[name].dtype))
    for name, factor in factors.items():
        out[name] = (out[name] * factor).astype(out[name].dtype)
    return out
```

```python
from contextlib import ExitStack

import concourse.bass as bass
from concourse import mybir

F32 = mybir.dt.float32
BF16 = mybir.dt.bfloat16
I32 = mybir.dt.int32
ALU = mybir.AluOpType
ACT = mybir.ActivationFunctionType
AX = mybir.AxisListType

NB, S, D = 32, 128, 128
H, HD = 16, 8
R, PT = 4, 4
GW = 32
LN_EPS = 1e-5
RMS_EPS = 1.1920929e-07
SCALE = float(HD) ** -0.5
LATENT, ROPE = 64, 64
RSQRT_GUESS = float(0x5F3759DF)
NEWTON = 3
ROOT_STEPS = 3 * NEWTON + 1

C_ID, C_CAUSAL, C_HEAD, C_REP, C_SIN = 0, 128, 256, 272, 400
C_TIE_G, C_TIE_E = 528, 544
C_END = 800
EX, FW = 16, 64
TILES = EX * FW // 128 + 1


class Phase:
    pass


def wait(eng, sem, count):
    if isinstance(count, int) and count <= 0:
        return
    eng.wait_ge(sem, count)


def at(i, n=1):
    return bass.ds(i, n)


MANY = 99


def body_pairs(eng, body, tail=1):
    body(0, 0, NB - 1)
    body(1, 1, NB - 2)
    with eng.Fori(1, NB // 2 - tail) as pair:
        b = pair * 2
        body(b, 0, MANY)
        body(b + 1, 1, MANY)
    for b in range(NB - 2 * tail, NB):
        body(b, b % 2, NB - 1 - b)


def group_pairs(eng, body):
    groups = NB // 4
    body(0, 0, groups - 1)
    body(1, 1, groups - 2)
    with eng.Fori(1, groups // 2 - 1) as pair:
        g = pair * 2
        body(g, 0, MANY)
        body(g + 1, 1, MANY)
    body(groups - 2, 0, 1)
    body(groups - 1, 1, 0)


def decoder(nc, t, out):
    with ExitStack() as ctx:
        def sb(name, shape, dt=F32):
            return ctx.enter_context(nc.sbuf_tensor(name, shape, dt))

        def sems(prefix, names):
            return [ctx.enter_context(nc.semaphore(f"{prefix}_{n}")) for n in names.split()]

        X = sb("X", [S, NB, D])
        consts = sb("consts", [128, C_END])
        ident = consts[:, C_ID:C_ID + 128]
        identb = sb("identb", [128, 128], BF16)
        causal4 = sb("causal4", [128, PT, 128], BF16)
        psum = ctx.enter_context(nc.psum_tensor("psum", [128, 8, 512], F32))
        bank = [psum[:, i, :] for i in range(8)]
        quads = [b.rearrange("s (p k) -> s p k", p=PT) for b in bank]

        stats = sb("stats", [S, 6])
        meanvar = sb("meanvar", [S, 2])
        carrier = sb("carrier", [1, 1])
        vareps = sb("vareps", [S, 1])
        rstd = sb("rstd", [S, 1])
        minus_half = sb("minus_half", [S, 32])
        xn = sb("xn", [S, 1, D])
        xnT = sb("xnT", [D, S])
        squares = sb("squares", [S, 2 * H, HD])
        ms = sb("ms", [S, 2 * H])
        ms_eps = sb("ms_eps", [S, 2 * H])
        rr = sb("rr", [S, 2 * H])
        rr_tmp = sb("rr_tmp", [S, 2 * H])
        kn1 = sb("kn1", [S, H, HD])
        kn2 = sb("kn2", [S, H, HD])
        qpad = sb("qpad", [S, PT, R, GW])
        kpad = sb("kpad", [S, PT, R, GW])
        qT = sb("qT", [128, 2, PT, S])
        kT = sb("kT", [128, 2, PT, S])
        values = sb("values", [S, 2, H, GW])
        outT = sb("outT", [128, R, S])
        negmax = sb("negmax", [S, 2, PT])
        probs = sb("probs", [S, 2, PT, S])
        probsT = sb("probsT", [S, 2, PT, S])
        recip = sb("recip", [S, H])
        attn = sb("attn", [S, 1, H, HD])
        w_dq = sb("w_dq", [LATENT, HD])
        w_uqT = sb("w_uqT", [LATENT, HD])
        w_dkv = sb("w_dkv", [2 * LATENT, HD])
        w_ukvT = sb("w_ukvT", [2 * LATENT, 2 * HD])
        w_qr = sb("w_qr", [ROPE, HD])
        w_kr = sb("w_kr", [ROPE, HD])
        w_oT = sb("w_oT", [HD, HD])
        qnw = sb("qnw", [128, HD])
        qnws = sb("qnws", [128, HD])
        knw = sb("knw", [128, HD])
        qkw = sb("qkw", [128, 1, HD])
        avT = sb("avT", [HD, HD])
        small = sb("small", [HD, 4, HD])
        wblk = sb("wblk", [128, 4, H, HD])

        attnT = sb("attnT", [H * HD, S])
        KEYS = 192
        ctxT = sb("ctxT", [D, NB, S])
        w_qx = sb("w_qx", [D, D])
        w_kvx = sb("w_kvx", [D, R, GW])
        w_cx = sb("w_cx", [D, D])
        k3T = sb("k3T", [128, 2, KEYS])
        kvT = sb("kvT", [128, S])
        v8 = sb("v8", [S, 2, GW])
        probs3 = sb("probs3", [S, 2, PT, KEYS])
        denom = sb("denom", [S, 2, H])
        wx = sb("wx", [D, 4, D])
        uc = sb("uc", [D, 4, D])
        gate_bias = sb("gate_bias", [D, 4])
        cell0 = sb("cell0", [D, 1])
        half_bias = sb("half_bias", [D, 2])
        cell2 = sb("cell2", [D, S])
        gates = sb("gates", [D, 3, S])
        keep = sb("keep", [D, S])
        fresh = sb("fresh", [D, S])
        seqT = sb("seqT", [D, NB, S])
        hidden = sb("hidden", [D, 2, 4, S])
        wqkv = sb("wqkv", [D, 3, D])
        w_p = sb("w_p", [D, D])
        w_o1 = sb("w_o1", [D, D])
        bias_rows = sb("bias_rows", [S, 7, D])
        bias_q = sb("bias_q", [S, 2, D])
        q2pad = sb("q2pad", [S, PT, R, GW])
        q2T = sb("q2T", [128, PT, S])
        posT = sb("posT", [128, PT, S])
        v_stage = sb("v_stage", [S, H, HD])
        pos_rows = sb("pos_rows", [S, 2, H, S + 1])
        pos_score = sb("pos_score", [S, 2, H, S])
        summed = sb("summed", [S, 2, PT, S])
        skew = [nc.dram_tensor(f"skew{i}", (H, S * (S + 1)), F32, kind="Internal").ap() for i in range(2)]
        stats4 = sb("stats4", [S, 4, 6])
        meanvar4 = sb("meanvar4", [S, 4, 2])
        vareps4 = sb("vareps4", [S, 4])
        rstd4 = sb("rstd4", [S, 4])
        xn4 = sb("xn4", [S, 4, D])
        itok = sb("itok", [1, S], I32)
        gathered = pos_score[:, :, :, :]
        yT = sb("yT", [D, NB, S])
        y_stage = hidden[:, :, :, :]
        w_gate = sb("w_gate", [D, EX])
        w_up1 = sb("w_up1", [D, TILES, 128])
        w_up3 = sb("w_up3", [D, TILES, 128])
        w_down = sb("w_down", [128, TILES, D])
        spread = yT[0:3 * EX, 0:TILES - 1, :]
        spreadb = sb("spreadb", [3 * EX, TILES - 1, 128], BF16)
        xT = sb("xT", [D, 2, 4, S])
        scores4 = sb("scores4", [S, 4, EX])
        top = sb("top", [S, 4, 4, 2, 2])
        pair_hi, pair_lo = top[:, :, :, 0, :], top[:, :, :, 1, :]
        best = sb("best", [S, 2, 4, 4])
        group_score = sb("group_score", [S, 4, 4])
        group_gt = sb("group_gt", [S, 4, 4, 4])
        group_eq = sb("group_eq", [S, 4, 4, 4])
        group_rank = sb("group_rank", [S, 4, 4])
        masked = sb("masked", [S, 4, 4, 4])
        scores_space = pos_score[:, :, :, :].rearrange("s a h k -> s (a h k)")
        expert_gt = scores_space[:, 0:1024].rearrange("s (k e f) -> s k e f", k=4, e=EX)
        expert_eq = scores_space[:, 1024:2048].rearrange("s (k e f) -> s k e f", k=4, e=EX)
        expert_rank = sb("expert_rank", [S, 4, EX])
        chosen = sb("chosen", [S, 4, EX])
        total = sb("total", [S, 4])
        combine = sb("combine", [S, 4, EX])
        parts3 = sb("parts3", [S, 4, 3, EX], BF16)
        combineT = sb("combineT", [3 * EX, 2, 4, S], BF16)
        rows_space = pos_rows[:, :, :, :].rearrange("s a h k -> s (a h k)")
        silu = rows_space[:, 0:1024].rearrange("m (a t) -> m a t", a=2)
        hidden_a = rows_space[:, 1024:2048].rearrange("m (a t) -> m a t", a=2)
        gated = rows_space[:, 2048:2560]
        ld = Phase()
        [ld.x, ld.w, ld.c, ld.b, ld.g, ld.d, ld.e, ld.f] = sems("ld", "x w c b g d e f")
        k0 = Phase()
        [k0.zero, k0.ones, k0.half, k0.kvzero, k0.wqx, k0.cast, k0.qnws, k0.qkw, k0.fold] = sems("k0", "zero ones half kvzero wqx cast qnws qkw fold")
        A = Phase()
        [A.proj, A.sq, A.ms, A.root, A.rr, A.qn, A.kn1, A.kn2, A.kn, A.v, A.qT_ps, A.qT, A.kT_ps, A.kT, A.s,
         A.mx, A.p, A.pT_ps, A.pT, A.o, A.oT, A.oT_ps, A.rec, A.on, A.x] = sems("a", "proj sq ms root rr qn kn1 kn2 kn v qT_ps qT kT_ps kT s mx p pT_ps pT o oT oT_ps rec on x")
        norm = sems("norm", "stats aggr var rstd xn xnT_ps xnT")

        def share_norm(q, base):
            q.base = base
            q.stats, q.aggr, q.var, q.rstd, q.xn, q.xnT_ps, q.xnT = norm

        share_norm(A, 0)
        A.summed, A.mixed, A.out_free, A.attn_free = A.s, A.p, A.on, A.x
        A.scores, A.prob_bank, A.out_bank = quads[0:2], bank[2:4], bank[4]
        A.ln_bank, A.proj_bank, A.head_bank = bank[5], bank[6], bank[7]
        A.probs, A.shared_v = probs, None
        B = Phase()
        [B.proj, B.q, B.k, B.kv, B.ksum, B.vT_ps, B.v, B.qT_ps, B.qT, B.s, B.mx, B.p, B.ab, B.pT_ps, B.pT,
         B.o, B.oT, B.oT_ps, B.rec, B.on, B.aT_ps, B.aT, B.y, B.x] = sems("b", "proj q k kv ksum vT_ps v qT_ps qT s mx p ab pT_ps pT o oT oT_ps rec on aT_ps aT y x")
        share_norm(B, NB)
        B.summed, B.mixed, B.out_free, B.attn_free = B.s, B.ab, B.x, B.aT_ps
        B.scores = [psum[:, 2 * i:2 * i + 2, 0:2 * KEYS].rearrange("s b (h k) -> s b h k", h=2) for i in range(2)]
        B.prob_bank, B.out_bank, B.ln_bank, B.head_bank = bank[4:6], bank[6], bank[7], bank[7]
        B.probs, B.shared_v = probs, v8
        C = Phase()
        [C.g, C.f, C.c, C.keep, C.fresh, C.cell, C.zero_cell, C.scaled, C.z, C.h, C.hT_ps, C.x] = sems("c", "g f c keep fresh cell zero_cell scaled z h hT_ps x")
        share_norm(C, 2 * NB)
        C.ln_bank = bank[2]
        C.gate_bank = bank[0:2]
        C.h_bank, C.hT_bank = bank[4:6], bank[6:8]
        P = Phase()
        [P.proj, P.q2, P.q, P.k, P.vst, P.v, P.bias, P.q2T_ps, P.q2T, P.qT_ps, P.qT, P.kT_ps, P.kT, P.e,
         P.es, P.s, P.add, P.mx, P.p, P.pT_ps, P.pT, P.o, P.oT, P.oT_ps, P.rec, P.on, P.aT_ps, P.aT, P.y,
         P.x, P.bqs, P.zeroed, P.pos, P.skewed, P.placed, P.gate] = sems("d", "proj q2 q k vst v bias q2T_ps q2T qT_ps qT kT_ps kT e es s add mx p pT_ps pT o oT oT_ps "
            "rec on aT_ps aT y x bqs zeroed pos skewed placed gate")
        share_norm(P, 3 * NB)
        P.summed, P.mixed, P.out_free, P.attn_free = P.add, P.p, P.x, P.aT_ps
        P.score_bank = quads[0:2]
        P.scores = [summed[:, i, :, :] for i in range(2)]
        P.prob_bank, P.out_bank, P.ln_bank, P.pos_bank, P.head_bank = bank[2:4], bank[4], bank[5], bank[6], bank[7]
        P.probs, P.shared_v = probs, None
        E = Phase()
        [E.by_pool, E.by_dve, E.by_act, E.mm, E.ev, E.st, E.turned, E.x] = sems("e", "by_pool by_dve by_act mm ev st turned x")
        share_norm(E, 4 * NB)
        E.ln_bank = bank[5]
        E.y_bank, E.turn_bank = bank[0:2], bank[2:4]

        def ln_group_stats(dve, q, g, prev):
            prev = prev + q.base
            wait(dve, q.aggr, prev)
            for k in range(4):
                last = dve.bn_stats(stats4[:, k, :], X[:, at(4 * g + k), :])
            last.then_inc(q.stats, 1)
            wait(dve, q.stats, prev + 1)
            wait(dve, q.xn, prev)
            wait(dve, q.var, prev)
            dve.memset(carrier[0:1, :], 0.0)
            for k in range(4):
                last = dve.bn_aggr(meanvar4[:, k, :], stats4[:, k, :])
            last.then_inc(q.aggr, 1)
            wait(dve, q.aggr, prev + 1)
            wait(dve, q.rstd, prev)
            dve.tensor_scalar(vareps4[:, :].unsqueeze(2), meanvar4[:, :, 1:2], LN_EPS, None, ALU.add).then_inc(q.var, 1)

        def ln_group_rstd(pool, q, n):
            wait(pool, q.var, q.base + n + 1)
            wait(pool, q.xn, q.base + n)
            pool.tensor_tensor(out=rstd4[:, :], in0=vareps4[:, :], in1=minus_half[:, 0:4], op=ALU.pow).then_inc(q.rstd, 1)

        def ln_group_apply(dve, q, g, n):
            wait(dve, q.rstd, q.base + n + 1)
            wait(dve, q.xnT_ps, q.base + n)
            for k in range(4):
                last = dve.tensor_scalar(xn4[:, k:k + 1, :], X[:, at(4 * g + k), :], meanvar4[:, k, 0:1], rstd4[:, k:k + 1],
                                         ALU.subtract, ALU.mult)
            last.then_inc(q.xn, 1)

        GATHER_POOL, GATHER_DVE, GATHER_ACT = (0, 4), (4, 6), (10, 6)

        def gather_weights(eng, copy, pair, k, share, sem):
            if not isinstance(pair, int) or pair > 0:
                eng.wait_ge(E.mm, 2 * pair + k - 1)
                eng.sem_inc(P.gate, 1)
            with eng.Fori(0, share[1]) as j:
                layer = eng.value_load(itok[0:1, at(32 * pair + 16 * k + share[0] + j)], min_val=0, max_val=NB - 1)
                copy(gathered[:, k, at(share[0] + j), :], ctxT[:, at(layer), :]).then_inc(sem, 1)

        def turn_group(pe, q, n):
            wait(pe, q.xn, q.base + n + 1)
            wait(pe, q.xnT, q.base + n)
            for k in range(4):
                last = pe.transpose(q.ln_bank[:, k * S:(k + 1) * S], xn4[:, k, :], ident)
            last.then_inc(q.xnT_ps, 1)
        F = Phase()
        [F.cast, F.gate, F.scores, F.route, F.split, F.cT_ps, F.cT, F.h1, F.h3, F.silu, F.gated, F.a, F.y,
         F.x] = sems("f", "cast gate scores route split cT_ps cT h1 h3 silu gated a y x")
        share_norm(F, 4 * NB + NB // 4)
        F.h1_bank, F.h3_bank = bank[0:2], bank[2:4]
        F.combine_bank, F.y_bank, F.ln_bank, F.gate_bank = bank[4], bank[5], bank[6], bank[7]
        NG = NB // 4
        ROUTE_STEPS = 29
        done = Phase()
        [done.out] = sems("done", "out")
        block = ctx.enter_context(nc.Block())

        def head4(ap):
            return ap.rearrange("s (r p) d -> s p r d", r=R)

        def ln_stats(dve, q, b, prev):
            prev = prev + q.base
            wait(dve, q.aggr, prev)
            dve.bn_stats(stats[:, :], X[:, at(b), :]).then_inc(q.stats, 1)
            wait(dve, q.stats, prev + 1)
            wait(dve, q.xn, prev)
            wait(dve, q.var, prev)
            dve.memset(carrier[0:1, :], 0.0)
            dve.bn_aggr(meanvar[:, :], stats[:, :]).then_inc(q.aggr, 1)
            wait(dve, q.aggr, prev + 1)
            wait(dve, q.rstd, prev)
            dve.tensor_scalar(vareps[:, :], meanvar[:, 1:2], LN_EPS, None, ALU.add).then_inc(q.var, 1)

        def turn_xn(pe, q, n, free, free_count):
            wait(pe, q.xn, q.base + n + 1)
            wait(pe, free, free_count)
            pe.transpose(q.ln_bank[:, 0:S], xn[:, 0, :], ident).then_inc(q.xnT_ps, 1)

        def save_xnT(act, q, n, dst, free, free_count):
            wait(act, q.xnT_ps, q.base + n + 1)
            wait(act, free, free_count)
            act.activation(dst, q.ln_bank[:, 0:S], ACT.Copy).then_inc(q.xnT, 1)

        def turn_heads(pe, q, src, src_sem, free_sem, free, sem, n):
            wait(pe, src_sem, n + 1)
            wait(pe, free_sem, free)
            for p in range(PT):
                last = pe.transpose(q.head_bank[:, p * S:(p + 1) * S], src[:, p, :, :].rearrange("s r k -> s (r k)"), ident)
            last.then_inc(sem, 1)

        def save_headsT(act, q, ps, sem, dst, n, free=None, free_count=0):
            wait(act, ps, n + 1)
            if free is not None:
                wait(act, free, free_count)
            act.activation(dst.rearrange("k p s -> k (p s)"), q.head_bank, ACT.Copy).then_inc(sem, 1)

        def turn_attn(pe, q, n):
            wait(pe, q.on, n + 1)
            wait(pe, q.aT, n)
            pe.transpose(q.out_bank[:, 144:144 + S], attn[:, 0, :, :].rearrange("s h d -> s (h d)"), ident).then_inc(q.aT_ps, 1)

        def save_attnT(act, q, n):
            wait(act, q.aT_ps, n + 1)
            wait(act, q.y, n)
            act.activation(attnT[:, :], q.out_bank[:, 144:144 + S], ACT.Copy).then_inc(q.aT, 1)

        def output(pe, q, n, weights):
            wait(pe, q.aT, n + 1)
            pe.matmul(q.out_bank[:, 272:272 + D], attnT[:, :], weights, start=True, stop=True).then_inc(q.y, 1)

        def residual_y(dve, q, n):
            wait(dve, q.y, n + 1)
            dve.tensor_tensor(X[:, at(n), :], X[:, at(n), :], q.out_bank[:, 272:272 + D].unsqueeze(1), ALU.add)\
               .then_inc(q.x, 1)

        def ln_rstd(pool, q, n):
            wait(pool, q.var, q.base + n + 1)
            wait(pool, q.xn, q.base + n)
            pool.tensor_tensor(out=rstd[:, :], in0=vareps[:, :], in1=minus_half[:, 0:1], op=ALU.pow).then_inc(q.rstd, 1)

        def ln_apply(dve, q, b, n):
            wait(dve, q.rstd, q.base + n + 1)
            wait(dve, q.xnT_ps, q.base + n)
            dve.tensor_scalar(xn[:, :, :], X[:, at(b), :], meanvar[:, 0:1], rstd[:, 0:1],
                              ALU.subtract, ALU.mult).then_inc(q.xn, 1)

        def row_max(dve, q, n, r):
            wait(dve, q.summed, n * R + r + 1)
            wait(dve, q.p, n * R + r - 1)
            scores = q.scores[r % 2]
            shape = [S, 2, 2] if len(scores.shape) == 4 else [S, PT]
            out = negmax[:, r % 2, :]
            if len(shape) == 3:
                out = out.rearrange("s (b h) -> s b h", b=2)
            dve.tensor_reduce(out, scores, AX.X, ALU.max, negate=True).then_inc(q.mx, 1)

        def exps(act, q, n, r):
            wait(act, q.mx, n * R + r + 1)
            wait(act, q.pT_ps, n * R + r - 1)
            for p in range(PT):
                last = act.activation(probs[:, r % 2, p, :], q.scores[r % 2][:, p, :], ACT.Exp,
                                      bias=negmax[:, r % 2, p:p + 1], scale=1.0)
            last.then_inc(q.p, 1)

        def turn_probs(pe, q, n, r):
            wait(pe, q.mixed, n * R + r + 1)
            wait(pe, q.pT, n * R + r - 1)
            for p in range(PT):
                last = pe.transpose(q.prob_bank[r % 2][:, p * S:(p + 1) * S], q.probs[:, r % 2, p, :], ident)
            last.then_inc(q.pT_ps, 1)

        def save_probsT(dve, q, n, r):
            wait(dve, q.pT_ps, n * R + r + 1)
            wait(dve, q.o, n * R + r - 1)
            dve.tensor_copy(probsT[:, r % 2, :, :].rearrange("s p k -> s (p k)"), q.prob_bank[r % 2]).then_inc(q.pT, 1)

        def weigh_values(pe, q, n, par, r):
            wait(pe, q.pT, n * R + r + 1)
            if r == 0:
                wait(pe, q.v, n + 1)
                wait(pe, q.out_free, n)
            for p in range(PT):
                v = values[:, par, r * PT + p, :] if q.shared_v is None else q.shared_v[:, par, :]
                last = pe.matmul(q.out_bank[p * GW:(p + 1) * GW, r * S:(r + 1) * S], v, probsT[:, r % 2, p, :],
                                 start=True, stop=True)
            last.then_inc(q.o, 1)

        def save_outT(act, q, n):
            wait(act, q.o, (n + 1) * R)
            wait(act, q.oT_ps, n)
            act.activation(outT[:, :, :].rearrange("k r s -> k (r s)"), q.out_bank, ACT.Copy).then_inc(q.oT, 1)

        def turn_out(pe, q, n):
            wait(pe, q.oT, n + 1)
            for r in range(R):
                last = pe.transpose(q.out_bank[:, r * S:(r + 1) * S], outT[:, r, :], ident)
            last.then_inc(q.oT_ps, 1)

        def normalise(dve, q, n, denominators=None):
            turned = q.out_bank.rearrange("s (h k) -> s h k", h=H)
            wait(dve, q.oT_ps, n + 1)
            wait(dve, q.on, n)
            dve.reciprocal(recip[:, :].unsqueeze(2), turned[:, :, HD:HD + 1] if denominators is None else denominators)\
               .then_inc(q.rec, 1)
            wait(dve, q.rec, n + 1)
            wait(dve, q.attn_free, n)
            dve.tensor_tensor(attn[:, 0, :, :], turned[:, :, 0:HD], recip[:, :].unsqueeze(2).broadcast_to([S, H, HD]),
                              ALU.mult).then_inc(q.on, 1)

        LOADS = 9 * 16
        LOADS_B = 7 * 16
        LOADS_C = 13 * 16
        LOADS_D = 12 * 16
        LOADS_F = 9 * 16

        @block.sync
        def _(sp):
            sp.dma_start(consts[:, :], t["consts"]).then_inc(ld.c, 16)
            for dst, src in [(w_dq, t["L0_attn_W_DQ"]), (w_uqT, t["L0_attn_W_UQ"]),
                             (w_dkv, t["L0_attn_W_DKV"]), (w_ukvT, t["L0_attn_W_UKV"]),
                             (w_qr, t["L0_attn_W_QR"]), (w_kr, t["L0_attn_W_KR"]),
                             (w_oT, t["L0_attn_W_O"]),
                             (qnw, t["L0_attn_q_norm_w"].partition_broadcast(128)),
                             (knw, t["L0_attn_k_norm_w"].partition_broadcast(128))]:
                sp.dma_start(dst[:, :], src).then_inc(ld.w, 16)
            for dst, src in [(w_qx[:, :], t["L0_xattn_Wq"]), (w_cx[:, :], t["L0_xattn_Wc"])]:
                sp.dma_start(dst, src).then_inc(ld.b, 16)
            sp.wait_ge(k0.kvzero, 1)
            for r in range(R):
                sp.dma_start(w_kvx[:, r, 0:2 * HD], t["L0_xattn_Wkv"]).then_inc(ld.b, 16)
            sp.dma_start(ctxT[:, :, :], t["ctx_1024"]).then_inc(ld.b, 16)
            for i, name in enumerate(["wf", "wi", "wc", "wo"]):
                sp.dma_start(wx[:, i, :], t["L0_ffn_" + name]).then_inc(ld.g, 16)
            for i, name in enumerate(["uf", "ui", "uc", "uo"]):
                sp.dma_start(uc[:, i, :], t["L0_ffn_" + name]).then_inc(ld.g, 16)
            for i, name in enumerate(["bf", "bi", "bc", "bo"]):
                sp.dma_start(gate_bias[:, i:i + 1], t["L0_ffn_" + name].rearrange("(m a) -> m a", a=1)).then_inc(ld.g, 16)
            sp.dma_start(cell0[:, :], t["L0_ffn_in_c"].rearrange("(m a) -> m a", a=1)).then_inc(ld.g, 16)
            for i, name in enumerate(["Wq", "Wk", "Wv"]):
                sp.dma_start(wqkv[:, i, :], t["L1_attn_" + name]).then_inc(ld.d, 16)
            sp.dma_start(w_p[:, :], t["L1_attn_Wp"]).then_inc(ld.d, 16)
            sp.dma_start(w_o1[:, :], t["L1_attn_Wo"]).then_inc(ld.d, 16)
            for i, name in enumerate(["bq", "u", "v", "bk", "bv", "bp", "bo"]):
                row = t["L1_attn_" + name]
                if len(row.shape) > 1:
                    row = row.rearrange("a h b p -> (a h b p)")
                sp.dma_start(bias_rows[:, i, :], row.partition_broadcast(S)).then_inc(ld.d, 16)

            def shift_positions(n, par):
                wait(sp, P.es, (n + 1) * R)
                sp.sem_inc(P.gate, 1)
                wait(sp, P.placed, 16 * (n - 1))
                sp.sem_inc(P.gate, 1)
                sp.dma_start(skew[par].rearrange("h (i c) -> i h c", i=S), pos_rows[:, par, :, :]).then_inc(P.skewed, 16)
                wait(sp, P.skewed, 16 * (n + 1))
                sp.sem_inc(P.gate, 1)
                wait(sp, P.add, (n - 1) * R)
                sp.sem_inc(P.gate, 1)
                sp.dma_start(pos_score[:, par, :, :], skew[par][:, S:S * (S + 1)].rearrange("h (i j) -> i h j", i=S))\
                  .then_inc(P.placed, 16)

            shift_positions(0, 0)
            shift_positions(1, 1)
            with sp.Fori(1, NB // 2) as pair:
                shift_positions(2 * pair, 0)
                shift_positions(2 * pair + 1, 1)
            sp.dma_start(itok[0:1, :], t["itok_S_0_31"].rearrange("(a s) -> a s", a=1)).then_inc(ld.e, 16)
            sp.dma_start(w_gate[:, :], t["L1_ffn_w_gate"]).then_inc(ld.f, 16)
            for dst, name in [(w_up1, "w1"), (w_up3, "w3")]:
                sp.dma_start(dst[:, 0:TILES - 1, :].rearrange("h t m -> h (t m)"),
                             t[f"L1_ffn_{name}_e"].rearrange("h e f -> h (e f)")).then_inc(ld.f, 16)
                sp.dma_start(dst[:, TILES - 1, :], t[f"L1_ffn_{name}_s"]).then_inc(ld.f, 16)
            pairs = t["L1_ffn_w2_e"].rearrange("f (t p) h -> p f t h", p=2)
            for p in range(2):
                sp.dma_start(w_down[p * FW:(p + 1) * FW, 0:TILES - 1, :], pairs[p]).then_inc(ld.f, 16)
            sp.dma_start(w_down[:, TILES - 1, :], t["L1_ffn_w2_s"]).then_inc(ld.f, 16)
            sp.dma_start(spread[:, :, :], t["spread"].rearrange("k (t m) -> k t m", t=TILES - 1)).then_inc(ld.f, 16)
            for g in range(NG):
                sp.wait_ge(F.x, g + 1)
                sp.dma_start(out[4 * g:4 * g + 4].rearrange("b s d -> s b d"), X[:, 4 * g:4 * g + 4, :]).then_inc(done.out, 16)
            sp.wait_ge(done.out, 16 * NG)


        @block.gpsimd
        def _(pool):
            pool.dma_start(X[:, :, :], t["x"].rearrange("b s d -> s b d")).then_inc(ld.x, 16)
            pool.memset(qpad[:, :, :, :], 0.0).then_inc(k0.zero, 1)
            pool.memset(kpad[:, :, :, :], 0.0).then_inc(k0.zero, 1)
            pool.memset(values[:, :, :, :], 0.0).then_inc(k0.ones, 1)
            pool.wait_ge(k0.ones, 1)
            pool.memset(values[:, :, :, HD:HD + 1], 1.0).then_inc(k0.ones, 1)
            pool.memset(minus_half[:, :], -0.5).then_inc(k0.half, 1)
            pool.memset(w_kvx[:, :, :], 0.0).then_inc(k0.kvzero, 1)
            pool.memset(v8[:, :, :], 0.0).then_inc(k0.kvzero, 1)
            pool.memset(q2pad[:, :, :, :], 0.0).then_inc(P.zeroed, 1)
            pool.memset(pos_rows[:, :, :, 0:1], 0.0).then_inc(P.zeroed, 1)
            pool.wait_ge(k0.half, 1)

            def residual(n):
                wait(pool, A.on, n + 1)
                pool.tensor_tensor(out=X[:, at(n), :], in0=X[:, at(n), :],
                                   in1=attn[:, :, :, :].rearrange("s a h d -> s a (h d)"), op=ALU.add).then_inc(A.x, 1)

            def body(b, par, left):
                if left >= 2:
                    ln_rstd(pool, A, b + 2)
                if not isinstance(b, int) or b > 0:
                    residual(b - 1)

            ln_rstd(pool, A, 0)
            ln_rstd(pool, A, 1)
            body_pairs(pool, body)
            residual(NB - 1)

            def cross_attention():
                def key_sum(n, par):
                    wait(pool, B.k, 2 * (n + 1))
                    pool.tensor_tensor(out=k3T[:, par, 64:128], in0=k3T[:, par, 0:64], in1=k3T[:, par, 128:192],
                                       op=ALU.add).then_inc(B.ksum, 1)

                def mix(n, r):
                    wait(pool, B.p, n * R + r + 1)
                    wait(pool, B.pT_ps, n * R + r - 1)
                    pool.tensor_tensor(out=probs[:, r % 2, :, :], in0=probs3[:, r % 2, :, 0:128],
                                       in1=probs3[:, r % 2, :, 64:192], op=ALU.add).then_inc(B.ab, 1)

                def body(b, par, left):
                    mix(b, 0)
                    mix(b, 1)
                    mix(b, 2)
                    if left >= 2:
                        ln_rstd(pool, B, b + 2)
                    mix(b, 3)
                    if left >= 2:
                        key_sum(b + 2, par)

                pool.wait_ge(A.x, NB)
                ln_rstd(pool, B, 0)
                key_sum(0, 0)
                ln_rstd(pool, B, 1)
                key_sum(1, 1)
                body_pairs(pool, body)

            cross_attention()

            def recurrence():
                pool.wait_ge(B.x, NB)
                ln_rstd(pool, C, 0)
                with pool.Fori(0, NB - 1) as s:
                    ln_rstd(pool, C, s + 1)

            recurrence()

            def relative_attention():
                def place_v(n, par):
                    wait(pool, P.vst, n + 1)
                    wait(pool, P.o, (n - 1) * R)
                    pool.tensor_tensor(out=values[:, par, :, 0:HD], in0=v_stage[:, :, :],
                                       in1=bias_rows[:, 4, :].rearrange("s (h d) -> s h d", h=H), op=ALU.add).then_inc(P.v, 1)

                def output_bias(n):
                    wait(pool, P.xn, P.base + n + 1)
                    pool.tensor_tensor(out=X[:, at(n), :], in0=X[:, at(n), :], in1=bias_rows[:, 6:7, :], op=ALU.add)\
                        .then_inc(P.bias, 1)

                def body(b, par, left):
                    if left >= 1:
                        place_v(b + 1, 1 - par)
                    if left >= 3:
                        ln_rstd(pool, P, b + 3)
                        output_bias(b + 3)

                pool.wait_ge(C.x, NB // 4)
                pool.wait_ge(ld.d, LOADS_D)
                for n in range(3):
                    ln_rstd(pool, P, n)
                    output_bias(n)
                    if n == 1:
                        place_v(0, 0)
                body_pairs(pool, body, tail=2)

            relative_attention()

            def position_weights():
                def gather(pair, k):
                    gather_weights(pool, pool.tensor_copy, pair, k, GATHER_POOL, E.by_pool)

                pool.wait_ge(P.x, NB)
                pool.wait_ge(ld.e, 16)
                ln_group_rstd(pool, E, 0)
                gather(0, 0)
                with pool.Fori(1, NB // 4) as g:
                    ln_group_rstd(pool, E, g)
                gather(0, 1)
                with pool.Fori(1, 4) as pair:
                    gather(pair, 0)
                    gather(pair, 1)

            position_weights()

            def experts():
                pool.wait_ge(E.x, NG)
                ln_group_rstd(pool, F, 0)
                with pool.Fori(1, NG) as g:
                    ln_group_rstd(pool, F, g)

            experts()

        @block.vector
        def _(dve):
            dve.wait_ge(ld.c, 16)
            dve.wait_ge(ld.w, LOADS)
            dve.tensor_copy(identb[:, :], ident).then_inc(k0.cast, 1)
            dve.tensor_copy(causal4[:, :, :], consts[:, C_CAUSAL:C_CAUSAL + S].unsqueeze(1).broadcast_to([S, PT, S])).then_inc(k0.cast, 1)
            dve.tensor_scalar(qnws[:, :], qnw[:, :], SCALE, None, ALU.mult).then_inc(k0.qnws, 1)
            dve.wait_ge(k0.qnws, 1)
            dve.tensor_tensor(qkw[:, 0, :], qnws[:, :], knw[:, :], ALU.mult).then_inc(k0.qkw, 1)
            dve.wait_ge(k0.fold, 1)
            dve.tensor_copy(avT[:, :], bank[0][0:HD, 0:HD]).then_inc(k0.fold, 1)
            dve.wait_ge(k0.fold, 3)
            dve.tensor_copy(small[:, 0:2, :], bank[1][0:HD, 0:2 * HD].rearrange("e (w d) -> e w d", w=2)).then_inc(k0.fold, 1)
            dve.tensor_tensor(small[:, 2, :], bank[1][0:HD, 2 * HD:3 * HD], qnws[0:HD, :], ALU.mult).then_inc(k0.fold, 1)
            dve.tensor_copy(small[:, 3, :], bank[1][0:HD, 3 * HD:4 * HD]).then_inc(k0.fold, 1)
            dve.wait_ge(k0.fold, 7)
            hmask = consts[:, C_HEAD:C_HEAD + H].unsqueeze(2).broadcast_to([128, H, HD])
            for w in range(4):
                dve.tensor_tensor(wblk[:, w, :, :],
                                  bank[2][:, w * HD:(w + 1) * HD].unsqueeze(1).broadcast_to([128, H, HD]),
                                  hmask, ALU.mult).then_inc(k0.fold, 1)

            heads = A.proj_bank.rearrange("s (w h d) -> s w h d", w=4, h=H)

            def rms_sum(n):
                wait(dve, A.sq, n + 1)
                wait(dve, A.root, ROOT_STEPS * n)
                dve.tensor_reduce(ms[:, :], squares[:, :, :], AX.X, ALU.add).then_inc(A.ms, 1)
                wait(dve, A.ms, n + 1)
                wait(dve, A.rr, n)
                dve.tensor_scalar(ms_eps[:, :], ms[:, :], 1.0 / HD, RMS_EPS, ALU.mult, ALU.add).then_inc(A.root, 1)

            def rms_root(n):
                wait(dve, A.root, n * ROOT_STEPS + 1)
                wait(dve, A.kn1, n)
                dve.tensor_scalar(rr[:, :].bitcast(I32), ms_eps[:, :].bitcast(I32), -0.5, RSQRT_GUESS,
                                  ALU.mult, ALU.add).then_inc(A.root, 1)
                for i in range(NEWTON):
                    wait(dve, A.root, n * ROOT_STEPS + 3 * i + 2)
                    dve.tensor_tensor(rr_tmp[:, :], rr[:, :], rr[:, :], ALU.mult).then_inc(A.root, 1)
                    wait(dve, A.root, n * ROOT_STEPS + 3 * i + 3)
                    dve.scalar_tensor_tensor(out=rr_tmp[:, :], in0=rr_tmp[:, :], scalar=-0.5, in1=ms_eps[:, :],
                                             op0=ALU.mult, op1=ALU.mult).then_inc(A.root, 1)
                    wait(dve, A.root, n * ROOT_STEPS + 3 * i + 4)
                    dve.scalar_tensor_tensor(out=rr[:, :], in0=rr_tmp[:, :], scalar=1.5, in1=rr[:, :],
                                             op0=ALU.add, op1=ALU.mult).then_inc(A.root if i < NEWTON - 1 else A.rr, 1)

            def query(n):
                wait(dve, A.rr, n + 1)
                wait(dve, A.v, n + 1)
                wait(dve, A.qT_ps, n)
                dve.tensor_tensor(qpad[:, :, :, 0:HD], head4(heads[:, 0, :, :]),
                                  head4(rr[:, 0:H].unsqueeze(2).broadcast_to([S, H, HD])), ALU.mult).then_inc(A.qn, 1)

            def key_1(n):
                wait(dve, A.kn2, n)
                dve.tensor_tensor(kn1[:, :, :], heads[:, 1, :, :], rr[:, H:2 * H].unsqueeze(2).broadcast_to([S, H, HD]),
                                  ALU.mult).then_inc(A.kn1, 1)

            def key_2(n):
                wait(dve, A.kn1, n + 1)
                wait(dve, A.kn, n)
                dve.tensor_tensor(kn2[:, :, :], kn1[:, :, :], qkw[:, :, :].broadcast_to([S, H, HD]), ALU.mult).then_inc(A.kn2, 1)

            def key_3(n):
                wait(dve, A.kn2, n + 1)
                wait(dve, A.kT_ps, n)
                dve.tensor_tensor(kpad[:, :, :, 0:HD], head4(kn2[:, :, :]), head4(heads[:, 2, :, :]), ALU.add).then_inc(A.kn, 1)

            def body(b, par, left):
                if left >= 1:
                    rms_sum(b + 1)
                row_max(dve, A, b, 1)
                if left >= 1:
                    rms_root(b + 1)
                save_probsT(dve, A, b, 0)
                if not isinstance(b, int) or b > 0:
                    normalise(dve, A, b - 1)
                if left >= 1:
                    query(b + 1)
                row_max(dve, A, b, 2)
                if left >= 1:
                    key_1(b + 1)
                save_probsT(dve, A, b, 1)
                if left >= 1:
                    key_2(b + 1)
                if left >= 2:
                    ln_stats(dve, A, b + 2, b + 2)
                row_max(dve, A, b, 3)
                if left >= 1:
                    key_3(b + 1)
                save_probsT(dve, A, b, 2)
                if left >= 2:
                    ln_apply(dve, A, b + 2, b + 2)
                save_probsT(dve, A, b, 3)
                if left >= 1:
                    row_max(dve, A, b + 1, 0)

            dve.wait_ge(ld.x, 16)
            dve.wait_ge(k0.zero, 2)
            ln_stats(dve, A, 0, 0)
            ln_apply(dve, A, 0, 0)
            rms_sum(0)
            rms_root(0)
            query(0)
            key_1(0)
            key_2(0)
            key_3(0)
            ln_stats(dve, A, 1, 1)
            ln_apply(dve, A, 1, 1)
            row_max(dve, A, 0, 0)
            body_pairs(dve, body)
            normalise(dve, A, NB - 1)

            def cross_attention():
                def body(b, par, left):
                    row_max(dve, B, b, 1)
                    save_probsT(dve, B, b, 0)
                    if not isinstance(b, int) or b > 0:
                        normalise(dve, B, b - 1, denom[:, 1 - par, :].unsqueeze(2))
                    row_max(dve, B, b, 2)
                    save_probsT(dve, B, b, 1)
                    if not isinstance(b, int) or b > 0:
                        residual_y(dve, B, b - 1)
                    if left >= 2:
                        ln_stats(dve, B, b + 2, b + 2)
                    row_max(dve, B, b, 3)
                    save_probsT(dve, B, b, 2)
                    if left >= 2:
                        ln_apply(dve, B, b + 2, b + 2)
                    save_probsT(dve, B, b, 3)
                    if left >= 1:
                        row_max(dve, B, b + 1, 0)

                dve.wait_ge(ld.b, LOADS_B)
                dve.tensor_scalar(w_qx[:, :], w_qx[:, :], SCALE, None, ALU.mult).then_inc(k0.wqx, 1)
                dve.wait_ge(A.x, NB)
                ln_stats(dve, B, 0, 0)
                ln_apply(dve, B, 0, 0)
                ln_stats(dve, B, 1, 1)
                ln_apply(dve, B, 1, 1)
                row_max(dve, B, 0, 0)
                body_pairs(dve, body)
                normalise(dve, B, NB - 1, denom[:, 1, :].unsqueeze(2))
                residual_y(dve, B, NB - 1)

            cross_attention()

            def recurrence():
                def cell(s):
                    wait(dve, C.f, s + 1)
                    dve.scalar_tensor_tensor(out=keep[:, :], in0=gates[:, 0, :], scalar=1.0, in1=cell2[:, :],
                                             op0=ALU.add, op1=ALU.mult).then_inc(C.keep, 1)
                    wait(dve, C.c, s + 1)
                    dve.scalar_tensor_tensor(out=fresh[:, :], in0=gates[:, 1, :], scalar=1.0, in1=gates[:, 2, :],
                                             op0=ALU.add, op1=ALU.mult).then_inc(C.fresh, 1)
                    wait(dve, C.fresh, s + 1)
                    dve.scalar_tensor_tensor(out=cell2[:, :], in0=keep[:, :], scalar=0.5, in1=fresh[:, :],
                                             op0=ALU.mult, op1=ALU.add).then_inc(C.cell, 1)

                dve.wait_ge(ld.g, LOADS_C)
                dve.tensor_scalar(uc[:, :, :], uc[:, :, :], 0.5, None, ALU.mult).then_inc(C.scaled, 1)
                dve.tensor_scalar(half_bias[:, :], gate_bias[:, 0:2], 0.5, None, ALU.mult).then_inc(C.scaled, 1)
                dve.memset(cell2[:, :], 0.0).then_inc(C.zero_cell, 1)
                dve.wait_ge(C.zero_cell, 1)
                dve.tensor_scalar(cell2[:, :], cell2[:, :], cell0[:, 0:1], None, ALU.add).then_inc(C.zero_cell, 1)
                dve.wait_ge(C.zero_cell, 2)
                dve.tensor_scalar(cell2[:, :], cell2[:, :], 2.0, None, ALU.mult).then_inc(C.cell, 1)
                ln_stats(dve, C, 0, 0)
                ln_apply(dve, C, 0, 0)
                dve.wait_ge(C.cell, 1)
                with dve.Fori(0, NB - 1) as s:
                    ln_stats(dve, C, s + 1, s + 1)
                    ln_apply(dve, C, s + 1, s + 1)
                    cell(s)
                cell(NB - 1)

                def residual_h(g, par):
                    wait(dve, C.hT_ps, g + 1)
                    dve.tensor_tensor(X[:, at(4 * g, 4), :], X[:, at(4 * g, 4), :],
                                      C.hT_bank[par].rearrange("s (b d) -> s b d", b=4), ALU.add).then_inc(C.x, 1)

                with dve.Fori(0, NB // 8) as pair:
                    residual_h(2 * pair, 0)
                    residual_h(2 * pair + 1, 1)

            recurrence()

            def relative_attention():
                proj = P.ln_bank[:, 128:512].rearrange("s (w h d) -> s w h d", w=3, h=H)

                def rows(i):
                    return bias_rows[:, i, :].rearrange("s (h d) -> s h d", h=H)

                def position_query(n):
                    wait(dve, P.proj, n + 1)
                    wait(dve, P.q2T_ps, n)
                    dve.tensor_tensor(q2pad[:, :, :, 0:HD], head4(proj[:, 0, :, :]),
                                      head4(bias_q[:, 1, :].rearrange("s (h d) -> s h d", h=H)), ALU.add).then_inc(P.q2, 1)

                def content(n):
                    wait(dve, P.qT_ps, n)
                    dve.tensor_tensor(qpad[:, :, :, 0:HD], head4(proj[:, 0, :, :]),
                                      head4(bias_q[:, 0, :].rearrange("s (h d) -> s h d", h=H)), ALU.add).then_inc(P.q, 1)
                    wait(dve, P.kT_ps, n)
                    dve.tensor_tensor(kpad[:, :, :, 0:HD], head4(proj[:, 1, :, :]), head4(rows(3)), ALU.add).then_inc(P.k, 1)
                    wait(dve, P.v, n)
                    dve.tensor_copy(v_stage[:, :, :], proj[:, 2, :, :]).then_inc(P.vst, 1)

                def add_max(n, par, r):
                    wait(dve, P.s, n * R + r + 1)
                    if r == 0:
                        wait(dve, P.placed, 16 * (n + 1))
                    wait(dve, P.p, n * R + r - 1)
                    dve.tensor_tensor(summed[:, r % 2, :, :], P.score_bank[r % 2],
                                      pos_score[:, par, r * PT:(r + 1) * PT, :], ALU.add).then_inc(P.add, 1)
                    row_max(dve, P, n, r)

                def body(b, par, left):
                    if left >= 2:
                        position_query(b + 2)
                    add_max(b, par, 1)
                    save_probsT(dve, P, b, 0)
                    if left >= 2:
                        content(b + 2)
                    if not isinstance(b, int) or b > 0:
                        normalise(dve, P, b - 1)
                    add_max(b, par, 2)
                    save_probsT(dve, P, b, 1)
                    if not isinstance(b, int) or b > 0:
                        residual_y(dve, P, b - 1)
                    add_max(b, par, 3)
                    if left >= 3:
                        ln_stats(dve, P, b + 3, b + 3)
                    save_probsT(dve, P, b, 2)
                    if left >= 3:
                        ln_apply(dve, P, b + 3, b + 3)
                    save_probsT(dve, P, b, 3)
                    if left >= 1:
                        add_max(b + 1, 1 - par, 0)

                dve.wait_ge(ld.d, LOADS_D)
                dve.tensor_scalar(wqkv[:, 0, :], wqkv[:, 0, :], SCALE, None, ALU.mult).then_inc(P.bqs, 1)
                dve.tensor_tensor(bias_q[:, :, :], bias_rows[:, 0:1, :].broadcast_to([S, 2, D]), bias_rows[:, 1:3, :],
                                  ALU.add).then_inc(P.bqs, 1)
                dve.wait_ge(P.bqs, 2)
                dve.tensor_scalar(bias_q[:, :, :], bias_q[:, :, :], SCALE, None, ALU.mult).then_inc(P.bqs, 1)
                dve.wait_ge(P.bqs, 3)
                dve.wait_ge(C.x, NB // 4)
                dve.wait_ge(P.pos, 1)
                dve.tensor_tensor(kpad[:, :, :, 0:HD],
                                  head4(P.pos_bank[:, 0:D].rearrange("s (h d) -> s h d", h=H)), head4(rows(5)),
                                  ALU.add).then_inc(P.pos, 1)
                dve.wait_ge(P.pos, 3)
                for n in range(2):
                    ln_stats(dve, P, n, n)
                    ln_apply(dve, P, n, n)
                    position_query(n)
                    content(n)
                ln_stats(dve, P, 2, 2)
                ln_apply(dve, P, 2, 2)
                add_max(0, 0, 0)
                body_pairs(dve, body, tail=2)
                normalise(dve, P, NB - 1)
                residual_y(dve, P, NB - 1)

            relative_attention()

            def position_weights():
                dve.wait_ge(ld.e, 16)
                dve.wait_ge(ld.f, LOADS_F)
                dve.tensor_copy(spreadb[:, :, :], spread[:, :, :]).then_inc(F.cast, 1)
                dve.wait_ge(P.x, NB)
                ln_group_stats(dve, E, 0, 0)
                ln_group_apply(dve, E, 0, 0)
                with dve.Fori(1, NB // 4) as g:
                    ln_group_stats(dve, E, g, g)
                    ln_group_apply(dve, E, g, g)

                def gather(pair, k):
                    gather_weights(dve, dve.tensor_copy, pair, k, GATHER_DVE, E.by_dve)

                gather(0, 0)
                gather(0, 1)
                with dve.Fori(1, 4) as pair:
                    gather(pair, 0)
                    gather(pair, 1)

                def residual_group(g, par):
                    wait(dve, E.turned, g + 1)
                    dve.tensor_tensor(X[:, at(4 * g, 4), :], X[:, at(4 * g, 4), :],
                                      E.turn_bank[par].rearrange("s (b d) -> s b d", b=4), ALU.add).then_inc(E.x, 1)

                with dve.Fori(0, NB // 8) as pair:
                    residual_group(2 * pair, 0)
                    residual_group(2 * pair + 1, 1)

            position_weights()

            def experts():
                def step(g, k, emit):
                    wait(dve, F.route, g * ROUTE_STEPS + k)
                    emit().then_inc(F.route, 1)

                def tt(out, a, b, op):
                    return lambda: dve.tensor_tensor(out, a, b, op)

                member = scores4[:, :, :].rearrange("s k (g i j) -> s (k g) i j", g=4, i=2)
                hi = pair_hi.rearrange("s k g i -> s (k g) i")
                lo = pair_lo.rearrange("s k g i -> s (k g) i")
                best1 = best[:, 0, :, :].rearrange("s k g -> s (k g)")
                best2 = best[:, 1, :, :].rearrange("s k g -> s (k g)")
                gscore = group_score[:, :, :]
                by_group = [S, 4, 4, 4]
                by_expert = [S, 4, EX, EX]
                lower_g = consts[:, C_TIE_G:C_TIE_G + 16].rearrange("s (a g h) -> s a g h", a=1, g=4).broadcast_to(by_group)
                lower_e = consts[:, C_TIE_E:C_TIE_E + EX * EX].rearrange("s (a e f) -> s a e f", a=1, e=EX)\
                    .broadcast_to(by_expert)
                allowed = group_rank[:, :, :].unsqueeze(3).broadcast_to(by_group)
                scores_g = scores4[:, :, :].rearrange("s k (g e) -> s k g e", g=4)
                flat = masked[:, :, :, :].rearrange("s k g e -> s k (g e)")
                part = [parts3[:, :, i, :] for i in range(3)]
                ROUTE = [
                    tt(hi, member[:, :, :, 0], member[:, :, :, 1], ALU.max),
                    tt(lo, member[:, :, :, 0], member[:, :, :, 1], ALU.min),
                    tt(best1, hi[:, :, 0], hi[:, :, 1], ALU.max),
                    tt(best2, hi[:, :, 0], hi[:, :, 1], ALU.min),
                    tt(hi[:, :, 0], lo[:, :, 0], lo[:, :, 1], ALU.max),
                    tt(best2, best2, hi[:, :, 0], ALU.max),
                    tt(gscore.rearrange("s k g -> s (k g)"), best1, best2, ALU.add),
                    tt(group_gt[:, :, :, :], gscore.unsqueeze(2).broadcast_to(by_group), gscore.unsqueeze(3).broadcast_to(by_group), ALU.is_gt),
                    tt(group_eq[:, :, :, :], gscore.unsqueeze(2).broadcast_to(by_group), gscore.unsqueeze(3).broadcast_to(by_group), ALU.is_equal),
                    tt(group_eq[:, :, :, :], group_eq[:, :, :, :], lower_g, ALU.mult),
                    tt(group_gt[:, :, :, :], group_gt[:, :, :, :], group_eq[:, :, :, :], ALU.add),
                    lambda: dve.tensor_reduce(group_rank[:, :, :], group_gt[:, :, :, :], AX.X, ALU.add),
                    lambda: dve.tensor_scalar(group_rank[:, :, :], group_rank[:, :, :], 2.0, None, ALU.is_lt),
                    tt(masked[:, :, :, :], scores_g, allowed, ALU.mult),
                    lambda: dve.scalar_tensor_tensor(out=masked[:, :, :, :], in0=allowed, scalar=-1.0, in1=masked[:, :, :, :],
                                                     op0=ALU.add, op1=ALU.add),
                    tt(expert_gt[:, :, :, :], flat.unsqueeze(2).broadcast_to(by_expert), flat.unsqueeze(3).broadcast_to(by_expert), ALU.is_gt),
                    tt(expert_eq[:, :, :, :], flat.unsqueeze(2).broadcast_to(by_expert), flat.unsqueeze(3).broadcast_to(by_expert), ALU.is_equal),
                    tt(expert_eq[:, :, :, :], expert_eq[:, :, :, :], lower_e, ALU.mult),
                    tt(expert_gt[:, :, :, :], expert_gt[:, :, :, :], expert_eq[:, :, :, :], ALU.add),
                    lambda: dve.tensor_reduce(expert_rank[:, :, :], expert_gt[:, :, :, :], AX.X, ALU.add),
                    lambda: dve.scalar_tensor_tensor(out=chosen[:, :, :], in0=expert_rank[:, :, :], scalar=4.0, in1=scores4[:, :, :],
                                                     op0=ALU.is_lt, op1=ALU.mult),
                    lambda: dve.tensor_reduce(total[:, :], chosen[:, :, :], AX.X, ALU.add),
                    lambda: dve.tensor_scalar(total[:, :], total[:, :], 1e-6, None, ALU.add),
                    lambda: dve.reciprocal(total[:, :], total[:, :]),
                    tt(combine[:, :, :], chosen[:, :, :], total[:, :].unsqueeze(2).broadcast_to([S, 4, EX]), ALU.mult),
                    lambda: dve.tensor_copy(part[0], combine[:, :, :]),
                    tt(combine[:, :, :], combine[:, :, :], part[0], ALU.subtract),
                    lambda: dve.tensor_copy(part[1], combine[:, :, :]),
                    tt(combine[:, :, :], combine[:, :, :], part[1], ALU.subtract),
                ]
                assert len(ROUTE) == ROUTE_STEPS

                def route(g, first, last):
                    for k in range(first, min(last, ROUTE_STEPS)):
                        if k == 0:
                            wait(dve, F.scores, g + 1)
                        if k == ROUTE_STEPS - 4:
                            wait(dve, F.cT_ps, g)
                        step(g, k, ROUTE[k])
                    if first <= ROUTE_STEPS < last:
                        wait(dve, F.route, (g + 1) * ROUTE_STEPS)
                        dve.tensor_copy(part[2], combine[:, :, :]).then_inc(F.split, 1)

                def tile(g, gpar, k):
                    n, par = g * TILES + k, (gpar + k) % 2
                    routed = g * (TILES - 1) + min(k, TILES - 1)
                    wait(dve, F.silu, n + 1)
                    wait(dve, F.h3, n + 1)
                    if k < TILES - 1:
                        wait(dve, F.a, routed)
                        dve.tensor_tensor(gated[:, :], silu[:, par, :], F.h3_bank[par], ALU.mult).then_inc(F.gated, 1)
                        wait(dve, F.gated, n + 1)
                        wait(dve, F.y, n - 1)
                        dve.tensor_tensor(hidden_a[:, par, :], gated[:, :], F.combine_bank, ALU.mult).then_inc(F.a, 1)
                    else:
                        wait(dve, F.y, n - 1)
                        dve.tensor_tensor(hidden_a[:, par, :], silu[:, par, :], F.h3_bank[par], ALU.mult).then_inc(F.gated, 1)

                def residual_y4(g):
                    wait(dve, F.y, (g + 1) * TILES)
                    dve.tensor_tensor(X[:, at(4 * g, 4), :], X[:, at(4 * g, 4), :],
                                      F.y_bank.rearrange("s (b d) -> s b d", b=4), ALU.add).then_inc(F.x, 1)

                def body(g, par, left):
                    tile(g, par, 0)
                    if not isinstance(g, int) or g > 0:
                        residual_y4(g - 1)
                    for k in range(1, TILES):
                        tile(g, par, k)
                        if left >= 1 and k >= 2:
                            route(g + 1, 5 * (k - 2), 5 * (k - 1))
                        if left >= 2 and k == TILES - 2:
                            ln_group_stats(dve, F, g + 2, g + 2)
                    if left >= 2:
                        ln_group_apply(dve, F, g + 2, g + 2)

                dve.wait_ge(E.x, NG)
                ln_group_stats(dve, F, 0, 0)
                ln_group_apply(dve, F, 0, 0)
                ln_group_stats(dve, F, 1, 1)
                ln_group_apply(dve, F, 1, 1)
                route(0, 0, ROUTE_STEPS + 1)
                group_pairs(dve, body)
                residual_y4(NG - 1)

            experts()

        @block.scalar
        def _(act):
            def square_heads(n):
                wait(act, A.proj, n + 1)
                wait(act, A.ms, n)
                act.activation(squares[:, :, :].rearrange("s h d -> s (h d)"), A.proj_bank[:, 0:2 * D], ACT.Square).then_inc(A.sq, 1)

            def save_values(n, par):
                wait(act, A.proj, n + 1)
                wait(act, A.o, (n - 1) * R)
                act.activation(values[:, par, :, 0:HD], A.proj_bank[:, 3 * D:4 * D].rearrange("s (h d) -> s h d", h=H),
                               ACT.Copy).then_inc(A.v, 1)

            def body(b, par, left):
                if not isinstance(b, int) or b > 0:
                    save_outT(act, A, b - 1)
                if left >= 1:
                    square_heads(b + 1)
                    save_values(b + 1, 1 - par)
                exps(act, A, b, 1)
                exps(act, A, b, 2)
                if left >= 1:
                    save_headsT(act, A, A.qT_ps, A.qT, qT[:, 1 - par, :, :], b + 1)
                exps(act, A, b, 3)
                if left >= 1:
                    save_headsT(act, A, A.kT_ps, A.kT, kT[:, 1 - par, :, :], b + 1)
                if left >= 2:
                    save_xnT(act, A, b + 2, xnT[:, :], A.proj, b + 2)
                if left >= 1:
                    exps(act, A, b + 1, 0)

            act.wait_ge(k0.ones, 2)
            save_xnT(act, A, 0, xnT[:, :], A.proj, 0)
            square_heads(0)
            save_values(0, 0)
            save_headsT(act, A, A.qT_ps, A.qT, qT[:, 0, :, :], 0)
            save_headsT(act, A, A.kT_ps, A.kT, kT[:, 0, :, :], 0)
            save_xnT(act, A, 1, xnT[:, :], A.proj, 1)
            exps(act, A, 0, 0)
            body_pairs(act, body)
            save_outT(act, A, NB - 1)

            def cross_attention():
                def save_q(n):
                    wait(act, B.proj, n + 1)
                    wait(act, B.qT_ps, n)
                    act.activation(qpad[:, :, :, 0:HD], head4(B.ln_bank[:, 128:256].rearrange("s (h d) -> s h d", h=H)),
                                   ACT.Copy).then_inc(B.q, 1)

                def save_kv(n, par):
                    wait(act, B.s, (n - 1) * R)
                    for c in range(2):
                        act.activation(k3T[:, par, 128 * c:128 * c + 64], B.ln_bank[:, 256 + 64 * c:320 + 64 * c], ACT.Copy).then_inc(B.k, 1)
                    wait(act, B.vT_ps, n)
                    act.activation(kvT[:, :], B.ln_bank[:, 256:384], ACT.Copy).then_inc(B.kv, 1)

                def save_v(n, par):
                    wait(act, B.vT_ps, n + 1)
                    wait(act, B.o, (n - 1) * R)
                    act.activation(v8[:, par, 0:HD], B.ln_bank[:, 384 + HD:384 + 2 * HD], ACT.Copy).then_inc(B.v, 1)

                def exps3(n, par, r):
                    wait(act, B.mx, n * R + r + 1)
                    wait(act, B.ab, n * R + r - 1)
                    wait(act, B.on, n - 1)
                    for p in range(PT):
                        h = r * PT + p
                        last = act.activation(probs3[:, r % 2, p, :], B.scores[r % 2][:, p // 2, p % 2, :], ACT.Exp,
                                              bias=negmax[:, r % 2, p:p + 1], scale=1.0, accum_out=denom[:, par, h:h + 1])
                    last.then_inc(B.p, 1)

                def body(b, par, left):
                    if left >= 1:
                        save_v(b + 1, 1 - par)
                    if not isinstance(b, int) or b > 0:
                        save_outT(act, B, b - 1)
                    exps3(b, par, 1)
                    if not isinstance(b, int) or b > 0:
                        save_attnT(act, B, b - 1)
                    exps3(b, par, 2)
                    if left >= 1:
                        save_headsT(act, B, B.qT_ps, B.qT, qT[:, 1 - par, :, :], b + 1)
                    exps3(b, par, 3)
                    if left >= 2:
                        save_xnT(act, B, b + 2, xnT[:, :], B.proj, b + 2)
                        save_q(b + 2)
                        save_kv(b + 2, par)
                    if left >= 1:
                        exps3(b + 1, 1 - par, 0)

                act.wait_ge(A.x, NB)
                act.wait_ge(k0.kvzero, 2)
                save_xnT(act, B, 0, xnT[:, :], B.proj, 0)
                save_q(0)
                save_kv(0, 0)
                save_v(0, 0)
                save_headsT(act, B, B.qT_ps, B.qT, qT[:, 0, :, :], 0)
                save_xnT(act, B, 1, xnT[:, :], B.proj, 1)
                save_q(1)
                save_kv(1, 1)
                exps3(0, 0, 0)
                body_pairs(act, body)
                save_outT(act, B, NB - 1)
                save_attnT(act, B, NB - 1)

            cross_attention()

            def recurrence():
                def activate(s, par):
                    wait(act, C.g, s + 1)
                    bank_g = C.gate_bank[par].rearrange("m (g s) -> m g s", g=4)
                    act.activation(gates[:, 0, :], bank_g[:, 0, :], ACT.Tanh, bias=half_bias[:, 0:1], scale=0.5).then_inc(C.f, 1)
                    act.activation(gates[:, 1, :], bank_g[:, 1, :], ACT.Tanh, bias=half_bias[:, 1:2], scale=0.5)
                    act.activation(gates[:, 2, :], bank_g[:, 2, :], ACT.Tanh, bias=gate_bias[:, 2:3], scale=1.0).then_inc(C.c, 1)

                act.wait_ge(B.x, NB)
                act.wait_ge(C.scaled, 2)
                save_xnT(act, C, 0, seqT[:, 0, :], C.xnT, 0)
                with act.Fori(0, NB // 2 - 1) as pair:
                    for k in range(2):
                        s = 2 * pair + k
                        save_xnT(act, C, s + 1, seqT[:, at(s + 1), :], C.xnT, 0)
                        activate(s, k)
                save_xnT(act, C, NB - 1, seqT[:, NB - 1, :], C.xnT, 0)
                activate(NB - 2, 0)
                activate(NB - 1, 1)

                def squash(g, par):
                    wait(act, C.z, g + 1)
                    wait(act, C.hT_ps, g - 1)
                    act.activation(hidden[:, par, :, :].rearrange("o b s -> o (b s)"), C.h_bank[par], ACT.Tanh,
                                   bias=gate_bias[:, 3:4], scale=1.0).then_inc(C.h, 1)

                squash(0, 0)
                squash(1, 1)
                with act.Fori(1, NB // 8) as pair:
                    squash(2 * pair, 0)
                    squash(2 * pair + 1, 1)

            recurrence()

            def relative_attention():
                def save_rows(n, par, r):
                    wait(act, P.e, n * R + r + 1)
                    if r == 0:
                        wait(act, P.skewed, 16 * (n - 1))
                    act.activation(pos_rows[:, par, r * PT:(r + 1) * PT, 1:S + 1],
                                   P.pos_bank.rearrange("s (p k) -> s p k", p=PT), ACT.Copy).then_inc(P.es, 1)

                def save_q2T(n):
                    save_headsT(act, P, P.q2T_ps, P.q2T, q2T[:, :, :], n, P.e, n * R)

                def save_qT(n, par):
                    save_headsT(act, P, P.qT_ps, P.qT, qT[:, par, :, :], n, P.s, (n - 1) * R)

                def save_kT(n, par):
                    save_headsT(act, P, P.kT_ps, P.kT, kT[:, par, :, :], n)

                def body(b, par, left):
                    if not isinstance(b, int) or b > 0:
                        save_outT(act, P, b - 1)
                    exps(act, P, b, 1)
                    if not isinstance(b, int) or b > 0:
                        save_attnT(act, P, b - 1)
                    if left >= 2:
                        save_q2T(b + 2)
                    exps(act, P, b, 2)
                    if left >= 2:
                        save_rows(b + 2, par, 0)
                        save_qT(b + 2, par)
                    exps(act, P, b, 3)
                    if left >= 2:
                        save_rows(b + 2, par, 1)
                        save_kT(b + 2, par)
                        save_rows(b + 2, par, 2)
                    if left >= 1:
                        exps(act, P, b + 1, 0)
                    if left >= 2:
                        save_rows(b + 2, par, 3)
                    if left >= 3:
                        save_xnT(act, P, b + 3, xnT[:, :], P.proj, b + 3)

                act.wait_ge(C.x, NB // 4)
                act.wait_ge(P.zeroed, 2)
                act.wait_ge(P.pos, 3)
                act.activation(posT[:, :, :].rearrange("k p s -> k (p s)"), P.head_bank, ACT.Copy).then_inc(P.pos, 1)
                for n in range(2):
                    save_xnT(act, P, n, xnT[:, :], P.proj, n)
                    save_q2T(n)
                    save_qT(n, n)
                    save_kT(n, n)
                    for r in range(R):
                        save_rows(n, n, r)
                save_xnT(act, P, 2, xnT[:, :], P.proj, 2)
                exps(act, P, 0, 0)
                body_pairs(act, body, tail=2)
                save_outT(act, P, NB - 1)
                save_attnT(act, P, NB - 1)

            relative_attention()

            def position_weights():
                act.wait_ge(P.x, NB)
                act.wait_ge(ld.e, 16)
                act.wait_ge(F.cast, 1)
                with act.Fori(0, NB // 4) as g:
                    wait(act, E.xnT_ps, E.base + g + 1)
                    act.activation(seqT[:, at(4 * g, 4), :], E.ln_bank.rearrange("d (b s) -> d b s", b=4), ACT.Copy).then_inc(E.xnT, 1)

                def gather(pair, k):
                    gather_weights(act, act.copy, pair, k, GATHER_ACT, E.by_act)

                def save_y(pair, k):
                    wait(act, E.mm, 2 * pair + k + 1)
                    act.activation(yT[:, :, at(32 * pair + 16 * k, 16)],
                                   E.y_bank[k].rearrange("o (s b) -> o b s", b=NB), ACT.Copy).then_inc(E.ev, 1)

                gather(0, 0)
                gather(0, 1)
                with act.Fori(0, 3) as pair:
                    for k in range(2):
                        save_y(pair, k)
                        gather(pair + 1, k)
                save_y(3, 0)
                save_y(3, 1)

                def stage(g, par):
                    wait(act, E.turned, g - 1)
                    act.activation(y_stage[:, par, :, :], yT[:, at(4 * g, 4), :], ACT.Copy).then_inc(E.st, 1)

                act.wait_ge(E.ev, 8)
                stage(0, 0)
                stage(1, 1)
                with act.Fori(1, NB // 8) as pair:
                    stage(2 * pair, 0)
                    stage(2 * pair + 1, 1)

            position_weights()

            def experts():
                def save_group(g, gpar):
                    wait(act, F.xnT_ps, F.base + g + 1)
                    act.activation(xT[:, gpar, :, :].rearrange("d b s -> d (b s)"), F.ln_bank, ACT.Copy).then_inc(F.xnT, 1)

                def gate(g):
                    wait(act, F.gate, g + 1)
                    wait(act, F.split, g)
                    act.activation(scores4[:, :, :].rearrange("s k e -> s (k e)"), F.gate_bank[:, 0:4 * EX], ACT.Sigmoid)\
                       .then_inc(F.scores, 1)

                def save_combine(g, gpar):
                    wait(act, F.cT_ps, g + 1)
                    act.activation(combineT[:, gpar, :, :].rearrange("e b s -> e (b s)"), F.gate_bank[0:3 * EX, :], ACT.Copy)\
                       .then_inc(F.cT, 1)

                def tile(g, gpar, k):
                    n, par = g * TILES + k, (gpar + k) % 2
                    wait(act, F.h1, n + 1)
                    wait(act, F.gated, n - 1)
                    act.activation(silu[:, par, :], F.h1_bank[par], ACT.Silu).then_inc(F.silu, 1)

                def body(g, par, left):
                    for k in range(TILES):
                        tile(g, par, k)
                        if left >= 1 and k == 0:
                            save_group(g + 1, 1 - par)
                        if left >= 1 and k == 1:
                            gate(g + 1)
                    if left >= 1:
                        save_combine(g + 1, 1 - par)

                act.wait_ge(E.x, NG)
                save_group(0, 0)
                gate(0)
                save_combine(0, 0)
                group_pairs(act, body)

            experts()

        @block.tensor
        def _(pe):
            pe.wait_ge(ld.c, 16)
            pe.wait_ge(ld.w, LOADS)
            pe.matmul(bank[0][0:HD, 0:HD], w_ukvT[:, HD:2 * HD], w_dkv[:, :], start=True, stop=True).then_inc(k0.fold, 1)
            pe.matmul(bank[1][0:HD, 0:HD], w_dq[:, :], w_uqT[:, :], start=True, stop=True)
            pe.matmul(bank[1][0:HD, HD:2 * HD], w_dkv[:, :], w_ukvT[:, 0:HD], start=True, stop=True)
            pe.matmul(bank[1][0:HD, 2 * HD:3 * HD], w_kr[:, :], w_qr[:, :], start=True, stop=True)
            pe.wait_ge(k0.fold, 2)
            pe.matmul(bank[1][0:HD, 3 * HD:4 * HD], avT[:, :], w_oT[:, :], start=True, stop=True).then_inc(k0.fold, 1)
            pe.wait_ge(k0.fold, 6)
            pe.matmul(bank[2][:, 0:4 * HD], consts[0:HD, C_REP:C_REP + 128], small[:, :, :].rearrange("e w d -> e (w d)"),
                      start=True, stop=True).then_inc(k0.fold, 1)

            def project(n):
                wait(pe, A.xnT, n + 1)
                wait(pe, A.kn, n)
                wait(pe, A.v, n)
                pe.matmul(A.proj_bank, xnT[:, :], wblk[:, :, :, :].rearrange("e w h d -> e (w h d)"),
                          start=True, stop=True).then_inc(A.proj, 1)

            def score(n, par, r):
                if r == 0:
                    wait(pe, A.kT, n + 1)
                wait(pe, A.p, n * R + r - 1)
                pe.matmul(bank[r % 2], identb[:, :], causal4[:, :, :].rearrange("s p k -> s (p k)"),
                          start=True, stop=False, skip_group_check=True)
                for p in range(PT):
                    last = pe.matmul(bank[r % 2][:, p * S:(p + 1) * S], qT[r * GW:r * GW + HD, par, p, :],
                                     kT[r * GW:r * GW + HD, par, p, :], start=False, stop=(p == PT - 1),
                                     skip_group_check=True)
                last.then_inc(A.s, 1)

            def body(b, par, left):
                turn_probs(pe, A, b, 0)
                if not isinstance(b, int) or b > 0:
                    turn_out(pe, A, b - 1)
                score(b, par, 2)
                turn_probs(pe, A, b, 1)
                weigh_values(pe, A, b, par, 0)
                score(b, par, 3)
                if left >= 1:
                    turn_heads(pe, A, qpad, A.qn, A.kT, b + 1, A.qT_ps, b + 1)
                turn_probs(pe, A, b, 2)
                weigh_values(pe, A, b, par, 1)
                if left >= 1:
                    turn_heads(pe, A, kpad, A.kn, A.qT, b + 2, A.kT_ps, b + 1)
                if left >= 2:
                    turn_xn(pe, A, b + 2, A.xnT, b + 2)
                turn_probs(pe, A, b, 3)
                weigh_values(pe, A, b, par, 2)
                if left >= 1:
                    score(b + 1, 1 - par, 0)
                weigh_values(pe, A, b, par, 3)
                if left >= 1:
                    score(b + 1, 1 - par, 1)
                if left >= 2:
                    project(b + 2)

            pe.wait_ge(k0.fold, 11)
            pe.wait_ge(k0.cast, 2)
            turn_xn(pe, A, 0, A.xnT, 0)
            project(0)
            turn_heads(pe, A, qpad, A.qn, A.kT, 0, A.qT_ps, 0)
            turn_heads(pe, A, kpad, A.kn, A.qT, 1, A.kT_ps, 0)
            turn_xn(pe, A, 1, A.xnT, 1)
            project(1)
            score(0, 0, 0)
            score(0, 0, 1)
            body_pairs(pe, body)
            turn_out(pe, A, NB - 1)

            def cross_attention():
                def project(n):
                    wait(pe, B.xnT, B.base + n + 1)
                    pe.matmul(B.ln_bank[:, 128:256], xnT[:, :], w_qx[:, :], start=True, stop=True)
                    pe.matmul(B.ln_bank[:, 256:384].unsqueeze(1), w_kvx[:, :, :].rearrange("e r k -> e (r k)"), ctxT[:, at(n), :],
                              start=True, stop=True).then_inc(B.proj, 1)

                def turn_v(n, par):
                    wait(pe, B.kv, n + 1)
                    pe.transpose(B.ln_bank[:, 384:512],
                                 kvT[:, :], ident).then_inc(B.vT_ps, 1)

                def score(n, par, r):
                    if r == 0:
                        wait(pe, B.qT, n + 1)
                        wait(pe, B.ksum, n + 1)
                    wait(pe, B.p, n * R + r - 1)
                    for p in range(PT):
                        last = pe.matmul(B.scores[r % 2][:, p // 2, p % 2, :], qT[r * GW:r * GW + HD, par, p, :],
                                         k3T[r * GW:r * GW + HD, par, :], start=True, stop=True)
                    last.then_inc(B.s, 1)

                def body(b, par, left):
                    later = not isinstance(b, int) or b > 0
                    turn_probs(pe, B, b, 0)
                    if later:
                        turn_out(pe, B, b - 1)
                    score(b, par, 2)
                    turn_probs(pe, B, b, 1)
                    if later:
                        turn_attn(pe, B, b - 1)
                    score(b, par, 3)
                    if later:
                        output(pe, B, b - 1, w_cx[:, :])
                    if left >= 1:
                        wait(pe, B.v, b + 2)
                        turn_heads(pe, B, qpad, B.q, B.qT, b + 1, B.qT_ps, b + 1)
                    weigh_values(pe, B, b, par, 0)
                    turn_probs(pe, B, b, 2)
                    weigh_values(pe, B, b, par, 1)
                    if left >= 2:
                        turn_xn(pe, B, b + 2, B.qT, b + 2)
                    turn_probs(pe, B, b, 3)
                    weigh_values(pe, B, b, par, 2)
                    if left >= 2:
                        project(b + 2)
                    if left >= 1:
                        score(b + 1, 1 - par, 0)
                    weigh_values(pe, B, b, par, 3)
                    if left >= 1:
                        score(b + 1, 1 - par, 1)
                    if left >= 2:
                        turn_v(b + 2, par)

                pe.wait_ge(A.x, NB)
                pe.wait_ge(k0.wqx, 1)
                turn_xn(pe, B, 0, B.qT, 0)
                project(0)
                turn_v(0, 0)
                wait(pe, B.v, 1)
                turn_heads(pe, B, qpad, B.q, B.qT, 0, B.qT_ps, 0)
                turn_xn(pe, B, 1, B.qT, 1)
                project(1)
                turn_v(1, 1)
                score(0, 0, 0)
                score(0, 0, 1)
                body_pairs(pe, body)
                turn_out(pe, B, NB - 1)
                turn_attn(pe, B, NB - 1)
                output(pe, B, NB - 1, w_cx[:, :])

            cross_attention()

            def recurrence():
                def inputs(s, par):
                    wait(pe, C.xnT, C.base + s + 1)
                    wait(pe, C.c, s - 1)
                    for g in range(3):
                        pe.matmul(C.gate_bank[par][:, g * S:(g + 1) * S].unsqueeze(1), wx[:, g, :], seqT[:, at(s), :],
                                  start=(g == 0), stop=False, skip_group_check=True)

                def state(s, par):
                    wait(pe, C.cell, s + 1)
                    for g in range(3):
                        last = pe.matmul(C.gate_bank[par][:, g * S:(g + 1) * S], uc[:, g, :], cell2[:, :],
                                         start=False, stop=(g == 2), skip_group_check=True)
                    last.then_inc(C.g, 1)

                pe.wait_ge(B.x, NB)
                pe.wait_ge(C.scaled, 2)
                turn_xn(pe, C, 0, C.xnT, C.base)
                inputs(0, 0)
                turn_xn(pe, C, 1, C.xnT, C.base + 1)
                inputs(1, 1)
                state(0, 0)
                with pe.Fori(0, NB // 2 - 1) as pair:
                    for k in range(2):
                        s = 2 * pair + k
                        turn_xn(pe, C, s + 2, C.xnT, C.base + s + 2)
                        inputs(s + 2, k)
                        state(s + 1, 1 - k)
                state(NB - 1, 1)

                def outputs(g, par):
                    wait(pe, C.h, g - 1)
                    pe.matmul(C.h_bank[par].rearrange("o (b s) -> o b s", b=4), wx[:, 3, :], seqT[:, at(4 * g, 4), :],
                              start=True, stop=False)
                    pe.matmul(C.h_bank[par].rearrange("o (b s) -> o b s", b=4), uc[:, 3, :],
                              cell2[:, :].unsqueeze(1).broadcast_to([D, 4, S]), start=False, stop=True).then_inc(C.z, 1)

                def turn_hidden(g, par):
                    wait(pe, C.h, g + 1)
                    wait(pe, C.x, g - 1)
                    for k in range(4):
                        last = pe.transpose(C.hT_bank[par][:, k * S:(k + 1) * S], hidden[:, par, k, :], ident)
                    last.then_inc(C.hT_ps, 1)

                pe.wait_ge(C.cell, NB + 1)
                outputs(0, 0)
                outputs(1, 1)
                turn_hidden(0, 0)
                turn_hidden(1, 1)
                with pe.Fori(1, NB // 8) as pair:
                    outputs(2 * pair, 0)
                    outputs(2 * pair + 1, 1)
                    turn_hidden(2 * pair, 0)
                    turn_hidden(2 * pair + 1, 1)

            recurrence()

            def relative_attention():
                def project(n):
                    wait(pe, P.xnT, P.base + n + 1)
                    pe.matmul(P.ln_bank[:, 128:512], xnT[:, :], wqkv[:, :, :].rearrange("e w d -> e (w d)"),
                              start=True, stop=True).then_inc(P.proj, 1)

                def turn_q2(n):
                    turn_heads(pe, P, q2pad, P.q2, P.kT, n, P.q2T_ps, n)

                def turn_q(n):
                    turn_heads(pe, P, qpad, P.q, P.q2T, n + 1, P.qT_ps, n)

                def turn_k(n):
                    turn_heads(pe, P, kpad, P.k, P.qT, n + 1, P.kT_ps, n)

                def position_score(n, r):
                    wait(pe, P.q2T, n + 1)
                    wait(pe, P.es, n * R + r)
                    for p in range(PT):
                        last = pe.matmul(P.pos_bank[:, p * S:(p + 1) * S], q2T[r * GW:r * GW + HD, p, :],
                                         posT[r * GW:r * GW + HD, p, :], start=True, stop=True)
                    last.then_inc(P.e, 1)

                def score(n, par, r):
                    if r == 0:
                        wait(pe, P.kT, n + 1)
                    wait(pe, P.add, n * R + r - 1)
                    for p in range(PT):
                        last = pe.matmul(P.score_bank[r % 2][:, p, :], qT[r * GW:r * GW + HD, par, p, :],
                                         kT[r * GW:r * GW + HD, par, p, :], start=True, stop=True)
                    last.then_inc(P.s, 1)

                def body(b, par, left):
                    later = not isinstance(b, int) or b > 0
                    turn_probs(pe, P, b, 0)
                    if later:
                        turn_out(pe, P, b - 1)
                    score(b, par, 2)
                    turn_probs(pe, P, b, 1)
                    if later:
                        turn_attn(pe, P, b - 1)
                    score(b, par, 3)
                    if left >= 2:
                        turn_q2(b + 2)
                    if later:
                        output(pe, P, b - 1, w_o1[:, :])
                    weigh_values(pe, P, b, par, 0)
                    turn_probs(pe, P, b, 2)
                    if left >= 2:
                        position_score(b + 2, 0)
                        turn_q(b + 2)
                    weigh_values(pe, P, b, par, 1)
                    if left >= 2:
                        position_score(b + 2, 1)
                        turn_k(b + 2)
                    turn_probs(pe, P, b, 3)
                    if left >= 2:
                        position_score(b + 2, 2)
                    weigh_values(pe, P, b, par, 2)
                    if left >= 1:
                        score(b + 1, 1 - par, 0)
                    if left >= 2:
                        position_score(b + 2, 3)
                    weigh_values(pe, P, b, par, 3)
                    if left >= 1:
                        score(b + 1, 1 - par, 1)
                    if left >= 3:
                        turn_xn(pe, P, b + 3, P.vst, b + 3)
                        project(b + 3)

                pe.wait_ge(ld.d, LOADS_D)
                pe.wait_ge(P.bqs, 1)
                pe.wait_ge(C.x, NB // 4)
                pe.matmul(P.pos_bank[:, 0:D], consts[:, C_SIN:C_SIN + S], w_p[:, :], start=True, stop=True).then_inc(P.pos, 1)
                pe.wait_ge(P.pos, 2)
                for p in range(PT):
                    last = pe.transpose(P.head_bank[:, p * S:(p + 1) * S], kpad[:, p, :, :].rearrange("s r k -> s (r k)"), ident)
                last.then_inc(P.pos, 1)
                pe.wait_ge(P.pos, 4)
                pe.wait_ge(P.zeroed, 2)
                for n in range(2):
                    turn_xn(pe, P, n, P.vst, n)
                    project(n)
                    turn_q2(n)
                    turn_q(n)
                    turn_k(n)
                    for r in range(R):
                        position_score(n, r)
                turn_xn(pe, P, 2, P.vst, 2)
                project(2)
                score(0, 0, 0)
                score(0, 0, 1)
                body_pairs(pe, body, tail=2)
                turn_out(pe, P, NB - 1)
                turn_attn(pe, P, NB - 1)
                output(pe, P, NB - 1, w_o1[:, :])

            relative_attention()

            def position_weights():
                pe.wait_ge(P.x, NB)
                turn_group(pe, E, 0)
                with pe.Fori(1, NB // 4) as g:
                    turn_group(pe, E, g)

                def multiply(pair, k):
                    wait(pe, E.by_pool, GATHER_POOL[1] * (2 * pair + k + 1))
                    wait(pe, E.by_dve, GATHER_DVE[1] * (2 * pair + k + 1))
                    wait(pe, E.by_act, GATHER_ACT[1] * (2 * pair + k + 1))
                    wait(pe, E.ev, 2 * pair + k - 1)
                    for j in range(16):
                        last = pe.matmul(E.y_bank[k][:, j * NB:(j + 1) * NB].unsqueeze(2), gathered[:, k, j, :],
                                         seqT[:, :, at(32 * pair + 16 * k + j)], start=True, stop=True)
                    last.then_inc(E.mm, 1)

                def turn_back(g, par):
                    wait(pe, E.st, g + 1)
                    wait(pe, E.x, g - 1)
                    for k in range(4):
                        last = pe.transpose(E.turn_bank[par][:, k * S:(k + 1) * S], y_stage[:, par, k, :], ident)
                    last.then_inc(E.turned, 1)

                pe.wait_ge(E.xnT, E.base + NB // 4)
                multiply(0, 0)
                multiply(0, 1)
                with pe.Fori(1, 4) as pair:
                    multiply(pair, 0)
                    multiply(pair, 1)
                turn_back(0, 0)
                turn_back(1, 1)
                with pe.Fori(1, NB // 8) as pair:
                    turn_back(2 * pair, 0)
                    turn_back(2 * pair + 1, 1)

            position_weights()

            def experts():
                def gate(g, gpar):
                    wait(pe, F.xnT, F.base + g + 1)
                    wait(pe, F.cT, g)
                    for k in range(4):
                        last = pe.matmul(F.gate_bank[:, k * EX:(k + 1) * EX], xT[:, gpar, k, :], w_gate[:, :], start=True, stop=True)
                    last.then_inc(F.gate, 1)

                def turn_combine(g):
                    wait(pe, F.split, g + 1)
                    for k in range(4):
                        last = pe.matmul(F.gate_bank[0:3 * EX, k * S:(k + 1) * S], parts3[:, k, :, :].rearrange("s c e -> s (c e)"),
                                         identb[:, :], start=True, stop=True)
                    last.then_inc(F.cT_ps, 1)

                def up(g, gpar, k):
                    n, par = g * TILES + k, (gpar + k) % 2
                    x = xT[:, gpar, :, :].rearrange("d b s -> d (b s)")
                    wait(pe, F.silu, n - 1)
                    pe.matmul(F.h1_bank[par], w_up1[:, k, :], x, start=True, stop=True).then_inc(F.h1, 1)
                    wait(pe, F.gated, n - 1)
                    last = pe.matmul(F.h3_bank[par], w_up3[:, k, :], x, start=True, stop=True)
                    if k < TILES - 1:
                        if k == 0:
                            wait(pe, F.cT, g + 1)
                        wait(pe, F.a, g * (TILES - 1) + k)
                        last = pe.matmul(F.combine_bank, spreadb[:, k, :], combineT[:, gpar, :, :].rearrange("e b s -> e (b s)"),
                                         start=True, stop=True)
                    last.then_inc(F.h3, 1)

                def down(g, gpar, k):
                    n, par = g * TILES + k, (gpar + k) % 2
                    if k == 0:
                        wait(pe, F.x, g)
                    if k < TILES - 1:
                        wait(pe, F.a, g * (TILES - 1) + k + 1)
                    else:
                        wait(pe, F.gated, n + 1)
                    for b in range(4):
                        last = pe.matmul(F.y_bank[:, b * D:(b + 1) * D], hidden_a[:, par, b * S:(b + 1) * S], w_down[:, k, :],
                                         start=(k == 0 and b == 0), stop=(k == TILES - 1 and b == 3), skip_group_check=True)
                    last.then_inc(F.y, 1)

                def body(g, par, left):
                    for k in range(TILES):
                        up(g, par, k)
                        if k > 0:
                            down(g, par, k - 1)
                        elif not isinstance(g, int) or g > 0:
                            down(g - 1, 1 - par, TILES - 1)
                        if left >= 1 and k == 0:
                            turn_group(pe, F, g + 1)
                        if left >= 1 and k == 1:
                            gate(g + 1, 1 - par)
                    if left >= 1:
                        turn_combine(g + 1)

                pe.wait_ge(ld.f, LOADS_F)
                pe.wait_ge(F.cast, 1)
                pe.wait_ge(E.x, NG)
                turn_group(pe, F, 0)
                gate(0, 0)
                turn_combine(0)
                group_pairs(pe, body)
                down(NG - 1, 1, TILES - 1)

            experts()


_INS = ['x', 'ctx_1024', 'itok_S_0_31',
        'L0_attn_W_DQ', 'L0_attn_W_UQ', 'L0_attn_W_DKV', 'L0_attn_W_UKV', 'L0_attn_W_QR', 'L0_attn_W_KR',
        'L0_attn_W_O', 'L0_attn_q_norm_w', 'L0_attn_k_norm_w', 'L0_xattn_Wq', 'L0_xattn_Wkv', 'L0_xattn_Wc',
        'L0_ffn_wf', 'L0_ffn_uf', 'L0_ffn_bf', 'L0_ffn_wi', 'L0_ffn_ui', 'L0_ffn_bi', 'L0_ffn_wc', 'L0_ffn_uc',
        'L0_ffn_bc', 'L0_ffn_wo', 'L0_ffn_uo', 'L0_ffn_bo', 'L0_ffn_in_c', 'L1_attn_Wq', 'L1_attn_bq',
        'L1_attn_Wk', 'L1_attn_bk', 'L1_attn_Wv', 'L1_attn_bv', 'L1_attn_Wp', 'L1_attn_bp', 'L1_attn_Wo',
        'L1_attn_bo', 'L1_attn_u', 'L1_attn_v', 'L1_ffn_w_gate', 'L1_ffn_w1_e', 'L1_ffn_w3_e', 'L1_ffn_w2_e',
        'L1_ffn_w1_s', 'L1_ffn_w3_s', 'L1_ffn_w2_s']

_TURNED = ['ctx_1024', 'L0_ffn_wf', 'L0_ffn_wi', 'L0_ffn_wc', 'L0_ffn_wo', 'L0_ffn_uf', 'L0_ffn_ui', 'L0_ffn_uc',
           'L0_ffn_uo', 'L1_ffn_w_gate', 'L1_ffn_w1_s', 'L1_ffn_w3_s', 'L1_ffn_w2_s', 'L1_ffn_w1_e', 'L1_ffn_w2_e', 'L1_ffn_w3_e',
           'L0_attn_W_UQ', 'L0_attn_W_UKV', 'L0_attn_W_O']


def _constants(np):
    c = np.zeros((128, C_END), np.float32)
    c[:, C_ID:C_ID + 128] = np.eye(128)
    q, k = np.arange(128)[:, None], np.arange(128)[None, :]
    c[:, C_CAUSAL:C_CAUSAL + 128] = np.where(k > q, -1e30, 0.0)
    c[:, C_HEAD:C_HEAD + H] = (q // HD == np.arange(H)[None, :])
    c[0:HD, C_REP:C_REP + 128] = (k % HD == np.arange(HD)[:, None])
    pos, idx = np.arange(S, dtype=np.float32), np.arange(D // 2, dtype=np.float32)
    inv = (np.float32(1.0) / np.float32(10000.0) ** (np.float32(2.0) * idx / np.float32(D))).astype(np.float32)
    ang = pos[None, :] * inv[:, None]
    c[:, C_SIN:C_SIN + S] = np.concatenate([np.sin(ang), np.cos(ang)], 0)
    c[:, C_TIE_G:C_TIE_G + 16] = np.tril(np.ones((4, 4)), -1).reshape(1, -1)
    c[:, C_TIE_E:C_TIE_E + EX * EX] = np.tril(np.ones((EX, EX)), -1).reshape(1, -1)
    return c


def _spread(np):
    e, col = np.arange(EX)[:, None], np.arange(EX * FW)[None, :]
    return np.tile((col // FW == e).astype(np.float32), (3, 1))


def kernel(**inputs):
    import numpy as _np
    import concourse.bacc as _bacc
    from concourse import mybir as _mybir
    from concourse.bass_utils import run_bass_kernel_spmd as _run

    nc = _bacc.Bacc("TRN2", target_bir_lowering=False, num_devices=1)
    arrays, tensors = {}, {}
    given = {name: _np.ascontiguousarray(inputs[name]) for name in _INS}
    for name in _TURNED:
        given[name] = _np.ascontiguousarray(_np.moveaxis(given[name], -1, 0))
    given["consts"] = _constants(_np)
    given["spread"] = _spread(_np)
    for name, a in given.items():
        arrays[f"in_{name}_dram"] = a
        tensors[name] = nc.dram_tensor(f"in_{name}_dram", a.shape, _mybir.dt.from_np(a.dtype), kind="ExternalInput").ap()
    out = nc.dram_tensor("out_0_dram", (NB, S, D), _mybir.dt.float32, kind="ExternalOutput").ap()
    decoder(nc, tensors, out)
    r = _run(nc, [arrays], core_ids=[0])
    return r.results[0]["out_0_dram"]
```

```python
from contextlib import ExitStack

import concourse.bass as bass
from concourse import mybir

F32 = mybir.dt.float32
BF16 = mybir.dt.bfloat16
I32 = mybir.dt.int32
ALU = mybir.AluOpType
ACT = mybir.ActivationFunctionType
AX = mybir.AxisListType

NB, S, D = 32, 128, 128
H, HD = 16, 8
R, PT = 4, 4
GW = 32
LN_EPS = 1e-5
RMS_EPS = 1.1920929e-07
SCALE = float(HD) ** -0.5
LATENT, ROPE = 64, 64
STACK, USED = 64, 48
LEFT_SLOTS = ((0, 3, 1), (3, 2, 1), (5, 1, 1))
RIGHT_SLOTS = ((1, 3, 2), (2, 2, 2), (0, 1, 1))
SPLIT_STEPS = 4
QUERY, KEY = 1, 2

C_ID, C_CAUSAL, C_HEAD, C_REP, C_SIN = 0, 128, 256, 272, 400
C_TIE_G, C_TIE_E, C_PARTS = 528, 544, 800
C_END = 802
EX, FW = 16, 64
TILES = EX * FW // 128 + 1


class Phase:
    pass


def wait(eng, sem, count):
    if isinstance(count, int) and count <= 0:
        return
    eng.wait_ge(sem, count)


def at(i, n=1):
    return bass.ds(i, n)


MANY = 99


def body_pairs(eng, body, tail=1):
    body(0, 0, NB - 1)
    body(1, 1, NB - 2)
    with eng.Fori(1, NB // 2 - tail) as pair:
        b = pair * 2
        body(b, 0, MANY)
        body(b + 1, 1, MANY)
    for b in range(NB - 2 * tail, NB):
        body(b, b % 2, NB - 1 - b)


def group_pairs(eng, body):
    groups = NB // 4
    body(0, 0, groups - 1)
    body(1, 1, groups - 2)
    with eng.Fori(1, groups // 2 - 1) as pair:
        g = pair * 2
        body(g, 0, MANY)
        body(g + 1, 1, MANY)
    body(groups - 2, 0, 1)
    body(groups - 1, 1, 0)


def decoder(nc, t, out):
    with ExitStack() as ctx:
        def sb(name, shape, dt=F32):
            return ctx.enter_context(nc.sbuf_tensor(name, shape, dt))

        def sems(prefix, names):
            return [ctx.enter_context(nc.semaphore(f"{prefix}_{n}")) for n in names.split()]

        X = sb("X", [S, NB, D])
        consts = sb("consts", [128, C_END])
        ident = consts[:, C_ID:C_ID + 128]
        identb = sb("identb", [128, 128], BF16)
        causal4 = sb("causal4", [128, PT, 128], BF16)
        psum = ctx.enter_context(nc.psum_tensor("psum", [128, 8, 512], F32))
        bank = [psum[:, i, :] for i in range(8)]
        quads = [b.rearrange("s (p k) -> s p k", p=PT) for b in bank]

        stats = sb("stats", [S, 6])
        meanvar = sb("meanvar", [S, 2])
        carrier = sb("carrier", [1, 1])
        vareps = sb("vareps", [S, 1])
        rstd = sb("rstd", [S, 1])
        minus_half = sb("minus_half", [S, 32])
        xn = sb("xn", [S, 1, D])
        xnT = sb("xnT", [D, S])
        squares = sb("squares", [S, 2 * H, HD])
        ms = sb("ms", [S, 2 * H])
        ms_eps = sb("ms_eps", [S, 2 * H])
        rr = sb("rr", [S, 2 * H])
        kn1 = sb("kn1", [S, H, HD])
        kn2 = sb("kn2", [S, H, HD])
        qT = sb("qT", [128, 2, H // 2, S], BF16)
        kT = sb("kT", [128, 2, H // 2, S], BF16)
        values = sb("values", [S, 2, H, GW])
        outT = sb("outT", [128, R, S])
        negmax = sb("negmax", [S, 2, PT])
        probs = sb("probs", [S, 2, PT, S])
        probsT = sb("probsT", [S, 2, PT, S])
        recip = sb("recip", [S, H])
        attn = sb("attn", [S, 1, H, HD])
        w_dq = sb("w_dq", [LATENT, HD])
        w_uqT = sb("w_uqT", [LATENT, HD])
        w_dkv = sb("w_dkv", [2 * LATENT, HD])
        w_ukvT = sb("w_ukvT", [2 * LATENT, 2 * HD])
        w_qr = sb("w_qr", [ROPE, HD])
        w_kr = sb("w_kr", [ROPE, HD])
        w_oT = sb("w_oT", [HD, HD])
        qnw = sb("qnw", [128, HD])
        qnws = sb("qnws", [128, HD])
        knw = sb("knw", [128, HD])
        qkw = sb("qkw", [128, 1, HD])
        avT = sb("avT", [HD, HD])
        small = sb("small", [HD, 4, HD])
        wblk = sb("wblk", [128, 4, H, HD])

        attnT = sb("attnT", [H * HD, S])
        stacks = sb("stacks", [S, 3, H, STACK], BF16)
        staged = sb("staged", [S, 3, H, HD])
        rest = sb("rest", [S, H, HD])
        v_stage = sb("v_stage", [S, 2, H, HD])
        KEYS = 192
        ctxT = sb("ctxT", [D, NB, S])
        w_qx = sb("w_qx", [D, D])
        w_kv = sb("w_kv", [D, 2 * HD])
        w_kvx = sb("w_kvx", [D, 2, STACK // HD, HD])
        w_cx = sb("w_cx", [D, D])
        k3T = sb("k3T", [128, 2, KEYS])
        key_top = sb("key_top", [128, KEYS], BF16)
        key_rest = sb("key_rest", [128, KEYS])
        kstack = sb("kstack", [128, 2, KEYS], BF16)
        kvT = sb("kvT", [128, S])
        v8 = sb("v8", [S, 2, GW])
        probs3 = sb("probs3", [S, 2, PT, KEYS])
        denom = sb("denom", [S, 2, H])
        wx = sb("wx", [D, 4, D])
        uc = sb("uc", [D, 4, D])
        gate_bias = sb("gate_bias", [D, 4])
        cell0 = sb("cell0", [D, 1])
        half_bias = sb("half_bias", [D, 2])
        cell2 = sb("cell2", [D, S])
        gates = sb("gates", [D, 3, S])
        keep = sb("keep", [D, S])
        fresh = sb("fresh", [D, S])
        seqT = sb("seqT", [D, NB, S])
        hidden = sb("hidden", [D, 2, 4, S])
        wqkv = sb("wqkv", [D, 3, D])
        w_p = sb("w_p", [D, D])
        w_o1 = sb("w_o1", [D, D])
        bias_rows = sb("bias_rows", [S, 7, D])
        bias_q = sb("bias_q", [S, 2, D])
        Q2, Q, K = 0, 1, 2
        q2T = sb("q2T", [128, H // 2, S], BF16)
        posT = sb("posT", [128, H // 2, S], BF16)
        pos_rows = sb("pos_rows", [S, 2, H, S + 1])
        pos_score = sb("pos_score", [S, 2, H, S])
        summed = sb("summed", [S, 2, PT, S])
        skew = [nc.dram_tensor(f"skew{i}", (H, S * (S + 1)), F32, kind="Internal").ap() for i in range(2)]
        stats4 = sb("stats4", [S, 4, 6])
        meanvar4 = sb("meanvar4", [S, 4, 2])
        vareps4 = sb("vareps4", [S, 4])
        rstd4 = sb("rstd4", [S, 4])
        xn4 = sb("xn4", [S, 4, D])
        itok = sb("itok", [1, S], I32)
        gathered = pos_score[:, :, :, :]
        yT = sb("yT", [D, NB, S])
        y_stage = hidden[:, :, :, :]
        w_gate = sb("w_gate", [D, EX])
        w_up1 = sb("w_up1", [D, TILES, 128])
        w_up3 = sb("w_up3", [D, TILES, 128])
        w_down = sb("w_down", [128, TILES, D])
        spread = yT[0:3 * EX, 0:TILES - 1, :]
        spreadb = sb("spreadb", [3 * EX, TILES - 1, 128], BF16)
        xT = summed[:, :, :, :]
        scores4 = sb("scores4", [S, 4, EX])
        top = sb("top", [S, 4, 4, 2, 2])
        pair_hi, pair_lo = top[:, :, :, 0, :], top[:, :, :, 1, :]
        best = sb("best", [S, 2, 4, 4])
        group_score = sb("group_score", [S, 4, 4])
        group_gt = sb("group_gt", [S, 4, 4, 4])
        group_eq = sb("group_eq", [S, 4, 4, 4])
        group_rank = sb("group_rank", [S, 4, 4])
        masked = sb("masked", [S, 4, 4, 4])
        scores_space = pos_score[:, :, :, :].rearrange("s a h k -> s (a h k)")
        expert_gt = scores_space[:, 0:1024].rearrange("s (k e f) -> s k e f", k=4, e=EX)
        expert_eq = scores_space[:, 1024:2048].rearrange("s (k e f) -> s k e f", k=4, e=EX)
        expert_rank = sb("expert_rank", [S, 4, EX])
        chosen = sb("chosen", [S, 4, EX])
        total = sb("total", [S, 4])
        combine = sb("combine", [S, 4, EX])
        parts3 = sb("parts3", [S, 4, 3, EX], BF16)
        combineT = sb("combineT", [3 * EX, 2, 4, S], BF16)
        rows_space = pos_rows[:, :, :, :].rearrange("s a h k -> s (a h k)")
        silu = rows_space[:, 0:1024].rearrange("m (a t) -> m a t", a=2)
        hidden_a = rows_space[:, 1024:2048].rearrange("m (a t) -> m a t", a=2)
        gated = rows_space[:, 2048:2560]
        ld = Phase()
        [ld.x, ld.w, ld.c, ld.b, ld.g, ld.d, ld.e, ld.f] = sems("ld", "x w c b g d e f")
        k0 = Phase()
        [k0.zero, k0.ones, k0.half, k0.kvzero, k0.wqx, k0.cast, k0.qnws, k0.qkw, k0.fold, k0.carry] = sems("k0", "zero ones half kvzero wqx cast qnws qkw fold carry")
        A = Phase()
        [A.proj, A.sq, A.ms, A.mse, A.rr, A.qn, A.qtop, A.kn1, A.kn2, A.kn, A.ktop, A.split, A.vst, A.v,
         A.qT_ps, A.qT, A.kT_ps, A.kT, A.s, A.mx, A.p, A.pT_ps, A.pT, A.o, A.oT, A.oT_ps, A.rec, A.on, A.x] = sems("a", "proj sq ms mse rr qn qtop kn1 kn2 kn ktop split vst v qT_ps qT kT_ps kT s mx p pT_ps pT o "
            "oT oT_ps rec on x")
        norm = sems("norm", "stats aggr var rstd xn xnT_ps xnT")

        def share_norm(q, base):
            q.base = base
            q.stats, q.aggr, q.var, q.rstd, q.xn, q.xnT_ps, q.xnT = norm

        share_norm(A, 0)
        A.summed, A.mixed, A.out_free, A.attn_free = A.s, A.p, A.on, A.x
        A.scores, A.prob_bank, A.out_bank = quads[0:2], bank[2:4], bank[4]
        A.ln_bank, A.proj_bank, A.head_bank = bank[5], bank[6], bank[7]
        A.probs, A.shared_v, A.stacked = probs, None, True
        B = Phase()
        [B.proj, B.q, B.k, B.kv, B.ksum, B.split, B.ks, B.vT_ps, B.v, B.qT_ps, B.qT, B.s, B.mx, B.p, B.ab,
         B.pT_ps, B.pT, B.o, B.oT, B.oT_ps, B.rec, B.on, B.aT_ps, B.aT, B.y, B.x] = sems("b", "proj q k kv ksum split ks vT_ps v qT_ps qT s mx p ab pT_ps pT o oT oT_ps rec on aT_ps aT y "
            "x")
        share_norm(B, NB)
        B.summed, B.mixed, B.out_free, B.attn_free = B.s, B.ab, B.x, B.aT_ps
        B.scores = [psum[:, 2 * i:2 * i + 2, 0:2 * KEYS].rearrange("s b (h k) -> s b h k", h=2) for i in range(2)]
        B.prob_bank, B.out_bank, B.ln_bank, B.head_bank = bank[4:6], bank[6], bank[7], bank[7]
        B.probs, B.shared_v, B.stacked = probs, v8, True
        C = Phase()
        [C.g, C.f, C.c, C.keep, C.fresh, C.cell, C.zero_cell, C.scaled, C.z, C.h, C.hT_ps, C.x] = sems("c", "g f c keep fresh cell zero_cell scaled z h hT_ps x")
        share_norm(C, 2 * NB)
        C.ln_bank = bank[2]
        C.gate_bank = bank[0:2]
        C.h_bank, C.hT_bank = bank[4:6], bank[6:8]
        P = Phase()
        [P.proj, P.q2, P.q, P.k, P.split, P.vst, P.v, P.bias, P.q2T_ps, P.q2T, P.qT_ps, P.qT, P.kT_ps, P.kT,
         P.e, P.es, P.s, P.add, P.mx, P.p, P.pT_ps, P.pT, P.o, P.oT, P.oT_ps, P.rec, P.on, P.aT_ps, P.aT,
         P.y, P.x, P.bqs, P.zeroed, P.pos, P.skewed, P.placed] = sems("d", "proj q2 q k split vst v bias q2T_ps q2T qT_ps qT kT_ps kT e es s add mx p pT_ps pT o oT "
            "oT_ps rec on aT_ps aT y x bqs zeroed pos skewed placed")
        share_norm(P, 3 * NB)

        def splits(n, which=0):
            return SPLIT_STEPS * (3 * n + which + 1)

        P.summed, P.mixed, P.out_free, P.attn_free = P.add, P.p, P.x, P.aT_ps
        P.score_bank = quads[0:2]
        P.scores = [summed[:, i, :, :] for i in range(2)]
        P.prob_bank, P.out_bank, P.ln_bank, P.pos_bank, P.head_bank = bank[2:4], bank[4], bank[5], bank[6], bank[7]
        P.probs, P.shared_v, P.stacked = probs, None, True
        E = Phase()
        [E.by_pool, E.by_dve, E.by_act, E.mm, E.ev, E.st, E.turned, E.x] = sems("e", "by_pool by_dve by_act mm ev st turned x")
        share_norm(E, 4 * NB)
        E.ln_bank = bank[5]
        E.y_bank, E.turn_bank = bank[0:2], bank[2:4]

        def ln_group_stats(dve, q, g, prev):
            prev = prev + q.base
            wait(dve, q.aggr, prev)
            for k in range(4):
                last = dve.bn_stats(stats4[:, k, :], X[:, at(4 * g + k), :])
            last.then_inc(q.stats, 1)
            wait(dve, q.stats, prev + 1)
            wait(dve, q.xn, prev)
            wait(dve, q.var, prev)
            dve.memset(carrier[0:1, :], 0.0)
            for k in range(4):
                last = dve.bn_aggr(meanvar4[:, k, :], stats4[:, k, :])
            last.then_inc(q.aggr, 1)
            wait(dve, q.aggr, prev + 1)
            wait(dve, q.rstd, prev)
            dve.tensor_scalar(vareps4[:, :].unsqueeze(2), meanvar4[:, :, 1:2], LN_EPS, None, ALU.add).then_inc(q.var, 1)

        def ln_group_rstd(pool, q, n):
            wait(pool, q.var, q.base + n + 1)
            wait(pool, q.xn, q.base + n)
            pool.tensor_tensor(out=rstd4[:, :], in0=vareps4[:, :], in1=minus_half[:, 0:4], op=ALU.pow).then_inc(q.rstd, 1)

        def ln_group_apply(dve, q, g, n):
            wait(dve, q.rstd, q.base + n + 1)
            wait(dve, q.xnT_ps, q.base + n)
            for k in range(4):
                last = dve.tensor_scalar(xn4[:, k:k + 1, :], X[:, at(4 * g + k), :], meanvar4[:, k, 0:1], rstd4[:, k:k + 1],
                                         ALU.subtract, ALU.mult)
            last.then_inc(q.xn, 1)

        GATHER_POOL, GATHER_DVE, GATHER_ACT = (0, 4), (4, 6), (10, 6)

        def gather_weights(eng, copy, pair, k, share, sem):
            if not isinstance(pair, int) or pair > 0:
                eng.wait_ge(E.mm, 2 * pair + k - 1)
                eng.sem_inc(k0.carry, 1)
            with eng.Fori(0, share[1]) as j:
                layer = eng.value_load(itok[0:1, at(32 * pair + 16 * k + share[0] + j)], min_val=0, max_val=NB - 1)
                copy(gathered[:, k, at(share[0] + j), :], ctxT[:, at(layer), :]).then_inc(sem, 1)

        def turn_group(pe, q, n):
            wait(pe, q.xn, q.base + n + 1)
            wait(pe, q.xnT, q.base + n)
            for k in range(4):
                last = pe.transpose(q.ln_bank[:, k * S:(k + 1) * S], xn4[:, k, :], ident)
            last.then_inc(q.xnT_ps, 1)
        F = Phase()
        [F.cast, F.gate, F.scores, F.route, F.split, F.cT_ps, F.cT, F.h1, F.h3, F.silu, F.gated, F.a, F.y,
         F.x] = sems("f", "cast gate scores route split cT_ps cT h1 h3 silu gated a y x")
        share_norm(F, 4 * NB + NB // 4)
        F.h1_bank, F.h3_bank = bank[0:2], bank[2:4]
        F.combine_bank, F.y_bank, F.ln_bank, F.gate_bank = bank[4], bank[5], bank[6], bank[7]
        NG = NB // 4
        ROUTE_STEPS = 29
        done = Phase()
        [done.out] = sems("done", "out")
        block = ctx.enter_context(nc.Block())

        def ln_stats(dve, q, b, prev):
            prev = prev + q.base
            wait(dve, q.aggr, prev)
            dve.bn_stats(stats[:, :], X[:, at(b), :]).then_inc(q.stats, 1)
            wait(dve, q.stats, prev + 1)
            wait(dve, q.xn, prev)
            wait(dve, q.var, prev)
            dve.memset(carrier[0:1, :], 0.0)
            dve.bn_aggr(meanvar[:, :], stats[:, :]).then_inc(q.aggr, 1)
            wait(dve, q.aggr, prev + 1)
            wait(dve, q.rstd, prev)
            dve.tensor_scalar(vareps[:, :], meanvar[:, 1:2], LN_EPS, None, ALU.add).then_inc(q.var, 1)

        def turn_xn(pe, q, n, free, free_count):
            wait(pe, q.xn, q.base + n + 1)
            wait(pe, free, free_count)
            pe.transpose(q.ln_bank[:, 0:S], xn[:, 0, :], ident).then_inc(q.xnT_ps, 1)

        def save_xnT(act, q, n, dst, free, free_count):
            wait(act, q.xnT_ps, q.base + n + 1)
            wait(act, free, free_count)
            act.activation(dst, q.ln_bank[:, 0:S], ACT.Copy).then_inc(q.xnT, 1)

        def split_heads(pool, which, slots, sem, count, begin):
            src, stack = staged[:, which, :, :], stacks[:, which, :, :].rearrange("s h (t d) -> s h t d", d=HD)

            def part(i):
                first, n, step = slots[i]
                return stack[:, :, first:first + (n - 1) * step + 1:step, :]

            def spread_out(ap, i):
                return ap.unsqueeze(2).broadcast_to([S, H, slots[i][1], HD])

            begin()
            pool.sem_inc(k0.carry, 1)
            pool.tensor_copy(part(0), spread_out(src, 0)).then_inc(sem, 1)
            wait(pool, sem, count + 1)
            pool.tensor_tensor(out=rest[:, :, :], in0=src, in1=part(0)[:, :, 0, :], op=ALU.subtract).then_inc(sem, 1)
            wait(pool, sem, count + 2)
            pool.sem_inc(k0.carry, 1)
            pool.tensor_copy(part(1), spread_out(rest[:, :, :], 1)).then_inc(sem, 1)
            wait(pool, sem, count + 3)
            pool.tensor_tensor(out=part(2)[:, :, 0, :], in0=rest[:, :, :], in1=part(1)[:, :, 0, :], op=ALU.subtract).then_inc(sem, 1)

        def part_slots(which, slots, i):
            first, n, step = slots[i]
            return stacks[:, which, :, :].rearrange("s h (t d) -> s h t d", d=HD)[:, :, first:first + (n - 1) * step + 1:step, :]

        def first_part(act, which, slots, src, sem):
            n = slots[0][1]
            act.activation(part_slots(which, slots, 0), src.unsqueeze(2).broadcast_to([S, H, n, HD]), ACT.Copy).then_inc(sem, 1)

        def other_parts(dve, which, slots, sem, count):
            wait(dve, sem, count)
            dve.tensor_tensor(rest[:, :, :], staged[:, which, :, :], part_slots(which, slots, 0)[:, :, 0, :], ALU.subtract).then_inc(sem, 1)
            wait(dve, sem, count + 1)
            n = slots[1][1]
            dve.tensor_copy(part_slots(which, slots, 1), rest[:, :, :].unsqueeze(2).broadcast_to([S, H, n, HD])).then_inc(sem, 1)
            wait(dve, sem, count + 2)
            dve.tensor_tensor(part_slots(which, slots, 2)[:, :, 0, :], rest[:, :, :], part_slots(which, slots, 1)[:, :, 0, :],
                              ALU.subtract).then_inc(sem, 1)

        def turn_stack(pe, q, which, sem):
            turned = q.head_bank.bitcast(BF16).rearrange("k (t s) -> k t s", s=S)
            for t in range(H // 2):
                last = pe.transpose(turned[:, t, :], stacks[:, which, 2 * t:2 * t + 2, :].rearrange("s h k -> s (h k)"), identb[:, :])
            last.then_inc(sem, 1)

        def save_stack(act, q, ps, sem, dst, n, free=None, free_count=0):
            wait(act, ps, n + 1)
            if free is not None:
                wait(act, free, free_count)
            act.activation(dst.rearrange("k t s -> k (t s)"), q.head_bank.bitcast(BF16), ACT.Copy).then_inc(sem, 1)

        def head(r, p):
            return 8 * (r // 2) + 2 * p + r % 2

        def rows_of(turned, r, p):
            half = (r % 2) * STACK
            return turned[half:half + USED, head(r, p) // 2, :]

        def turn_attn(pe, q, n):
            wait(pe, q.on, n + 1)
            wait(pe, q.aT, n)
            pe.transpose(q.out_bank[:, 144:144 + S], attn[:, 0, :, :].rearrange("s h d -> s (h d)"), ident).then_inc(q.aT_ps, 1)

        def save_attnT(act, q, n):
            wait(act, q.aT_ps, n + 1)
            wait(act, q.y, n)
            act.activation(attnT[:, :], q.out_bank[:, 144:144 + S], ACT.Copy).then_inc(q.aT, 1)

        def output(pe, q, n, weights):
            wait(pe, q.aT, n + 1)
            pe.matmul(q.out_bank[:, 272:272 + D], attnT[:, :], weights, start=True, stop=True).then_inc(q.y, 1)

        def residual_y(dve, q, n):
            wait(dve, q.y, n + 1)
            dve.tensor_tensor(X[:, at(n), :], X[:, at(n), :], q.out_bank[:, 272:272 + D].unsqueeze(1), ALU.add)\
               .then_inc(q.x, 1)

        def ln_rstd(pool, q, n):
            wait(pool, q.var, q.base + n + 1)
            wait(pool, q.xn, q.base + n)
            pool.tensor_tensor(out=rstd[:, :], in0=vareps[:, :], in1=minus_half[:, 0:1], op=ALU.pow).then_inc(q.rstd, 1)

        def ln_apply(dve, q, b, n):
            wait(dve, q.rstd, q.base + n + 1)
            wait(dve, q.xnT_ps, q.base + n)
            dve.tensor_scalar(xn[:, :, :], X[:, at(b), :], meanvar[:, 0:1], rstd[:, 0:1],
                              ALU.subtract, ALU.mult).then_inc(q.xn, 1)

        def row_max(dve, q, n, r):
            wait(dve, q.summed, n * R + r + 1)
            wait(dve, q.p, n * R + r - 1)
            scores = q.scores[r % 2]
            shape = [S, 2, 2] if len(scores.shape) == 4 else [S, PT]
            out = negmax[:, r % 2, :]
            if len(shape) == 3:
                out = out.rearrange("s (b h) -> s b h", b=2)
            dve.tensor_reduce(out, scores, AX.X, ALU.max, negate=True).then_inc(q.mx, 1)

        def exps(act, q, n, r):
            wait(act, q.mx, n * R + r + 1)
            wait(act, q.pT_ps, n * R + r - 1)
            for p in range(PT):
                last = act.activation(probs[:, r % 2, p, :], q.scores[r % 2][:, p, :], ACT.Exp,
                                      bias=negmax[:, r % 2, p:p + 1], scale=1.0)
            last.then_inc(q.p, 1)

        def turn_probs(pe, q, n, r):
            wait(pe, q.mixed, n * R + r + 1)
            wait(pe, q.pT, n * R + r - 1)
            for p in range(PT):
                last = pe.transpose(q.prob_bank[r % 2][:, p * S:(p + 1) * S], q.probs[:, r % 2, p, :], ident)
            last.then_inc(q.pT_ps, 1)

        def save_probsT(dve, q, n, r):
            wait(dve, q.pT_ps, n * R + r + 1)
            wait(dve, q.o, n * R + r - 1)
            dve.tensor_copy(probsT[:, r % 2, :, :].rearrange("s p k -> s (p k)"), q.prob_bank[r % 2]).then_inc(q.pT, 1)

        def weigh_values(pe, q, n, par, r):
            wait(pe, q.pT, n * R + r + 1)
            if r == 0:
                wait(pe, q.v, n + 1)
                wait(pe, q.out_free, n)
            for p in range(PT):
                v = values[:, par, head(r, p) if q.stacked else r * PT + p, :] if q.shared_v is None else q.shared_v[:, par, :]
                last = pe.matmul(q.out_bank[p * GW:(p + 1) * GW, r * S:(r + 1) * S], v, probsT[:, r % 2, p, :],
                                 start=True, stop=True)
            last.then_inc(q.o, 1)

        def save_outT(act, q, n):
            wait(act, q.o, (n + 1) * R)
            wait(act, q.oT_ps, n)
            act.activation(outT[:, :, :].rearrange("k r s -> k (r s)"), q.out_bank, ACT.Copy).then_inc(q.oT, 1)

        def turn_out(pe, q, n):
            wait(pe, q.oT, n + 1)
            for r in range(R):
                last = pe.transpose(q.out_bank[:, r * S:(r + 1) * S], outT[:, r, :], ident)
            last.then_inc(q.oT_ps, 1)

        def normalise(dve, q, n, denominators=None):
            turned = q.out_bank.rearrange("s (h k) -> s h k", h=H)
            wait(dve, q.oT_ps, n + 1)
            wait(dve, q.on, n)
            dve.reciprocal(recip[:, :].unsqueeze(2), turned[:, :, HD:HD + 1] if denominators is None else denominators)\
               .then_inc(q.rec, 1)
            wait(dve, q.rec, n + 1)
            wait(dve, q.attn_free, n)
            if q.stacked:
                for half in range(2):
                    last = dve.tensor_tensor(
                        attn[:, 0, :, :].rearrange("s (j p half) d -> s half j p d", j=2, half=2)[:, half],
                        turned[:, :, 0:HD].rearrange("s (j half p) d -> s half j p d", j=2, half=2)[:, half],
                        recip[:, :].rearrange("s (j half p) -> s half j p", j=2, half=2)[:, half].unsqueeze(3).broadcast_to([S, 2, PT, HD]),
                        ALU.mult)
                last.then_inc(q.on, 1)
                return
            dve.tensor_tensor(attn[:, 0, :, :], turned[:, :, 0:HD], recip[:, :].unsqueeze(2).broadcast_to([S, H, HD]),
                              ALU.mult).then_inc(q.on, 1)

        LOADS = 9 * 16
        LOADS_B = 4 * 16
        LOADS_C = 13 * 16
        LOADS_D = 12 * 16
        LOADS_F = 9 * 16

        @block.sync
        def _(sp):
            sp.dma_start(consts[:, :], t["consts"]).then_inc(ld.c, 16)
            for dst, src in [(w_dq, t["L0_attn_W_DQ"]), (w_uqT, t["L0_attn_W_UQ"]),
                             (w_dkv, t["L0_attn_W_DKV"]), (w_ukvT, t["L0_attn_W_UKV"]),
                             (w_qr, t["L0_attn_W_QR"]), (w_kr, t["L0_attn_W_KR"]),
                             (w_oT, t["L0_attn_W_O"]),
                             (qnw, t["L0_attn_q_norm_w"].partition_broadcast(128)),
                             (knw, t["L0_attn_k_norm_w"].partition_broadcast(128))]:
                sp.dma_start(dst[:, :], src).then_inc(ld.w, 16)
            for dst, src in [(w_qx[:, :], t["L0_xattn_Wq"]), (w_cx[:, :], t["L0_xattn_Wc"])]:
                sp.dma_start(dst, src).then_inc(ld.b, 16)
            sp.dma_start(w_kv[:, :], t["L0_xattn_Wkv"]).then_inc(ld.b, 16)
            sp.dma_start(ctxT[:, :, :], t["ctx_1024"]).then_inc(ld.b, 16)
            for i, name in enumerate(["wf", "wi", "wc", "wo"]):
                sp.dma_start(wx[:, i, :], t["L0_ffn_" + name]).then_inc(ld.g, 16)
            for i, name in enumerate(["uf", "ui", "uc", "uo"]):
                sp.dma_start(uc[:, i, :], t["L0_ffn_" + name]).then_inc(ld.g, 16)
            for i, name in enumerate(["bf", "bi", "bc", "bo"]):
                sp.dma_start(gate_bias[:, i:i + 1], t["L0_ffn_" + name].rearrange("(m a) -> m a", a=1)).then_inc(ld.g, 16)
            sp.dma_start(cell0[:, :], t["L0_ffn_in_c"].rearrange("(m a) -> m a", a=1)).then_inc(ld.g, 16)
            for i, name in enumerate(["Wq", "Wk", "Wv"]):
                sp.dma_start(wqkv[:, i, :], t["L1_attn_" + name]).then_inc(ld.d, 16)
            sp.dma_start(w_p[:, :], t["L1_attn_Wp"]).then_inc(ld.d, 16)
            sp.dma_start(w_o1[:, :], t["L1_attn_Wo"]).then_inc(ld.d, 16)
            for i, name in enumerate(["bq", "u", "v", "bk", "bv", "bp", "bo"]):
                row = t["L1_attn_" + name]
                if len(row.shape) > 1:
                    row = row.rearrange("a h b p -> (a h b p)")
                sp.dma_start(bias_rows[:, i, :], row.partition_broadcast(S)).then_inc(ld.d, 16)

            def shift_positions(n, par):
                wait(sp, P.es, (n + 1) * R)
                sp.sem_inc(k0.carry, 1)
                wait(sp, P.placed, 16 * (n - 1))
                sp.sem_inc(k0.carry, 1)
                sp.dma_start(skew[par].rearrange("h (i c) -> i h c", i=S), pos_rows[:, par, :, :]).then_inc(P.skewed, 16)
                wait(sp, P.skewed, 16 * (n + 1))
                sp.sem_inc(k0.carry, 1)
                wait(sp, P.add, (n - 1) * R)
                sp.sem_inc(k0.carry, 1)
                sp.dma_start(pos_score[:, par, :, :], skew[par][:, S:S * (S + 1)].rearrange("h (i j) -> i h j", i=S))\
                  .then_inc(P.placed, 16)

            shift_positions(0, 0)
            shift_positions(1, 1)
            with sp.Fori(1, NB // 2) as pair:
                shift_positions(2 * pair, 0)
                shift_positions(2 * pair + 1, 1)
            sp.dma_start(itok[0:1, :], t["itok_S_0_31"].rearrange("(a s) -> a s", a=1)).then_inc(ld.e, 16)
            sp.dma_start(w_gate[:, :], t["L1_ffn_w_gate"]).then_inc(ld.f, 16)
            for dst, name in [(w_up1, "w1"), (w_up3, "w3")]:
                sp.dma_start(dst[:, 0:TILES - 1, :].rearrange("h t m -> h (t m)"),
                             t[f"L1_ffn_{name}_e"].rearrange("h e f -> h (e f)")).then_inc(ld.f, 16)
                sp.dma_start(dst[:, TILES - 1, :], t[f"L1_ffn_{name}_s"]).then_inc(ld.f, 16)
            pairs = t["L1_ffn_w2_e"].rearrange("f (t p) h -> p f t h", p=2)
            for p in range(2):
                sp.dma_start(w_down[p * FW:(p + 1) * FW, 0:TILES - 1, :], pairs[p]).then_inc(ld.f, 16)
            sp.dma_start(w_down[:, TILES - 1, :], t["L1_ffn_w2_s"]).then_inc(ld.f, 16)
            sp.dma_start(spread[:, :, :], t["spread"].rearrange("k (t m) -> k t m", t=TILES - 1)).then_inc(ld.f, 16)
            for g in range(NG):
                sp.wait_ge(F.x, g + 1)
                sp.dma_start(out[4 * g:4 * g + 4].rearrange("b s d -> s b d"), X[:, 4 * g:4 * g + 4, :]).then_inc(done.out, 16)
            sp.wait_ge(done.out, 16 * NG)


        @block.gpsimd
        def _(pool):
            pool.dma_start(X[:, :, :], t["x"].rearrange("b s d -> s b d")).then_inc(ld.x, 16)
            pool.memset(stacks[:, :, :, :], 0.0).then_inc(k0.zero, 1)
            pool.memset(values[:, :, :, :], 0.0).then_inc(k0.ones, 1)
            pool.wait_ge(k0.ones, 1)
            pool.memset(values[:, :, :, HD:HD + 1], 1.0).then_inc(k0.ones, 1)
            pool.memset(minus_half[:, :], -0.5).then_inc(k0.half, 1)
            pool.memset(w_kvx[:, :, :, :], 0.0).then_inc(k0.kvzero, 1)
            pool.memset(v8[:, :, :], 0.0).then_inc(k0.kvzero, 1)
            pool.memset(pos_rows[:, :, :, 0:1], 0.0).then_inc(P.zeroed, 1)
            pool.wait_ge(k0.half, 1)

            def rms_rsqrt(n):
                wait(pool, A.mse, n + 1)
                wait(pool, A.kn1, n)
                for i in range(2):
                    pool.tensor_tensor(out=rr[:, i * H:(i + 1) * H], in0=ms_eps[:, i * H:(i + 1) * H],
                                       in1=minus_half[:, 0:H], op=ALU.pow).then_inc(A.rr, 1)

            def residual(n):
                wait(pool, A.on, n + 1)
                pool.tensor_tensor(out=X[:, at(n), :], in0=X[:, at(n), :],
                                   in1=attn[:, :, :, :].rearrange("s a h d -> s a (h d)"), op=ALU.add).then_inc(A.x, 1)

            def place_v(n, par):
                wait(pool, A.vst, n + 1)
                wait(pool, A.o, (n - 1) * R)
                pool.sem_inc(k0.carry, 1)
                pool.tensor_copy(values[:, par, :, 0:HD], v_stage[:, par, :, :]).then_inc(A.v, 1)

            def body(b, par, left):
                if left >= 3:
                    ln_rstd(pool, A, b + 3)
                if left >= 1:
                    place_v(b + 1, 1 - par)
                if left >= 2:
                    rms_rsqrt(b + 2)
                if not isinstance(b, int) or b > 0:
                    residual(b - 1)

            pool.wait_ge(k0.ones, 2)
            for n in range(3):
                ln_rstd(pool, A, n)
                if n < 2:
                    rms_rsqrt(n)
                if n == 0:
                    place_v(0, 0)
            body_pairs(pool, body, tail=2)
            residual(NB - 1)

            def cross_attention():
                def key_sum(n, par):
                    wait(pool, B.k, 2 * (n + 1))
                    pool.tensor_tensor(out=k3T[:, par, 64:128], in0=k3T[:, par, 0:64], in1=k3T[:, par, 128:192],
                                       op=ALU.add).then_inc(B.ksum, 1)

                def mix(n, r):
                    wait(pool, B.p, n * R + r + 1)
                    wait(pool, B.pT_ps, n * R + r - 1)
                    pool.tensor_tensor(out=probs[:, r % 2, :, :], in0=probs3[:, r % 2, :, 0:128],
                                       in1=probs3[:, r % 2, :, 64:192], op=ALU.add).then_inc(B.ab, 1)

                def body(b, par, left):
                    mix(b, 0)
                    mix(b, 1)
                    mix(b, 2)
                    if left >= 2:
                        ln_rstd(pool, B, b + 2)
                    mix(b, 3)
                    if left >= 2:
                        key_sum(b + 2, par)

                pool.wait_ge(A.x, NB)
                ln_rstd(pool, B, 0)
                key_sum(0, 0)
                ln_rstd(pool, B, 1)
                key_sum(1, 1)
                body_pairs(pool, body)

            cross_attention()

            def recurrence():
                pool.wait_ge(B.x, NB)
                ln_rstd(pool, C, 0)
                with pool.Fori(0, NB - 1) as s:
                    ln_rstd(pool, C, s + 1)

            recurrence()

            def relative_attention():
                def place_v(n, par):
                    wait(pool, P.vst, n + 1)
                    wait(pool, P.o, (n - 1) * R)
                    pool.tensor_tensor(out=values[:, par, :, 0:HD], in0=v_stage[:, par, :, :],
                                       in1=bias_rows[:, 4, :].rearrange("s (h d) -> s h d", h=H), op=ALU.add).then_inc(P.v, 1)

                def output_bias(n):
                    wait(pool, P.xn, P.base + n + 1)
                    pool.tensor_tensor(out=X[:, at(n), :], in0=X[:, at(n), :], in1=bias_rows[:, 6:7, :], op=ALU.add)\
                        .then_inc(P.bias, 1)

                def split(n, which):
                    def begin():
                        wait(pool, [P.q2, P.q, P.k][which], n + 1)
                        wait(pool, [P.q2T_ps, P.qT_ps, P.kT_ps][which], n)
                    split_heads(pool, which, RIGHT_SLOTS if which == K else LEFT_SLOTS, P.split, splits(n, which), begin)

                def split_positions():
                    def begin():
                        wait(pool, P.pos, 2)
                    split_heads(pool, K, RIGHT_SLOTS, P.split, 0, begin)

                def body(b, par, left):
                    if left >= 1:
                        place_v(b + 1, 1 - par)
                    if left >= 3:
                        split(b + 3, Q2)
                        split(b + 3, Q)
                    if left >= 4:
                        ln_rstd(pool, P, b + 4)
                    if left >= 3:
                        split(b + 3, K)
                    if left >= 4:
                        output_bias(b + 4)

                pool.wait_ge(C.x, NB // 4)
                pool.wait_ge(ld.d, LOADS_D)
                pool.wait_ge(P.zeroed, 1)
                split_positions()
                pool.wait_ge(P.pos, 3)
                for n in range(4):
                    ln_rstd(pool, P, n)
                    output_bias(n)
                    if n < 3:
                        for which in (Q2, Q, K):
                            split(n, which)
                    if n == 0:
                        place_v(0, 0)
                body_pairs(pool, body, tail=2)

            relative_attention()

            def position_weights():
                def gather(pair, k):
                    gather_weights(pool, pool.tensor_copy, pair, k, GATHER_POOL, E.by_pool)

                pool.wait_ge(P.x, NB)
                pool.wait_ge(ld.e, 16)
                ln_group_rstd(pool, E, 0)
                gather(0, 0)
                with pool.Fori(1, NB // 4) as g:
                    ln_group_rstd(pool, E, g)
                gather(0, 1)
                with pool.Fori(1, 4) as pair:
                    gather(pair, 0)
                    gather(pair, 1)

            position_weights()

            def experts():
                pool.wait_ge(E.x, NG)
                ln_group_rstd(pool, F, 0)
                with pool.Fori(1, NG) as g:
                    ln_group_rstd(pool, F, g)

            experts()

        @block.vector
        def _(dve):
            dve.wait_ge(ld.c, 16)
            dve.wait_ge(ld.w, LOADS)
            dve.tensor_copy(identb[:, :], ident).then_inc(k0.cast, 1)
            dve.tensor_copy(causal4[:, :, :], consts[:, C_CAUSAL:C_CAUSAL + S].unsqueeze(1).broadcast_to([S, PT, S])).then_inc(k0.cast, 1)
            dve.tensor_scalar(qnws[:, :], qnw[:, :], SCALE, None, ALU.mult).then_inc(k0.qnws, 1)
            dve.wait_ge(k0.qnws, 1)
            dve.tensor_tensor(qkw[:, 0, :], qnws[:, :], knw[:, :], ALU.mult).then_inc(k0.qkw, 1)
            dve.wait_ge(k0.fold, 1)
            dve.tensor_copy(avT[:, :], bank[0][0:HD, 0:HD]).then_inc(k0.fold, 1)
            dve.wait_ge(k0.fold, 3)
            dve.tensor_copy(small[:, 0:2, :], bank[1][0:HD, 0:2 * HD].rearrange("e (w d) -> e w d", w=2)).then_inc(k0.fold, 1)
            dve.tensor_tensor(small[:, 2, :], bank[1][0:HD, 2 * HD:3 * HD], qnws[0:HD, :], ALU.mult).then_inc(k0.fold, 1)
            dve.tensor_copy(small[:, 3, :], bank[1][0:HD, 3 * HD:4 * HD]).then_inc(k0.fold, 1)
            dve.wait_ge(k0.fold, 7)
            hmask = consts[:, C_HEAD:C_HEAD + H].unsqueeze(2).broadcast_to([128, H, HD])
            for w in range(4):
                dve.tensor_tensor(wblk[:, w, :, :],
                                  bank[2][:, w * HD:(w + 1) * HD].unsqueeze(1).broadcast_to([128, H, HD]),
                                  hmask, ALU.mult).then_inc(k0.fold, 1)

            heads = A.proj_bank.rearrange("s (w h d) -> s w h d", w=4, h=H)

            def rms_sum(n):
                wait(dve, A.sq, n + 1)
                wait(dve, A.mse, n)
                dve.tensor_reduce(ms[:, :], squares[:, :, :], AX.X, ALU.add).then_inc(A.ms, 1)
                wait(dve, A.ms, n + 1)
                wait(dve, A.rr, 2 * n)
                dve.tensor_scalar(ms_eps[:, :], ms[:, :], 1.0 / HD, RMS_EPS, ALU.mult, ALU.add).then_inc(A.mse, 1)

            def query(n):
                wait(dve, A.rr, 2 * n + 1)
                wait(dve, A.vst, n + 1)
                wait(dve, A.qtop, n)
                dve.tensor_tensor(staged[:, QUERY, :, :], heads[:, 0, :, :],
                                  rr[:, 0:H].unsqueeze(2).broadcast_to([S, H, HD]), ALU.mult).then_inc(A.qn, 1)

            def query_parts(n):
                wait(dve, A.qtop, n + 1)
                other_parts(dve, QUERY, LEFT_SLOTS, A.split, 6 * n)

            def key_parts(n):
                wait(dve, A.ktop, n + 1)
                other_parts(dve, KEY, RIGHT_SLOTS, A.split, 6 * n + 3)

            def key_1(n):
                wait(dve, A.rr, 2 * n + 2)
                wait(dve, A.kn2, n)
                dve.tensor_tensor(kn1[:, :, :], heads[:, 1, :, :], rr[:, H:2 * H].unsqueeze(2).broadcast_to([S, H, HD]),
                                  ALU.mult).then_inc(A.kn1, 1)

            def key_2(n):
                wait(dve, A.kn1, n + 1)
                wait(dve, A.kn, n)
                dve.tensor_tensor(kn2[:, :, :], kn1[:, :, :], qkw[:, :, :].broadcast_to([S, H, HD]), ALU.mult).then_inc(A.kn2, 1)

            def key_3(n):
                wait(dve, A.kn2, n + 1)
                wait(dve, A.ktop, n)
                dve.tensor_tensor(staged[:, KEY, :, :], kn2[:, :, :], heads[:, 2, :, :], ALU.add).then_inc(A.kn, 1)

            def body(b, par, left):
                row_max(dve, A, b, 1)
                if left >= 3:
                    ln_stats(dve, A, b + 3, b + 3)
                save_probsT(dve, A, b, 0)
                if left >= 1:
                    key_parts(b + 1)
                if left >= 2:
                    rms_sum(b + 2)
                row_max(dve, A, b, 2)
                save_probsT(dve, A, b, 1)
                if not isinstance(b, int) or b > 0:
                    normalise(dve, A, b - 1)
                if left >= 3:
                    ln_apply(dve, A, b + 3, b + 3)
                row_max(dve, A, b, 3)
                if left >= 2:
                    query(b + 2)
                save_probsT(dve, A, b, 2)
                if left >= 2:
                    query_parts(b + 2)
                if left >= 1:
                    row_max(dve, A, b + 1, 0)
                save_probsT(dve, A, b, 3)
                if left >= 2:
                    key_1(b + 2)
                    key_2(b + 2)
                    key_3(b + 2)

            dve.wait_ge(ld.x, 16)
            dve.wait_ge(k0.zero, 1)
            for n in range(3):
                ln_stats(dve, A, n, n)
                ln_apply(dve, A, n, n)
                if n < 2:
                    rms_sum(n)
                    query(n)
                    query_parts(n)
                    key_1(n)
                    key_2(n)
                    key_3(n)
                if n == 0:
                    key_parts(n)
            row_max(dve, A, 0, 0)
            body_pairs(dve, body, tail=2)
            normalise(dve, A, NB - 1)

            def cross_attention():
                def key_stack(n, par):
                    keys = k3T[:, par, :]
                    wait(dve, B.ksum, n + 1)
                    wait(dve, B.ks, 4 * n)
                    dve.tensor_copy(key_top[:, :], keys).then_inc(B.ks, 1)
                    wait(dve, B.ks, 4 * n + 1)
                    dve.scalar_tensor_tensor(out=key_rest[:, :], in0=key_top[:, :], scalar=consts[:, C_PARTS:C_PARTS + 1], in1=keys,
                                             op0=ALU.mult, op1=ALU.add).then_inc(B.ks, 1)
                    wait(dve, B.ks, 4 * n + 2)
                    dve.tensor_copy(key_top[:, :], key_rest[:, :]).then_inc(B.ks, 1)
                    wait(dve, B.ks, 4 * n + 3)
                    wait(dve, B.s, (n - 1) * R)
                    dve.scalar_tensor_tensor(out=kstack[:, par, :], in0=key_top[:, :], scalar=consts[:, C_PARTS + 1:C_PARTS + 2],
                                             in1=key_rest[:, :], op0=ALU.mult, op1=ALU.add).then_inc(B.ks, 1)

                def query_parts(n):
                    wait(dve, B.q, 2 * n + 2)
                    other_parts(dve, QUERY, LEFT_SLOTS, B.split, 3 * n)

                def body(b, par, left):
                    row_max(dve, B, b, 1)
                    save_probsT(dve, B, b, 0)
                    if left >= 1:
                        query_parts(b + 1)
                    if not isinstance(b, int) or b > 0:
                        normalise(dve, B, b - 1, denom[:, 1 - par, :].unsqueeze(2))
                    row_max(dve, B, b, 2)
                    save_probsT(dve, B, b, 1)
                    if left >= 1:
                        key_stack(b + 1, 1 - par)
                    if not isinstance(b, int) or b > 0:
                        residual_y(dve, B, b - 1)
                    if left >= 2:
                        ln_stats(dve, B, b + 2, b + 2)
                    row_max(dve, B, b, 3)
                    save_probsT(dve, B, b, 2)
                    if left >= 2:
                        ln_apply(dve, B, b + 2, b + 2)
                    if left >= 1:
                        row_max(dve, B, b + 1, 0)
                    save_probsT(dve, B, b, 3)

                dve.wait_ge(ld.b, LOADS_B)
                dve.tensor_scalar(w_qx[:, :], w_qx[:, :], SCALE, None, ALU.mult).then_inc(k0.wqx, 1)
                dve.wait_ge(k0.kvzero, 1)
                for slots, cols in [(slice(0, USED // HD), w_kv[:, 0:HD]), (slice(USED // HD, USED // HD + 1), w_kv[:, HD:2 * HD])]:
                    n = slots.stop - slots.start
                    dve.tensor_copy(w_kvx[:, :, slots, :], cols.unsqueeze(1).unsqueeze(1).broadcast_to([D, 2, n, HD])).then_inc(k0.wqx, 1)
                dve.wait_ge(A.x, NB)
                ln_stats(dve, B, 0, 0)
                ln_apply(dve, B, 0, 0)
                query_parts(0)
                key_stack(0, 0)
                ln_stats(dve, B, 1, 1)
                ln_apply(dve, B, 1, 1)
                row_max(dve, B, 0, 0)
                body_pairs(dve, body)
                normalise(dve, B, NB - 1, denom[:, 1, :].unsqueeze(2))
                residual_y(dve, B, NB - 1)

            cross_attention()

            def recurrence():
                def cell(s):
                    wait(dve, C.f, s + 1)
                    dve.scalar_tensor_tensor(out=keep[:, :], in0=gates[:, 0, :], scalar=1.0, in1=cell2[:, :],
                                             op0=ALU.add, op1=ALU.mult).then_inc(C.keep, 1)
                    wait(dve, C.c, s + 1)
                    dve.scalar_tensor_tensor(out=fresh[:, :], in0=gates[:, 1, :], scalar=1.0, in1=gates[:, 2, :],
                                             op0=ALU.add, op1=ALU.mult).then_inc(C.fresh, 1)
                    wait(dve, C.fresh, s + 1)
                    dve.scalar_tensor_tensor(out=cell2[:, :], in0=keep[:, :], scalar=0.5, in1=fresh[:, :],
                                             op0=ALU.mult, op1=ALU.add).then_inc(C.cell, 1)

                dve.wait_ge(ld.g, LOADS_C)
                dve.tensor_scalar(uc[:, :, :], uc[:, :, :], 0.5, None, ALU.mult).then_inc(C.scaled, 1)
                dve.tensor_scalar(half_bias[:, :], gate_bias[:, 0:2], 0.5, None, ALU.mult).then_inc(C.scaled, 1)
                dve.memset(cell2[:, :], 0.0).then_inc(C.zero_cell, 1)
                dve.wait_ge(C.zero_cell, 1)
                dve.tensor_scalar(cell2[:, :], cell2[:, :], cell0[:, 0:1], None, ALU.add).then_inc(C.zero_cell, 1)
                dve.wait_ge(C.zero_cell, 2)
                dve.tensor_scalar(cell2[:, :], cell2[:, :], 2.0, None, ALU.mult).then_inc(C.cell, 1)
                ln_stats(dve, C, 0, 0)
                ln_apply(dve, C, 0, 0)
                dve.wait_ge(C.cell, 1)
                with dve.Fori(0, NB - 1) as s:
                    ln_stats(dve, C, s + 1, s + 1)
                    ln_apply(dve, C, s + 1, s + 1)
                    cell(s)
                cell(NB - 1)

                def residual_h(g, par):
                    wait(dve, C.hT_ps, g + 1)
                    dve.tensor_tensor(X[:, at(4 * g, 4), :], X[:, at(4 * g, 4), :],
                                      C.hT_bank[par].rearrange("s (b d) -> s b d", b=4), ALU.add).then_inc(C.x, 1)

                with dve.Fori(0, NB // 8) as pair:
                    residual_h(2 * pair, 0)
                    residual_h(2 * pair + 1, 1)

            recurrence()

            def relative_attention():
                proj = P.ln_bank[:, 128:512].rearrange("s (w h d) -> s w h d", w=3, h=H)

                def rows(i):
                    return bias_rows[:, i, :].rearrange("s (h d) -> s h d", h=H)

                def stage_query(n, which):
                    if which == Q2:
                        wait(dve, P.proj, n + 1)
                    wait(dve, P.split, splits(n - 1, which + 1))
                    dve.tensor_tensor(staged[:, which, :, :], proj[:, 0, :, :],
                                      bias_q[:, 1 - which, :].rearrange("s (h d) -> s h d", h=H), ALU.add)\
                       .then_inc(P.q2 if which == Q2 else P.q, 1)

                def stage_key_value(n, par):
                    wait(dve, P.split, splits(n, 0))
                    dve.tensor_tensor(staged[:, K, :, :], proj[:, 1, :, :], rows(3), ALU.add).then_inc(P.k, 1)
                    wait(dve, P.v, n - 1)
                    dve.tensor_copy(v_stage[:, par, :, :], proj[:, 2, :, :]).then_inc(P.vst, 1)

                def add_max(n, par, r):
                    wait(dve, P.s, n * R + r + 1)
                    if r == 0:
                        wait(dve, P.placed, 16 * (n + 1))
                    wait(dve, P.p, n * R + r - 1)
                    dve.tensor_tensor(summed[:, r % 2, :, :], P.score_bank[r % 2],
                                      pos_score[:, par, r * PT:(r + 1) * PT, :], ALU.add).then_inc(P.add, 1)
                    row_max(dve, P, n, r)

                def body(b, par, left):
                    add_max(b, par, 1)
                    save_probsT(dve, P, b, 0)
                    if left >= 3:
                        stage_query(b + 3, Q2)
                        stage_query(b + 3, Q)
                    add_max(b, par, 2)
                    save_probsT(dve, P, b, 1)
                    if not isinstance(b, int) or b > 0:
                        normalise(dve, P, b - 1)
                    if left >= 3:
                        stage_key_value(b + 3, 1 - par)
                    add_max(b, par, 3)
                    if left >= 4:
                        ln_stats(dve, P, b + 4, b + 4)
                    if not isinstance(b, int) or b > 0:
                        residual_y(dve, P, b - 1)
                    save_probsT(dve, P, b, 2)
                    if left >= 4:
                        ln_apply(dve, P, b + 4, b + 4)
                    if left >= 1:
                        add_max(b + 1, 1 - par, 0)
                    save_probsT(dve, P, b, 3)

                dve.wait_ge(ld.d, LOADS_D)
                dve.tensor_scalar(wqkv[:, 0, :], wqkv[:, 0, :], SCALE, None, ALU.mult).then_inc(P.bqs, 1)
                dve.tensor_tensor(bias_q[:, :, :], bias_rows[:, 0:1, :].broadcast_to([S, 2, D]), bias_rows[:, 1:3, :],
                                  ALU.add).then_inc(P.bqs, 1)
                dve.wait_ge(P.bqs, 2)
                dve.tensor_scalar(bias_q[:, :, :], bias_q[:, :, :], SCALE, None, ALU.mult).then_inc(P.bqs, 1)
                dve.wait_ge(P.bqs, 3)
                dve.wait_ge(C.x, NB // 4)
                dve.wait_ge(P.pos, 1)
                dve.tensor_tensor(staged[:, K, :, :], P.pos_bank[:, 0:D].rearrange("s (h d) -> s h d", h=H), rows(5),
                                  ALU.add).then_inc(P.pos, 1)
                dve.wait_ge(P.pos, 3)
                for n in range(3):
                    ln_stats(dve, P, n, n)
                    ln_apply(dve, P, n, n)
                    stage_query(n, Q2)
                    stage_query(n, Q)
                    stage_key_value(n, n % 2)
                ln_stats(dve, P, 3, 3)
                ln_apply(dve, P, 3, 3)
                add_max(0, 0, 0)
                body_pairs(dve, body, tail=2)
                normalise(dve, P, NB - 1)
                residual_y(dve, P, NB - 1)

            relative_attention()

            def position_weights():
                dve.wait_ge(ld.e, 16)
                dve.wait_ge(ld.f, LOADS_F)
                dve.tensor_copy(spreadb[:, :, :], spread[:, :, :]).then_inc(F.cast, 1)
                dve.wait_ge(P.x, NB)
                ln_group_stats(dve, E, 0, 0)
                ln_group_apply(dve, E, 0, 0)
                with dve.Fori(1, NB // 4) as g:
                    ln_group_stats(dve, E, g, g)
                    ln_group_apply(dve, E, g, g)

                def gather(pair, k):
                    gather_weights(dve, dve.tensor_copy, pair, k, GATHER_DVE, E.by_dve)

                gather(0, 0)
                gather(0, 1)
                with dve.Fori(1, 4) as pair:
                    gather(pair, 0)
                    gather(pair, 1)

                def residual_group(g, par):
                    wait(dve, E.turned, g + 1)
                    dve.tensor_tensor(X[:, at(4 * g, 4), :], X[:, at(4 * g, 4), :],
                                      E.turn_bank[par].rearrange("s (b d) -> s b d", b=4), ALU.add).then_inc(E.x, 1)

                with dve.Fori(0, NB // 8) as pair:
                    residual_group(2 * pair, 0)
                    residual_group(2 * pair + 1, 1)

            position_weights()

            def experts():
                def step(g, k, emit):
                    wait(dve, F.route, g * ROUTE_STEPS + k)
                    emit().then_inc(F.route, 1)

                def tt(out, a, b, op):
                    return lambda: dve.tensor_tensor(out, a, b, op)

                member = scores4[:, :, :].rearrange("s k (g i j) -> s (k g) i j", g=4, i=2)
                hi = pair_hi.rearrange("s k g i -> s (k g) i")
                lo = pair_lo.rearrange("s k g i -> s (k g) i")
                best1 = best[:, 0, :, :].rearrange("s k g -> s (k g)")
                best2 = best[:, 1, :, :].rearrange("s k g -> s (k g)")
                gscore = group_score[:, :, :]
                by_group = [S, 4, 4, 4]
                by_expert = [S, 4, EX, EX]
                lower_g = consts[:, C_TIE_G:C_TIE_G + 16].rearrange("s (a g h) -> s a g h", a=1, g=4).broadcast_to(by_group)
                lower_e = consts[:, C_TIE_E:C_TIE_E + EX * EX].rearrange("s (a e f) -> s a e f", a=1, e=EX)\
                    .broadcast_to(by_expert)
                allowed = group_rank[:, :, :].unsqueeze(3).broadcast_to(by_group)
                scores_g = scores4[:, :, :].rearrange("s k (g e) -> s k g e", g=4)
                flat = masked[:, :, :, :].rearrange("s k g e -> s k (g e)")
                part = [parts3[:, :, i, :] for i in range(3)]
                ROUTE = [
                    tt(hi, member[:, :, :, 0], member[:, :, :, 1], ALU.max),
                    tt(lo, member[:, :, :, 0], member[:, :, :, 1], ALU.min),
                    tt(best1, hi[:, :, 0], hi[:, :, 1], ALU.max),
                    tt(best2, hi[:, :, 0], hi[:, :, 1], ALU.min),
                    tt(hi[:, :, 0], lo[:, :, 0], lo[:, :, 1], ALU.max),
                    tt(best2, best2, hi[:, :, 0], ALU.max),
                    tt(gscore.rearrange("s k g -> s (k g)"), best1, best2, ALU.add),
                    tt(group_gt[:, :, :, :], gscore.unsqueeze(2).broadcast_to(by_group), gscore.unsqueeze(3).broadcast_to(by_group), ALU.is_gt),
                    tt(group_eq[:, :, :, :], gscore.unsqueeze(2).broadcast_to(by_group), gscore.unsqueeze(3).broadcast_to(by_group), ALU.is_equal),
                    tt(group_eq[:, :, :, :], group_eq[:, :, :, :], lower_g, ALU.mult),
                    tt(group_gt[:, :, :, :], group_gt[:, :, :, :], group_eq[:, :, :, :], ALU.add),
                    lambda: dve.tensor_reduce(group_rank[:, :, :], group_gt[:, :, :, :], AX.X, ALU.add),
                    lambda: dve.tensor_scalar(group_rank[:, :, :], group_rank[:, :, :], 2.0, None, ALU.is_lt),
                    tt(masked[:, :, :, :], scores_g, allowed, ALU.mult),
                    lambda: dve.scalar_tensor_tensor(out=masked[:, :, :, :], in0=allowed, scalar=-1.0, in1=masked[:, :, :, :],
                                                     op0=ALU.add, op1=ALU.add),
                    tt(expert_gt[:, :, :, :], flat.unsqueeze(2).broadcast_to(by_expert), flat.unsqueeze(3).broadcast_to(by_expert), ALU.is_gt),
                    tt(expert_eq[:, :, :, :], flat.unsqueeze(2).broadcast_to(by_expert), flat.unsqueeze(3).broadcast_to(by_expert), ALU.is_equal),
                    tt(expert_eq[:, :, :, :], expert_eq[:, :, :, :], lower_e, ALU.mult),
                    tt(expert_gt[:, :, :, :], expert_gt[:, :, :, :], expert_eq[:, :, :, :], ALU.add),
                    lambda: dve.tensor_reduce(expert_rank[:, :, :], expert_gt[:, :, :, :], AX.X, ALU.add),
                    lambda: dve.scalar_tensor_tensor(out=chosen[:, :, :], in0=expert_rank[:, :, :], scalar=4.0, in1=scores4[:, :, :],
                                                     op0=ALU.is_lt, op1=ALU.mult),
                    lambda: dve.tensor_reduce(total[:, :], chosen[:, :, :], AX.X, ALU.add),
                    lambda: dve.tensor_scalar(total[:, :], total[:, :], 1e-6, None, ALU.add),
                    lambda: dve.reciprocal(total[:, :], total[:, :]),
                    tt(combine[:, :, :], chosen[:, :, :], total[:, :].unsqueeze(2).broadcast_to([S, 4, EX]), ALU.mult),
                    lambda: dve.tensor_copy(part[0], combine[:, :, :]),
                    tt(combine[:, :, :], combine[:, :, :], part[0], ALU.subtract),
                    lambda: dve.tensor_copy(part[1], combine[:, :, :]),
                    tt(combine[:, :, :], combine[:, :, :], part[1], ALU.subtract),
                ]
                assert len(ROUTE) == ROUTE_STEPS

                def route(g, first, last):
                    for k in range(first, min(last, ROUTE_STEPS)):
                        if k == 0:
                            wait(dve, F.scores, g + 1)
                        if k == ROUTE_STEPS - 4:
                            wait(dve, F.cT_ps, g)
                        step(g, k, ROUTE[k])
                    if first <= ROUTE_STEPS < last:
                        wait(dve, F.route, (g + 1) * ROUTE_STEPS)
                        dve.tensor_copy(part[2], combine[:, :, :]).then_inc(F.split, 1)

                def tile(g, gpar, k):
                    n, par = g * TILES + k, (gpar + k) % 2
                    routed = g * (TILES - 1) + min(k, TILES - 1)
                    wait(dve, F.silu, n + 1)
                    wait(dve, F.h3, n + 1)
                    if k < TILES - 1:
                        wait(dve, F.a, routed)
                        dve.tensor_tensor(gated[:, :], silu[:, par, :], F.h3_bank[par], ALU.mult).then_inc(F.gated, 1)
                        wait(dve, F.gated, n + 1)
                        wait(dve, F.y, n - 1)
                        dve.tensor_tensor(hidden_a[:, par, :], gated[:, :], F.combine_bank, ALU.mult).then_inc(F.a, 1)
                    else:
                        wait(dve, F.y, n - 1)
                        dve.tensor_tensor(hidden_a[:, par, :], silu[:, par, :], F.h3_bank[par], ALU.mult).then_inc(F.gated, 1)

                def residual_y4(g):
                    wait(dve, F.y, (g + 1) * TILES)
                    dve.tensor_tensor(X[:, at(4 * g, 4), :], X[:, at(4 * g, 4), :],
                                      F.y_bank.rearrange("s (b d) -> s b d", b=4), ALU.add).then_inc(F.x, 1)

                def body(g, par, left):
                    tile(g, par, 0)
                    if not isinstance(g, int) or g > 0:
                        residual_y4(g - 1)
                    for k in range(1, TILES):
                        tile(g, par, k)
                        if left >= 1 and k >= 2:
                            route(g + 1, 5 * (k - 2), 5 * (k - 1))
                        if left >= 2 and k == TILES - 2:
                            ln_group_stats(dve, F, g + 2, g + 2)
                    if left >= 2:
                        ln_group_apply(dve, F, g + 2, g + 2)

                dve.wait_ge(E.x, NG)
                ln_group_stats(dve, F, 0, 0)
                ln_group_apply(dve, F, 0, 0)
                ln_group_stats(dve, F, 1, 1)
                ln_group_apply(dve, F, 1, 1)
                route(0, 0, ROUTE_STEPS + 1)
                group_pairs(dve, body)
                residual_y4(NG - 1)

            experts()

        @block.scalar
        def _(act):
            def square_heads(n):
                wait(act, A.proj, n + 1)
                wait(act, A.ms, n)
                act.activation(squares[:, :, :].rearrange("s h d -> s (h d)"), A.proj_bank[:, 0:2 * D], ACT.Square).then_inc(A.sq, 1)

            def top_query(n):
                wait(act, A.qn, n + 1)
                wait(act, A.qT_ps, n)
                first_part(act, QUERY, LEFT_SLOTS, staged[:, QUERY, :, :], A.qtop)

            def top_key(n):
                wait(act, A.kn, n + 1)
                wait(act, A.kT_ps, n)
                first_part(act, KEY, RIGHT_SLOTS, staged[:, KEY, :, :], A.ktop)

            def save_values(n, par):
                wait(act, A.proj, n + 1)
                wait(act, A.v, n - 1)
                act.activation(v_stage[:, par, :, :], A.proj_bank[:, 3 * D:4 * D].rearrange("s (h d) -> s h d", h=H),
                               ACT.Copy).then_inc(A.vst, 1)

            def body(b, par, left):
                exps(act, A, b, 1)
                if left >= 1:
                    top_key(b + 1)
                if not isinstance(b, int) or b > 0:
                    save_outT(act, A, b - 1)
                if left >= 2:
                    square_heads(b + 2)
                    save_values(b + 2, par)
                exps(act, A, b, 2)
                if left >= 1:
                    save_stack(act, A, A.qT_ps, A.qT, qT[:, 1 - par, :, :], b + 1)
                if left >= 1:
                    save_stack(act, A, A.kT_ps, A.kT, kT[:, 1 - par, :, :], b + 1)
                exps(act, A, b, 3)
                if left >= 2:
                    top_query(b + 2)
                if left >= 1:
                    exps(act, A, b + 1, 0)
                if left >= 3:
                    save_xnT(act, A, b + 3, xnT[:, :], A.proj, b + 3)

            act.wait_ge(k0.zero, 1)
            for n in range(3):
                save_xnT(act, A, n, xnT[:, :], A.proj, n)
                if n < 2:
                    square_heads(n)
                    save_values(n, n)
                    top_query(n)
                if n == 0:
                    top_key(0)
                    save_stack(act, A, A.qT_ps, A.qT, qT[:, 0, :, :], 0)
                    save_stack(act, A, A.kT_ps, A.kT, kT[:, 0, :, :], 0)
            exps(act, A, 0, 0)
            body_pairs(act, body, tail=2)
            save_outT(act, A, NB - 1)

            def cross_attention():
                def save_q(n):
                    wait(act, B.proj, n + 1)
                    wait(act, B.split, 3 * n)
                    queries = B.ln_bank[:, 128:256].rearrange("s (h d) -> s h d", h=H)
                    act.activation(staged[:, QUERY, :, :], queries, ACT.Copy).then_inc(B.q, 1)
                    wait(act, B.qT_ps, n)
                    first_part(act, QUERY, LEFT_SLOTS, queries, B.q)

                def save_kv(n, par):
                    wait(act, B.ks, 4 * (n - 1))
                    for c in range(2):
                        act.activation(k3T[:, par, 128 * c:128 * c + 64], B.ln_bank[:, 256 + 64 * c:320 + 64 * c], ACT.Copy).then_inc(B.k, 1)
                    wait(act, B.vT_ps, n)
                    act.activation(kvT[:, :], B.ln_bank[:, 256:384], ACT.Copy).then_inc(B.kv, 1)

                def save_v(n, par):
                    wait(act, B.vT_ps, n + 1)
                    wait(act, B.o, (n - 1) * R)
                    act.activation(v8[:, par, 0:HD], B.ln_bank[:, 384 + USED:384 + USED + HD], ACT.Copy).then_inc(B.v, 1)

                def exps3(n, par, r):
                    wait(act, B.mx, n * R + r + 1)
                    wait(act, B.ab, n * R + r - 1)
                    wait(act, B.on, n - 1)
                    for p in range(PT):
                        h = r * PT + p
                        last = act.activation(probs3[:, r % 2, p, :], B.scores[r % 2][:, p // 2, p % 2, :], ACT.Exp,
                                              bias=negmax[:, r % 2, p:p + 1], scale=1.0, accum_out=denom[:, par, h:h + 1])
                    last.then_inc(B.p, 1)

                def body(b, par, left):
                    if left >= 1:
                        save_v(b + 1, 1 - par)
                    if not isinstance(b, int) or b > 0:
                        save_outT(act, B, b - 1)
                    exps3(b, par, 1)
                    if not isinstance(b, int) or b > 0:
                        save_attnT(act, B, b - 1)
                    exps3(b, par, 2)
                    if left >= 1:
                        save_stack(act, B, B.qT_ps, B.qT, qT[:, 1 - par, :, :], b + 1)
                    exps3(b, par, 3)
                    if left >= 2:
                        save_xnT(act, B, b + 2, xnT[:, :], B.proj, b + 2)
                    if left >= 1:
                        exps3(b + 1, 1 - par, 0)
                    if left >= 2:
                        save_q(b + 2)
                        save_kv(b + 2, par)

                act.wait_ge(A.x, NB)
                act.wait_ge(k0.kvzero, 2)
                save_xnT(act, B, 0, xnT[:, :], B.proj, 0)
                save_q(0)
                save_kv(0, 0)
                save_v(0, 0)
                save_stack(act, B, B.qT_ps, B.qT, qT[:, 0, :, :], 0)
                save_xnT(act, B, 1, xnT[:, :], B.proj, 1)
                save_q(1)
                save_kv(1, 1)
                exps3(0, 0, 0)
                body_pairs(act, body)
                save_outT(act, B, NB - 1)
                save_attnT(act, B, NB - 1)

            cross_attention()

            def recurrence():
                def activate(s, par):
                    wait(act, C.g, s + 1)
                    bank_g = C.gate_bank[par].rearrange("m (g s) -> m g s", g=4)
                    act.activation(gates[:, 0, :], bank_g[:, 0, :], ACT.Tanh, bias=half_bias[:, 0:1], scale=0.5).then_inc(C.f, 1)
                    act.activation(gates[:, 1, :], bank_g[:, 1, :], ACT.Tanh, bias=half_bias[:, 1:2], scale=0.5)
                    act.activation(gates[:, 2, :], bank_g[:, 2, :], ACT.Tanh, bias=gate_bias[:, 2:3], scale=1.0).then_inc(C.c, 1)

                act.wait_ge(B.x, NB)
                act.wait_ge(C.scaled, 2)
                save_xnT(act, C, 0, seqT[:, 0, :], C.xnT, 0)
                with act.Fori(0, NB // 2 - 1) as pair:
                    for k in range(2):
                        s = 2 * pair + k
                        save_xnT(act, C, s + 1, seqT[:, at(s + 1), :], C.xnT, 0)
                        activate(s, k)
                save_xnT(act, C, NB - 1, seqT[:, NB - 1, :], C.xnT, 0)
                activate(NB - 2, 0)
                activate(NB - 1, 1)

                def squash(g, par):
                    wait(act, C.z, g + 1)
                    wait(act, C.hT_ps, g - 1)
                    act.activation(hidden[:, par, :, :].rearrange("o b s -> o (b s)"), C.h_bank[par], ACT.Tanh,
                                   bias=gate_bias[:, 3:4], scale=1.0).then_inc(C.h, 1)

                squash(0, 0)
                squash(1, 1)
                with act.Fori(1, NB // 8) as pair:
                    squash(2 * pair, 0)
                    squash(2 * pair + 1, 1)

            recurrence()

            def relative_attention():
                def save_rows(n, par, r):
                    wait(act, P.e, n * R + r + 1)
                    if r == 0:
                        wait(act, P.skewed, 16 * (n - 1))
                    act.activation(pos_rows[:, par, r * PT:(r + 1) * PT, 1:S + 1],
                                   P.pos_bank.rearrange("s (p k) -> s p k", p=PT), ACT.Copy).then_inc(P.es, 1)

                def save_q2T(n):
                    save_stack(act, P, P.q2T_ps, P.q2T, q2T[:, :, :], n, P.e, n * R)

                def save_qT(n, par):
                    save_stack(act, P, P.qT_ps, P.qT, qT[:, par, :, :], n, P.s, (n - 1) * R)

                def save_kT(n, par):
                    save_stack(act, P, P.kT_ps, P.kT, kT[:, par, :, :], n)

                def body(b, par, left):
                    if not isinstance(b, int) or b > 0:
                        save_outT(act, P, b - 1)
                    exps(act, P, b, 1)
                    if left >= 2:
                        save_q2T(b + 2)
                    if not isinstance(b, int) or b > 0:
                        save_attnT(act, P, b - 1)
                    exps(act, P, b, 2)
                    if left >= 2:
                        save_rows(b + 2, par, 0)
                        save_qT(b + 2, par)
                        save_rows(b + 2, par, 1)
                    exps(act, P, b, 3)
                    if left >= 2:
                        save_kT(b + 2, par)
                        save_rows(b + 2, par, 2)
                    if left >= 1:
                        exps(act, P, b + 1, 0)
                    if left >= 2:
                        save_rows(b + 2, par, 3)
                    if left >= 4:
                        save_xnT(act, P, b + 4, xnT[:, :], P.proj, b + 4)

                act.wait_ge(C.x, NB // 4)
                act.wait_ge(P.zeroed, 1)
                act.wait_ge(P.pos, 3)
                act.activation(posT[:, :, :].rearrange("k t s -> k (t s)"), P.head_bank.bitcast(BF16), ACT.Copy).then_inc(P.pos, 1)
                for n in range(2):
                    save_xnT(act, P, n, xnT[:, :], P.proj, n)
                    save_q2T(n)
                    save_qT(n, n)
                    save_kT(n, n)
                    for r in range(R):
                        save_rows(n, n, r)
                save_xnT(act, P, 2, xnT[:, :], P.proj, 2)
                save_xnT(act, P, 3, xnT[:, :], P.proj, 3)
                exps(act, P, 0, 0)
                body_pairs(act, body, tail=2)
                save_outT(act, P, NB - 1)
                save_attnT(act, P, NB - 1)

            relative_attention()

            def position_weights():
                act.wait_ge(P.x, NB)
                act.wait_ge(ld.e, 16)
                act.wait_ge(F.cast, 1)
                with act.Fori(0, NB // 4) as g:
                    wait(act, E.xnT_ps, E.base + g + 1)
                    act.activation(seqT[:, at(4 * g, 4), :], E.ln_bank.rearrange("d (b s) -> d b s", b=4), ACT.Copy).then_inc(E.xnT, 1)

                def gather(pair, k):
                    gather_weights(act, act.copy, pair, k, GATHER_ACT, E.by_act)

                def save_y(pair, k):
                    wait(act, E.mm, 2 * pair + k + 1)
                    act.activation(yT[:, :, at(32 * pair + 16 * k, 16)],
                                   E.y_bank[k].rearrange("o (s b) -> o b s", b=NB), ACT.Copy).then_inc(E.ev, 1)

                gather(0, 0)
                gather(0, 1)
                with act.Fori(0, 3) as pair:
                    for k in range(2):
                        save_y(pair, k)
                        gather(pair + 1, k)
                save_y(3, 0)
                save_y(3, 1)

                def stage(g, par):
                    wait(act, E.turned, g - 1)
                    act.activation(y_stage[:, par, :, :], yT[:, at(4 * g, 4), :], ACT.Copy).then_inc(E.st, 1)

                act.wait_ge(E.ev, 8)
                stage(0, 0)
                stage(1, 1)
                with act.Fori(1, NB // 8) as pair:
                    stage(2 * pair, 0)
                    stage(2 * pair + 1, 1)

            position_weights()

            def experts():
                def save_group(g, gpar):
                    wait(act, F.xnT_ps, F.base + g + 1)
                    act.activation(xT[:, gpar, :, :].rearrange("d b s -> d (b s)"), F.ln_bank, ACT.Copy).then_inc(F.xnT, 1)

                def gate(g):
                    wait(act, F.gate, g + 1)
                    wait(act, F.split, g)
                    act.activation(scores4[:, :, :].rearrange("s k e -> s (k e)"), F.gate_bank[:, 0:4 * EX], ACT.Sigmoid)\
                       .then_inc(F.scores, 1)

                def save_combine(g, gpar):
                    wait(act, F.cT_ps, g + 1)
                    act.activation(combineT[:, gpar, :, :].rearrange("e b s -> e (b s)"), F.gate_bank[0:3 * EX, :], ACT.Copy)\
                       .then_inc(F.cT, 1)

                def tile(g, gpar, k):
                    n, par = g * TILES + k, (gpar + k) % 2
                    wait(act, F.h1, n + 1)
                    wait(act, F.gated, n - 1)
                    act.activation(silu[:, par, :], F.h1_bank[par], ACT.Silu).then_inc(F.silu, 1)

                def body(g, par, left):
                    for k in range(TILES):
                        tile(g, par, k)
                        if left >= 1 and k == 0:
                            save_group(g + 1, 1 - par)
                        if left >= 1 and k == 1:
                            gate(g + 1)
                    if left >= 1:
                        save_combine(g + 1, 1 - par)

                act.wait_ge(E.x, NG)
                save_group(0, 0)
                gate(0)
                save_combine(0, 0)
                group_pairs(act, body)

            experts()

        @block.tensor
        def _(pe):
            pe.wait_ge(ld.c, 16)
            pe.wait_ge(ld.w, LOADS)
            pe.matmul(bank[0][0:HD, 0:HD], w_ukvT[:, HD:2 * HD], w_dkv[:, :], start=True, stop=True).then_inc(k0.fold, 1)
            pe.matmul(bank[1][0:HD, 0:HD], w_dq[:, :], w_uqT[:, :], start=True, stop=True)
            pe.matmul(bank[1][0:HD, HD:2 * HD], w_dkv[:, :], w_ukvT[:, 0:HD], start=True, stop=True)
            pe.matmul(bank[1][0:HD, 2 * HD:3 * HD], w_kr[:, :], w_qr[:, :], start=True, stop=True)
            pe.wait_ge(k0.fold, 2)
            pe.matmul(bank[1][0:HD, 3 * HD:4 * HD], avT[:, :], w_oT[:, :], start=True, stop=True).then_inc(k0.fold, 1)
            pe.wait_ge(k0.fold, 6)
            pe.matmul(bank[2][:, 0:4 * HD], consts[0:HD, C_REP:C_REP + 128], small[:, :, :].rearrange("e w d -> e (w d)"),
                      start=True, stop=True).then_inc(k0.fold, 1)

            def project(n):
                wait(pe, A.xnT, n + 1)
                wait(pe, A.kn, n)
                wait(pe, A.vst, n)
                pe.matmul(A.proj_bank, xnT[:, :], wblk[:, :, :, :].rearrange("e w h d -> e (w h d)"),
                          start=True, stop=True).then_inc(A.proj, 1)

            def score(n, par, r):
                if r == 0:
                    wait(pe, A.kT, n + 1)
                wait(pe, A.p, n * R + r - 1)
                pe.matmul(bank[r % 2], identb[:, :], causal4[:, :, :].rearrange("s p k -> s (p k)"),
                          start=True, stop=False, skip_group_check=True)
                for p in range(PT):
                    last = pe.matmul(bank[r % 2][:, p * S:(p + 1) * S], rows_of(qT[:, par, :, :], r, p),
                                     rows_of(kT[:, par, :, :], r, p), start=False, stop=(p == PT - 1),
                                     skip_group_check=True)
                last.then_inc(A.s, 1)

            def turn_queries(n):
                wait(pe, A.split, 6 * n + 3)
                wait(pe, A.kT, n)
                turn_stack(pe, A, QUERY, A.qT_ps)

            def turn_keys(n):
                wait(pe, A.split, 6 * n + 6)
                wait(pe, A.qT, n + 1)
                turn_stack(pe, A, KEY, A.kT_ps)

            def body(b, par, left):
                turn_probs(pe, A, b, 0)
                if left >= 2:
                    project(b + 2)
                score(b, par, 2)
                if not isinstance(b, int) or b > 0:
                    turn_out(pe, A, b - 1)
                turn_probs(pe, A, b, 1)
                if left >= 1:
                    turn_queries(b + 1)
                score(b, par, 3)
                weigh_values(pe, A, b, par, 0)
                if left >= 1:
                    turn_keys(b + 1)
                turn_probs(pe, A, b, 2)
                if left >= 1:
                    score(b + 1, 1 - par, 0)
                weigh_values(pe, A, b, par, 1)
                if left >= 3:
                    turn_xn(pe, A, b + 3, A.xnT, b + 3)
                turn_probs(pe, A, b, 3)
                if left >= 1:
                    score(b + 1, 1 - par, 1)
                weigh_values(pe, A, b, par, 2)
                weigh_values(pe, A, b, par, 3)

            pe.wait_ge(k0.fold, 11)
            pe.wait_ge(k0.cast, 2)
            for n in range(3):
                turn_xn(pe, A, n, A.xnT, n)
                if n < 2:
                    project(n)
                if n == 0:
                    turn_queries(0)
                    turn_keys(0)
            score(0, 0, 0)
            score(0, 0, 1)
            body_pairs(pe, body, tail=2)
            turn_out(pe, A, NB - 1)

            def cross_attention():
                def project(n):
                    wait(pe, B.xnT, B.base + n + 1)
                    pe.matmul(B.ln_bank[:, 128:256], xnT[:, :], w_qx[:, :], start=True, stop=True)
                    pe.matmul(B.ln_bank[:, 256:384].unsqueeze(1), w_kvx[:, :, :, :].rearrange("e a t d -> e (a t d)"), ctxT[:, at(n), :],
                              start=True, stop=True).then_inc(B.proj, 1)

                def turn_v(n, par):
                    wait(pe, B.kv, n + 1)
                    pe.transpose(B.ln_bank[:, 384:512],
                                 kvT[:, :], ident).then_inc(B.vT_ps, 1)

                def turn_queries(n):
                    wait(pe, B.v, n + 1)
                    wait(pe, B.split, 3 * n + 3)
                    turn_stack(pe, B, QUERY, B.qT_ps)

                def score(n, par, r):
                    if r == 0:
                        wait(pe, B.qT, n + 1)
                        wait(pe, B.ks, 4 * (n + 1))
                    wait(pe, B.p, n * R + r - 1)
                    for p in range(PT):
                        last = pe.matmul(B.scores[r % 2][:, p // 2, p % 2, :], rows_of(qT[:, par, :, :], r, p),
                                         kstack[(r % 2) * STACK:(r % 2) * STACK + USED, par, :], start=True, stop=True)
                    last.then_inc(B.s, 1)

                def body(b, par, left):
                    later = not isinstance(b, int) or b > 0
                    turn_probs(pe, B, b, 0)
                    if later:
                        turn_out(pe, B, b - 1)
                    score(b, par, 2)
                    turn_probs(pe, B, b, 1)
                    if later:
                        turn_attn(pe, B, b - 1)
                    score(b, par, 3)
                    if later:
                        output(pe, B, b - 1, w_cx[:, :])
                    if left >= 1:
                        turn_queries(b + 1)
                    weigh_values(pe, B, b, par, 0)
                    turn_probs(pe, B, b, 2)
                    if left >= 1:
                        score(b + 1, 1 - par, 0)
                    weigh_values(pe, B, b, par, 1)
                    if left >= 2:
                        turn_xn(pe, B, b + 2, B.qT, b + 2)
                    turn_probs(pe, B, b, 3)
                    if left >= 1:
                        score(b + 1, 1 - par, 1)
                    weigh_values(pe, B, b, par, 2)
                    if left >= 2:
                        project(b + 2)
                    weigh_values(pe, B, b, par, 3)
                    if left >= 2:
                        turn_v(b + 2, par)

                pe.wait_ge(A.x, NB)
                pe.wait_ge(k0.wqx, 3)
                turn_xn(pe, B, 0, B.qT, 0)
                project(0)
                turn_v(0, 0)
                turn_queries(0)
                turn_xn(pe, B, 1, B.qT, 1)
                project(1)
                turn_v(1, 1)
                score(0, 0, 0)
                score(0, 0, 1)
                body_pairs(pe, body)
                turn_out(pe, B, NB - 1)
                turn_attn(pe, B, NB - 1)
                output(pe, B, NB - 1, w_cx[:, :])

            cross_attention()

            def recurrence():
                def inputs(s, par):
                    wait(pe, C.xnT, C.base + s + 1)
                    wait(pe, C.c, s - 1)
                    for g in range(3):
                        pe.matmul(C.gate_bank[par][:, g * S:(g + 1) * S].unsqueeze(1), wx[:, g, :], seqT[:, at(s), :],
                                  start=(g == 0), stop=False, skip_group_check=True)

                def state(s, par):
                    wait(pe, C.cell, s + 1)
                    for g in range(3):
                        last = pe.matmul(C.gate_bank[par][:, g * S:(g + 1) * S], uc[:, g, :], cell2[:, :],
                                         start=False, stop=(g == 2), skip_group_check=True)
                    last.then_inc(C.g, 1)

                pe.wait_ge(B.x, NB)
                pe.wait_ge(C.scaled, 2)
                turn_xn(pe, C, 0, C.xnT, C.base)
                inputs(0, 0)
                turn_xn(pe, C, 1, C.xnT, C.base + 1)
                inputs(1, 1)
                state(0, 0)
                with pe.Fori(0, NB // 2 - 1) as pair:
                    for k in range(2):
                        s = 2 * pair + k
                        turn_xn(pe, C, s + 2, C.xnT, C.base + s + 2)
                        inputs(s + 2, k)
                        state(s + 1, 1 - k)
                state(NB - 1, 1)

                def outputs(g, par):
                    wait(pe, C.h, g - 1)
                    pe.matmul(C.h_bank[par].rearrange("o (b s) -> o b s", b=4), wx[:, 3, :], seqT[:, at(4 * g, 4), :],
                              start=True, stop=False)
                    pe.matmul(C.h_bank[par].rearrange("o (b s) -> o b s", b=4), uc[:, 3, :],
                              cell2[:, :].unsqueeze(1).broadcast_to([D, 4, S]), start=False, stop=True).then_inc(C.z, 1)

                def turn_hidden(g, par):
                    wait(pe, C.h, g + 1)
                    wait(pe, C.x, g - 1)
                    for k in range(4):
                        last = pe.transpose(C.hT_bank[par][:, k * S:(k + 1) * S], hidden[:, par, k, :], ident)
                    last.then_inc(C.hT_ps, 1)

                pe.wait_ge(C.cell, NB + 1)
                outputs(0, 0)
                outputs(1, 1)
                turn_hidden(0, 0)
                turn_hidden(1, 1)
                with pe.Fori(1, NB // 8) as pair:
                    outputs(2 * pair, 0)
                    outputs(2 * pair + 1, 1)
                    turn_hidden(2 * pair, 0)
                    turn_hidden(2 * pair + 1, 1)

            recurrence()

            def relative_attention():
                def project(n):
                    wait(pe, P.xnT, P.base + n + 1)
                    pe.matmul(P.ln_bank[:, 128:512], xnT[:, :], wqkv[:, :, :].rearrange("e w d -> e (w d)"),
                              start=True, stop=True).then_inc(P.proj, 1)

                def turn(n, which):
                    wait(pe, P.split, splits(n, which + 1))
                    wait(pe, [P.kT, P.q2T, P.qT][which], n if which == Q2 else n + 1)
                    turn_stack(pe, P, which, [P.q2T_ps, P.qT_ps, P.kT_ps][which])

                def turn_q2(n):
                    turn(n, Q2)

                def turn_q(n):
                    turn(n, Q)

                def turn_k(n):
                    turn(n, K)

                def position_score(n, r):
                    wait(pe, P.q2T, n + 1)
                    wait(pe, P.es, n * R + r)
                    for p in range(PT):
                        last = pe.matmul(P.pos_bank[:, p * S:(p + 1) * S], rows_of(q2T, r, p), rows_of(posT, r, p), start=True, stop=True)
                    last.then_inc(P.e, 1)

                def score(n, par, r):
                    if r == 0:
                        wait(pe, P.kT, n + 1)
                    wait(pe, P.add, n * R + r - 1)
                    for p in range(PT):
                        last = pe.matmul(P.score_bank[r % 2][:, p, :], rows_of(qT[:, par, :, :], r, p),
                                         rows_of(kT[:, par, :, :], r, p), start=True, stop=True)
                    last.then_inc(P.s, 1)

                def body(b, par, left):
                    later = not isinstance(b, int) or b > 0
                    turn_probs(pe, P, b, 0)
                    if left >= 3:
                        project(b + 3)
                    score(b, par, 2)
                    if later:
                        turn_out(pe, P, b - 1)
                    turn_probs(pe, P, b, 1)
                    if left >= 2:
                        turn_q2(b + 2)
                    score(b, par, 3)
                    if later:
                        turn_attn(pe, P, b - 1)
                    if left >= 2:
                        position_score(b + 2, 0)
                        turn_q(b + 2)
                    if later:
                        output(pe, P, b - 1, w_o1[:, :])
                    if left >= 2:
                        position_score(b + 2, 1)
                    weigh_values(pe, P, b, par, 0)
                    turn_probs(pe, P, b, 2)
                    if left >= 1:
                        score(b + 1, 1 - par, 0)
                    if left >= 2:
                        turn_k(b + 2)
                    weigh_values(pe, P, b, par, 1)
                    if left >= 2:
                        position_score(b + 2, 2)
                    turn_probs(pe, P, b, 3)
                    if left >= 1:
                        score(b + 1, 1 - par, 1)
                    weigh_values(pe, P, b, par, 2)
                    if left >= 2:
                        position_score(b + 2, 3)
                    if left >= 4:
                        turn_xn(pe, P, b + 4, P.vst, b + 4)
                    weigh_values(pe, P, b, par, 3)

                pe.wait_ge(ld.d, LOADS_D)
                pe.wait_ge(P.bqs, 1)
                pe.wait_ge(C.x, NB // 4)
                pe.matmul(P.pos_bank[:, 0:D], consts[:, C_SIN:C_SIN + S], w_p[:, :], start=True, stop=True).then_inc(P.pos, 1)
                pe.wait_ge(P.split, SPLIT_STEPS)
                turn_stack(pe, P, K, P.pos)
                pe.wait_ge(P.pos, 4)
                for n in range(2):
                    turn_xn(pe, P, n, P.vst, n)
                    project(n)
                    turn_q2(n)
                    turn_q(n)
                    turn_k(n)
                    for r in range(R):
                        position_score(n, r)
                turn_xn(pe, P, 2, P.vst, 2)
                project(2)
                turn_xn(pe, P, 3, P.vst, 3)
                score(0, 0, 0)
                score(0, 0, 1)
                body_pairs(pe, body, tail=2)
                turn_out(pe, P, NB - 1)
                turn_attn(pe, P, NB - 1)
                output(pe, P, NB - 1, w_o1[:, :])

            relative_attention()

            def position_weights():
                pe.wait_ge(P.x, NB)
                turn_group(pe, E, 0)
                with pe.Fori(1, NB // 4) as g:
                    turn_group(pe, E, g)

                def multiply(pair, k):
                    wait(pe, E.by_pool, GATHER_POOL[1] * (2 * pair + k + 1))
                    wait(pe, E.by_dve, GATHER_DVE[1] * (2 * pair + k + 1))
                    wait(pe, E.by_act, GATHER_ACT[1] * (2 * pair + k + 1))
                    wait(pe, E.ev, 2 * pair + k - 1)
                    for j in range(16):
                        last = pe.matmul(E.y_bank[k][:, j * NB:(j + 1) * NB].unsqueeze(2), gathered[:, k, j, :],
                                         seqT[:, :, at(32 * pair + 16 * k + j)], start=True, stop=True)
                    last.then_inc(E.mm, 1)

                def turn_back(g, par):
                    wait(pe, E.st, g + 1)
                    wait(pe, E.x, g - 1)
                    for k in range(4):
                        last = pe.transpose(E.turn_bank[par][:, k * S:(k + 1) * S], y_stage[:, par, k, :], ident)
                    last.then_inc(E.turned, 1)

                pe.wait_ge(E.xnT, E.base + NB // 4)
                multiply(0, 0)
                multiply(0, 1)
                with pe.Fori(1, 4) as pair:
                    multiply(pair, 0)
                    multiply(pair, 1)
                turn_back(0, 0)
                turn_back(1, 1)
                with pe.Fori(1, NB // 8) as pair:
                    turn_back(2 * pair, 0)
                    turn_back(2 * pair + 1, 1)

            position_weights()

            def experts():
                def gate(g, gpar):
                    wait(pe, F.xnT, F.base + g + 1)
                    wait(pe, F.cT, g)
                    for k in range(4):
                        last = pe.matmul(F.gate_bank[:, k * EX:(k + 1) * EX], xT[:, gpar, k, :], w_gate[:, :], start=True, stop=True)
                    last.then_inc(F.gate, 1)

                def turn_combine(g):
                    wait(pe, F.split, g + 1)
                    for k in range(4):
                        last = pe.matmul(F.gate_bank[0:3 * EX, k * S:(k + 1) * S], parts3[:, k, :, :].rearrange("s c e -> s (c e)"),
                                         identb[:, :], start=True, stop=True)
                    last.then_inc(F.cT_ps, 1)

                def up(g, gpar, k):
                    n, par = g * TILES + k, (gpar + k) % 2
                    x = xT[:, gpar, :, :].rearrange("d b s -> d (b s)")
                    wait(pe, F.silu, n - 1)
                    pe.matmul(F.h1_bank[par], w_up1[:, k, :], x, start=True, stop=True).then_inc(F.h1, 1)
                    wait(pe, F.gated, n - 1)
                    last = pe.matmul(F.h3_bank[par], w_up3[:, k, :], x, start=True, stop=True)
                    if k < TILES - 1:
                        if k == 0:
                            wait(pe, F.cT, g + 1)
                        wait(pe, F.a, g * (TILES - 1) + k)
                        last = pe.matmul(F.combine_bank, spreadb[:, k, :], combineT[:, gpar, :, :].rearrange("e b s -> e (b s)"),
                                         start=True, stop=True)
                    last.then_inc(F.h3, 1)

                def down(g, gpar, k):
                    n, par = g * TILES + k, (gpar + k) % 2
                    if k == 0:
                        wait(pe, F.x, g)
                    if k < TILES - 1:
                        wait(pe, F.a, g * (TILES - 1) + k + 1)
                    else:
                        wait(pe, F.gated, n + 1)
                    for b in range(4):
                        last = pe.matmul(F.y_bank[:, b * D:(b + 1) * D], hidden_a[:, par, b * S:(b + 1) * S], w_down[:, k, :],
                                         start=(k == 0 and b == 0), stop=(k == TILES - 1 and b == 3), skip_group_check=True)
                    last.then_inc(F.y, 1)

                def body(g, par, left):
                    for k in range(TILES):
                        up(g, par, k)
                        if k > 0:
                            down(g, par, k - 1)
                        elif not isinstance(g, int) or g > 0:
                            down(g - 1, 1 - par, TILES - 1)
                        if left >= 1 and k == 0:
                            turn_group(pe, F, g + 1)
                        if left >= 1 and k == 1:
                            gate(g + 1, 1 - par)
                    if left >= 1:
                        turn_combine(g + 1)

                pe.wait_ge(ld.f, LOADS_F)
                pe.wait_ge(F.cast, 1)
                pe.wait_ge(E.x, NG)
                turn_group(pe, F, 0)
                gate(0, 0)
                turn_combine(0)
                group_pairs(pe, body)
                down(NG - 1, 1, TILES - 1)

            experts()


_INS = ['x', 'ctx_1024', 'itok_S_0_31',
        'L0_attn_W_DQ', 'L0_attn_W_UQ', 'L0_attn_W_DKV', 'L0_attn_W_UKV', 'L0_attn_W_QR', 'L0_attn_W_KR',
        'L0_attn_W_O', 'L0_attn_q_norm_w', 'L0_attn_k_norm_w', 'L0_xattn_Wq', 'L0_xattn_Wkv', 'L0_xattn_Wc',
        'L0_ffn_wf', 'L0_ffn_uf', 'L0_ffn_bf', 'L0_ffn_wi', 'L0_ffn_ui', 'L0_ffn_bi', 'L0_ffn_wc', 'L0_ffn_uc',
        'L0_ffn_bc', 'L0_ffn_wo', 'L0_ffn_uo', 'L0_ffn_bo', 'L0_ffn_in_c', 'L1_attn_Wq', 'L1_attn_bq',
        'L1_attn_Wk', 'L1_attn_bk', 'L1_attn_Wv', 'L1_attn_bv', 'L1_attn_Wp', 'L1_attn_bp', 'L1_attn_Wo',
        'L1_attn_bo', 'L1_attn_u', 'L1_attn_v', 'L1_ffn_w_gate', 'L1_ffn_w1_e', 'L1_ffn_w3_e', 'L1_ffn_w2_e',
        'L1_ffn_w1_s', 'L1_ffn_w3_s', 'L1_ffn_w2_s']

_TURNED = ['ctx_1024', 'L0_ffn_wf', 'L0_ffn_wi', 'L0_ffn_wc', 'L0_ffn_wo', 'L0_ffn_uf', 'L0_ffn_ui', 'L0_ffn_uc',
           'L0_ffn_uo', 'L1_ffn_w_gate', 'L1_ffn_w1_s', 'L1_ffn_w3_s', 'L1_ffn_w2_s', 'L1_ffn_w1_e', 'L1_ffn_w2_e', 'L1_ffn_w3_e',
           'L0_attn_W_UQ', 'L0_attn_W_UKV', 'L0_attn_W_O']


def _constants(np):
    c = np.zeros((128, C_END), np.float32)
    c[:, C_ID:C_ID + 128] = np.eye(128)
    q, k = np.arange(128)[:, None], np.arange(128)[None, :]
    c[:, C_CAUSAL:C_CAUSAL + 128] = np.where(k > q, -1e30, 0.0)
    c[:, C_HEAD:C_HEAD + H] = (q // HD == np.arange(H)[None, :])
    c[0:HD, C_REP:C_REP + 128] = (k % HD == np.arange(HD)[:, None])
    pos, idx = np.arange(S, dtype=np.float32), np.arange(D // 2, dtype=np.float32)
    inv = (np.float32(1.0) / np.float32(10000.0) ** (np.float32(2.0) * idx / np.float32(D))).astype(np.float32)
    ang = pos[None, :] * inv[:, None]
    c[:, C_SIN:C_SIN + S] = np.concatenate([np.sin(ang), np.cos(ang)], 0)
    c[:, C_TIE_G:C_TIE_G + 16] = np.tril(np.ones((4, 4)), -1).reshape(1, -1)
    c[:, C_TIE_E:C_TIE_E + EX * EX] = np.tril(np.ones((EX, EX)), -1).reshape(1, -1)
    part = np.array([3, 1, 2, 1, 2, 1, 0, 0])[np.arange(128) // HD % 8]
    c[:, C_PARTS], c[:, C_PARTS + 1] = np.where(part >= 2, -1, 0), np.where(part == 3, -1, 0)
    return c


def _spread(np):
    e, col = np.arange(EX)[:, None], np.arange(EX * FW)[None, :]
    return np.tile((col // FW == e).astype(np.float32), (3, 1))


def kernel(**inputs):
    import numpy as _np
    import concourse.bacc as _bacc
    from concourse import mybir as _mybir
    from concourse.bass_utils import run_bass_kernel_spmd as _run

    nc = _bacc.Bacc("TRN2", target_bir_lowering=False, num_devices=1)
    arrays, tensors = {}, {}
    given = {name: _np.ascontiguousarray(inputs[name]) for name in _INS}
    for name in _TURNED:
        given[name] = _np.ascontiguousarray(_np.moveaxis(given[name], -1, 0))
    given["consts"] = _constants(_np)
    given["spread"] = _spread(_np)
    for name, a in given.items():
        arrays[f"in_{name}_dram"] = a
        tensors[name] = nc.dram_tensor(f"in_{name}_dram", a.shape, _mybir.dt.from_np(a.dtype), kind="ExternalInput").ap()
    out = nc.dram_tensor("out_0_dram", (NB, S, D), _mybir.dt.float32, kind="ExternalOutput").ap()
    decoder(nc, tensors, out)
    r = _run(nc, [arrays], core_ids=[0])
    return r.results[0]["out_0_dram"]
```
